# Optimizing a Trainium2 kernel written in Bass

```python
import numpy as np
import jax
import jax.numpy as jnp

def _softmax(x, axis=-1):
    return jax.nn.softmax(x, axis=axis)

def _gelu(x):
    return jax.nn.gelu(x, approximate=True)

def _silu(x):
    return jax.nn.silu(x)

def _sigmoid(x):
    return jax.nn.sigmoid(x)

def _layernorm(x, axis=-1, eps=1e-05):
    m = jnp.mean(x, axis=axis, keepdims=True)
    v = jnp.var(x, axis=axis, keepdims=True)
    return (x - m) / jnp.sqrt(v + eps)

def _scatter_add(tgt, idx, src, axis=0):
    return tgt.at[idx].add(src)

def _segment_sum(src, seg, n):
    return jax.ops.segment_sum(src, seg, n)
kernel_name = 'mk_conv_seq_d4_conv_nhwc768_r4_56dfe1'

def setup_inputs(seed: int=0):
    np.random.seed(seed)
    _w = jnp.asarray

    def _rec_inputs():
        import jax
        import jax.numpy as jnp
        _gk = jax.random.key(seed)
        x = -0.0002221 + 1 * jax.random.normal(jax.random.fold_in(_gk, 1), (8, 16, 16, 192), jnp.float32)
        return x
    x = _rec_inputs()

    def _L0_conv_setup():
        import jax, jax.numpy as jnp
        import numpy as np
        B, H, W, DIM = (8, 16, 16, 192)
        NH = 12
        HD = DIM // NH
        WS = 14
        N = WS * WS
        MLP = 4 * DIM
        EPS = 1e-05

        def layernorm(x, w, b):
            mu = jnp.mean(x, axis=-1, keepdims=True)
            var = jnp.var(x, axis=-1, keepdims=True)
            return (x - mu) * jax.lax.rsqrt(var + EPS) * w + b

        def window_partition(x, ws):
            b, h, w, c = x.shape
            pad_h = (ws - h % ws) % ws
            pad_w = (ws - w % ws) % ws
            x = jnp.pad(x, ((0, 0), (0, pad_h), (0, pad_w), (0, 0)))
            hp, wp = (h + pad_h, w + pad_w)
            x = x.reshape(b, hp // ws, ws, wp // ws, ws, c)
            windows = x.transpose(0, 1, 3, 2, 4, 5).reshape(-1, ws, ws, c)
            return (windows, (hp, wp))

        def window_unpartition(windows, ws, pad_hw, hw):
            hp, wp = pad_hw
            h, w = hw
            b = windows.shape[0] // (hp * wp // ws // ws)
            x = windows.reshape(b, hp // ws, wp // ws, ws, ws, -1)
            x = x.transpose(0, 1, 3, 2, 4, 5).reshape(b, hp, wp, -1)
            return x[:, :h, :w, :]
        key = jax.random.key(seed)
        ks = jax.random.split(key, 8)
        f = lambda k, shape: jax.random.normal(k, shape, jnp.float32) * 0.02
        return {'x': jax.random.normal(ks[0], (B, H, W, DIM), jnp.float32), 'n1_w': jnp.ones((DIM,), jnp.float32), 'n1_b': jnp.zeros((DIM,), jnp.float32), 'qkv_w': f(ks[1], (DIM, 3 * DIM)), 'qkv_b': jnp.zeros((3 * DIM,), jnp.float32), 'proj_w': f(ks[2], (DIM, DIM)), 'proj_b': jnp.zeros((DIM,), jnp.float32), 'rel_pos_h': f(ks[3], (2 * WS - 1, HD)), 'rel_pos_w': f(ks[4], (2 * WS - 1, HD)), 'n2_w': jnp.ones((DIM,), jnp.float32), 'n2_b': jnp.zeros((DIM,), jnp.float32), 'lin1_w': f(ks[5], (DIM, MLP)), 'lin1_b': jnp.zeros((MLP,), jnp.float32), 'lin2_w': f(ks[6], (MLP, DIM)), 'lin2_b': jnp.zeros((DIM,), jnp.float32)}
    _L0_conv_all = _L0_conv_setup()
    _L0_conv_in = {k: v for k, v in _L0_conv_all.items() if k in ('n1_w', 'n1_b', 'qkv_w', 'qkv_b', 'proj_w', 'proj_b', 'rel_pos_h', 'rel_pos_w', 'n2_w', 'n2_b', 'lin1_w', 'lin1_b', 'lin2_w', 'lin2_b')}
    del _L0_conv_all

    def _L1_conv_setup():
        import jax, jax.numpy as jnp
        import numpy as np
        WS = 14
        NH = 12
        C = 192
        HD = C // NH
        MLP = 768
        EPS = 1e-06

        def _layernorm(x, g, b):
            mu = jnp.mean(x, axis=-1, keepdims=True)
            var = jnp.mean(jnp.square(x - mu), axis=-1, keepdims=True)
            return (x - mu) * jax.lax.rsqrt(var + EPS) * g + b
        key = jax.random.key(seed)
        ks = jax.random.split(key, 8)
        B, H, W = (8, 16, 16)
        f32 = jnp.float32
        d = {}
        d['x'] = jax.random.normal(ks[0], (B, H, W, C), f32)
        d['ln1_g'] = jnp.ones((C,), f32)
        d['ln1_b'] = jnp.zeros((C,), f32)
        d['qkv_w'] = jax.random.normal(ks[1], (C, 3 * C), f32) * 0.02
        d['qkv_b'] = jnp.zeros((3 * C,), f32)
        d['proj_w'] = jax.random.normal(ks[2], (C, C), f32) * 0.02
        d['proj_b'] = jnp.zeros((C,), f32)
        d['rel_pos_h'] = jax.random.normal(ks[3], (2 * WS - 1, HD), f32) * 0.02
        d['rel_pos_w'] = jax.random.normal(ks[4], (2 * WS - 1, HD), f32) * 0.02
        d['ln2_g'] = jnp.ones((C,), f32)
        d['ln2_b'] = jnp.zeros((C,), f32)
        d['mlp_w1'] = jax.random.normal(ks[5], (C, MLP), f32) * 0.02
        d['mlp_b1'] = jnp.zeros((MLP,), f32)
        d['mlp_w2'] = jax.random.normal(ks[6], (MLP, C), f32) * 0.02
        d['mlp_b2'] = jnp.zeros((C,), f32)
        return d
    _L1_conv_all = _L1_conv_setup()
    _L1_conv_in = {k: v for k, v in _L1_conv_all.items() if k in ('ln1_g', 'ln1_b', 'qkv_w', 'qkv_b', 'proj_w', 'proj_b', 'rel_pos_h', 'rel_pos_w', 'ln2_g', 'ln2_b', 'mlp_w1', 'mlp_b1', 'mlp_w2', 'mlp_b2')}
    del _L1_conv_all

    def _L2_conv_setup():
        import jax, jax.numpy as jnp
        import numpy as np
        DIM = 192
        N_BLOCKS = 8
        BLOCK = DIM // N_BLOCKS
        HIDDEN = BLOCK * 1
        LAMBDA = 0.01

        def _softshrink(x, lam):
            return jnp.sign(x) * jnp.maximum(jnp.abs(x) - lam, 0.0)
        key = jax.random.key(seed)
        ks = jax.random.split(key, 5)
        B, H, W = (2, 32, 64)
        x = jax.random.normal(ks[0], (B, H, W, DIM), dtype=jnp.float32)
        std = 0.02
        w1r = std * jax.random.truncated_normal(ks[1], -2.0, 2.0, (N_BLOCKS, BLOCK, HIDDEN), jnp.float32)
        w1i = std * jax.random.truncated_normal(ks[2], -2.0, 2.0, (N_BLOCKS, BLOCK, HIDDEN), jnp.float32)
        w2r = std * jax.random.truncated_normal(ks[3], -2.0, 2.0, (N_BLOCKS, HIDDEN, BLOCK), jnp.float32)
        w2i = std * jax.random.truncated_normal(ks[4], -2.0, 2.0, (N_BLOCKS, HIDDEN, BLOCK), jnp.float32)
        b1r = jnp.zeros((N_BLOCKS, HIDDEN), jnp.float32)
        b1i = jnp.zeros((N_BLOCKS, HIDDEN), jnp.float32)
        b2r = jnp.zeros((N_BLOCKS, BLOCK), jnp.float32)
        b2i = jnp.zeros((N_BLOCKS, BLOCK), jnp.float32)
        return {'x': x, 'w1r': w1r, 'w1i': w1i, 'b1r': b1r, 'b1i': b1i, 'w2r': w2r, 'w2i': w2i, 'b2r': b2r, 'b2i': b2i}
    _L2_conv_all = _L2_conv_setup()
    _L2_conv_in = {k: v for k, v in _L2_conv_all.items() if k in ('w1r', 'w1i', 'b1r', 'b1i', 'w2r', 'w2i', 'b2r', 'b2i')}
    del _L2_conv_all

    def _L3_conv_setup():
        import jax, jax.numpy as jnp
        import numpy as np
        NUM_HEADS = 8
        HIDDEN_SIZE = 192
        BLOCK = HIDDEN_SIZE // NUM_HEADS
        FACTOR = 1
        LAMBDA = 0.01
        FRACTION = 1.0
        SCALE = 0.02

        def softshrink(x, lambd):
            return jnp.where(x > lambd, x - lambd, jnp.where(x < -lambd, x + lambd, jnp.zeros_like(x)))
        key = jax.random.key(seed)
        k = jax.random.split(key, 5)
        B, H, W = (4, 32, 32)
        x = jax.random.normal(k[0], (B, H, W, HIDDEN_SIZE), dtype=jnp.float32)
        w1 = SCALE * jax.random.normal(k[1], (2, NUM_HEADS, BLOCK, BLOCK * FACTOR), dtype=jnp.float32)
        b1 = SCALE * jax.random.normal(k[2], (2, NUM_HEADS, BLOCK * FACTOR), dtype=jnp.float32)
        w2 = SCALE * jax.random.normal(k[3], (2, NUM_HEADS, BLOCK * FACTOR, BLOCK), dtype=jnp.float32)
        b2 = SCALE * jax.random.normal(k[4], (2, NUM_HEADS, BLOCK), dtype=jnp.float32)
        return {'x': x, 'w1': w1, 'b1': b1, 'w2': w2, 'b2': b2}
    _L3_conv_all = _L3_conv_setup()
    _L3_conv_in = {k: v for k, v in _L3_conv_all.items() if k in ('w1', 'b1', 'w2', 'b2')}
    del _L3_conv_all
    return {'x': x, 'L0_conv_n1_w': _L0_conv_in['n1_w'], 'L0_conv_n1_b': _L0_conv_in['n1_b'], 'L0_conv_qkv_w': _L0_conv_in['qkv_w'], 'L0_conv_qkv_b': _L0_conv_in['qkv_b'], 'L0_conv_proj_w': _L0_conv_in['proj_w'], 'L0_conv_proj_b': _L0_conv_in['proj_b'], 'L0_conv_rel_pos_h': _L0_conv_in['rel_pos_h'], 'L0_conv_rel_pos_w': _L0_conv_in['rel_pos_w'], 'L0_conv_n2_w': _L0_conv_in['n2_w'], 'L0_conv_n2_b': _L0_conv_in['n2_b'], 'L0_conv_lin1_w': _L0_conv_in['lin1_w'], 'L0_conv_lin1_b': _L0_conv_in['lin1_b'], 'L0_conv_lin2_w': _L0_conv_in['lin2_w'], 'L0_conv_lin2_b': _L0_conv_in['lin2_b'], 'L1_conv_ln1_g': _L1_conv_in['ln1_g'], 'L1_conv_ln1_b': _L1_conv_in['ln1_b'], 'L1_conv_qkv_w': _L1_conv_in['qkv_w'], 'L1_conv_qkv_b': _L1_conv_in['qkv_b'], 'L1_conv_proj_w': _L1_conv_in['proj_w'], 'L1_conv_proj_b': _L1_conv_in['proj_b'], 'L1_conv_rel_pos_h': _L1_conv_in['rel_pos_h'], 'L1_conv_rel_pos_w': _L1_conv_in['rel_pos_w'], 'L1_conv_ln2_g': _L1_conv_in['ln2_g'], 'L1_conv_ln2_b': _L1_conv_in['ln2_b'], 'L1_conv_mlp_w1': _L1_conv_in['mlp_w1'], 'L1_conv_mlp_b1': _L1_conv_in['mlp_b1'], 'L1_conv_mlp_w2': _L1_conv_in['mlp_w2'], 'L1_conv_mlp_b2': _L1_conv_in['mlp_b2'], 'L2_conv_w1r': _L2_conv_in['w1r'], 'L2_conv_w1i': _L2_conv_in['w1i'], 'L2_conv_b1r': _L2_conv_in['b1r'], 'L2_conv_b1i': _L2_conv_in['b1i'], 'L2_conv_w2r': _L2_conv_in['w2r'], 'L2_conv_w2i': _L2_conv_in['w2i'], 'L2_conv_b2r': _L2_conv_in['b2r'], 'L2_conv_b2i': _L2_conv_in['b2i'], 'L3_conv_w1': _L3_conv_in['w1'], 'L3_conv_b1': _L3_conv_in['b1'], 'L3_conv_w2': _L3_conv_in['w2'], 'L3_conv_b2': _L3_conv_in['b2']}

def reference(x, L0_conv_n1_w, L0_conv_n1_b, L0_conv_qkv_w, L0_conv_qkv_b, L0_conv_proj_w, L0_conv_proj_b, L0_conv_rel_pos_h, L0_conv_rel_pos_w, L0_conv_n2_w, L0_conv_n2_b, L0_conv_lin1_w, L0_conv_lin1_b, L0_conv_lin2_w, L0_conv_lin2_b, L1_conv_ln1_g, L1_conv_ln1_b, L1_conv_qkv_w, L1_conv_qkv_b, L1_conv_proj_w, L1_conv_proj_b, L1_conv_rel_pos_h, L1_conv_rel_pos_w, L1_conv_ln2_g, L1_conv_ln2_b, L1_conv_mlp_w1, L1_conv_mlp_b1, L1_conv_mlp_w2, L1_conv_mlp_b2, L2_conv_w1r, L2_conv_w1i, L2_conv_b1r, L2_conv_b1i, L2_conv_w2r, L2_conv_w2i, L2_conv_b2r, L2_conv_b2i, L3_conv_w1, L3_conv_b1, L3_conv_w2, L3_conv_b2):
    import jax
    import jax.numpy as jnp

    def _L0_conv_ref(x, n1_w, n1_b, qkv_w, qkv_b, proj_w, proj_b, rel_pos_h, rel_pos_w, n2_w, n2_b, lin1_w, lin1_b, lin2_w, lin2_b):
        import jax, jax.numpy as jnp
        import numpy as np
        B, H, W, DIM = (8, 16, 16, 192)
        NH = 12
        HD = DIM // NH
        WS = 14
        N = WS * WS
        MLP = 4 * DIM
        EPS = 1e-05

        def layernorm(x, w, b):
            mu = jnp.mean(x, axis=-1, keepdims=True)
            var = jnp.var(x, axis=-1, keepdims=True)
            return (x - mu) * jax.lax.rsqrt(var + EPS) * w + b

        def window_partition(x, ws):
            b, h, w, c = x.shape
            pad_h = (ws - h % ws) % ws
            pad_w = (ws - w % ws) % ws
            x = jnp.pad(x, ((0, 0), (0, pad_h), (0, pad_w), (0, 0)))
            hp, wp = (h + pad_h, w + pad_w)
            x = x.reshape(b, hp // ws, ws, wp // ws, ws, c)
            windows = x.transpose(0, 1, 3, 2, 4, 5).reshape(-1, ws, ws, c)
            return (windows, (hp, wp))

        def window_unpartition(windows, ws, pad_hw, hw):
            hp, wp = pad_hw
            h, w = hw
            b = windows.shape[0] // (hp * wp // ws // ws)
            x = windows.reshape(b, hp // ws, wp // ws, ws, ws, -1)
            x = x.transpose(0, 1, 3, 2, 4, 5).reshape(b, hp, wp, -1)
            return x[:, :h, :w, :]
        shortcut = x
        h = layernorm(x, n1_w, n1_b)
        win, pad_hw = window_partition(h, WS)
        bw = win.shape[0]
        qkv = win.reshape(bw, N, DIM) @ qkv_w + qkv_b
        qkv = qkv.reshape(bw, N, 3, NH, HD).transpose(2, 0, 3, 1, 4)
        qkv = qkv.reshape(3, bw * NH, N, HD)
        q, k, v = (qkv[0], qkv[1], qkv[2])
        scale = HD ** (-0.5)
        attn = jnp.einsum('bqc,bkc->bqk', q * scale, k)
        coords = jnp.arange(WS)[:, None] - jnp.arange(WS)[None, :] + (WS - 1)
        Rh = rel_pos_h[coords]
        Rw = rel_pos_w[coords]
        r_q = q.reshape(-1, WS, WS, HD)
        rel_h = jnp.einsum('bhwc,hkc->bhwk', r_q, Rh)
        rel_w = jnp.einsum('bhwc,wkc->bhwk', r_q, Rw)
        attn = (attn.reshape(-1, WS, WS, WS, WS) + rel_h[:, :, :, :, None] + rel_w[:, :, :, None, :]).reshape(-1, N, N)
        attn = jax.nn.softmax(attn, axis=-1)
        out = jnp.einsum('bqk,bkc->bqc', attn, v)
        out = out.reshape(bw, NH, WS, WS, HD).transpose(0, 2, 3, 1, 4)
        out = out.reshape(bw, WS, WS, DIM) @ proj_w + proj_b
        out = window_unpartition(out, WS, pad_hw, (H, W))
        x = shortcut + out
        h2 = layernorm(x, n2_w, n2_b)
        mlp = jax.nn.gelu(h2 @ lin1_w + lin1_b, approximate=False) @ lin2_w + lin2_b
        return x + mlp

    def _L1_conv_ref(x, ln1_g, ln1_b, qkv_w, qkv_b, proj_w, proj_b, rel_pos_h, rel_pos_w, ln2_g, ln2_b, mlp_w1, mlp_b1, mlp_w2, mlp_b2):
        import jax, jax.numpy as jnp
        import numpy as np
        WS = 14
        NH = 12
        C = 192
        HD = C // NH
        MLP = 768
        EPS = 1e-06

        def _layernorm(x, g, b):
            mu = jnp.mean(x, axis=-1, keepdims=True)
            var = jnp.mean(jnp.square(x - mu), axis=-1, keepdims=True)
            return (x - mu) * jax.lax.rsqrt(var + EPS) * g + b
        B, H, W, _ = x.shape
        xn = _layernorm(x, ln1_g, ln1_b)
        pad_h = -H % WS
        pad_w = -W % WS
        Hp, Wp = (H + pad_h, W + pad_w)
        xp = jnp.pad(xn, ((0, 0), (0, pad_h), (0, pad_w), (0, 0)))
        win = xp.reshape(B, Hp // WS, WS, Wp // WS, WS, C)
        win = win.transpose(0, 1, 3, 2, 4, 5).reshape(-1, WS, WS, C)
        Bn = win.shape[0]
        N = WS * WS
        qkv = win.reshape(Bn, N, C) @ qkv_w + qkv_b
        qkv = qkv.reshape(Bn, N, 3, NH, HD).transpose(2, 0, 3, 1, 4)
        qkv = qkv.reshape(3, Bn * NH, N, HD)
        q, k, v = (qkv[0], qkv[1], qkv[2])
        scale = HD ** (-0.5)
        attn = jnp.einsum('bnd,bmd->bnm', q * scale, k)
        coords = jnp.arange(WS)[:, None] - jnp.arange(WS)[None, :] + (WS - 1)
        Rh = rel_pos_h[coords]
        Rw = rel_pos_w[coords]
        rq = q.reshape(Bn * NH, WS, WS, HD)
        rel_h = jnp.einsum('bhwc,hkc->bhwk', rq, Rh)
        rel_w = jnp.einsum('bhwc,wkc->bhwk', rq, Rw)
        attn = (attn.reshape(Bn * NH, WS, WS, WS, WS) + rel_h[:, :, :, :, None] + rel_w[:, :, :, None, :]).reshape(Bn * NH, N, N)
        attn = jax.nn.softmax(attn, axis=-1)
        out = jnp.einsum('bnm,bmd->bnd', attn, v)
        out = out.reshape(Bn, NH, WS, WS, HD).transpose(0, 2, 3, 1, 4).reshape(Bn, WS, WS, C)
        out = out @ proj_w + proj_b
        out = out.reshape(B, Hp // WS, Wp // WS, WS, WS, C)
        out = out.transpose(0, 1, 3, 2, 4, 5).reshape(B, Hp, Wp, C)[:, :H, :W, :]
        x1 = x + out
        y = _layernorm(x1, ln2_g, ln2_b)
        y = jax.nn.gelu(y @ mlp_w1 + mlp_b1, approximate=False) @ mlp_w2 + mlp_b2
        return x1 + y

    def _L2_conv_ref(x, w1r, w1i, b1r, b1i, w2r, w2i, b2r, b2i):
        import jax, jax.numpy as jnp
        import numpy as np
        DIM = 192
        N_BLOCKS = 8
        BLOCK = DIM // N_BLOCKS
        HIDDEN = BLOCK * 1
        LAMBDA = 0.01

        def _softshrink(x, lam):
            return jnp.sign(x) * jnp.maximum(jnp.abs(x) - lam, 0.0)
        B, H, W, D = x.shape
        residual = x
        xf = jnp.fft.rfft2(x, axes=(1, 2), norm='ortho')
        xf = xf.reshape(B, H, W // 2 + 1, N_BLOCKS, BLOCK)
        xr, xi = (jnp.real(xf), jnp.imag(xf))
        o1r = jnp.einsum('bhwns,nse->bhwne', xr, w1r) - jnp.einsum('bhwns,nse->bhwne', xi, w1i) + b1r
        o1i = jnp.einsum('bhwns,nse->bhwne', xr, w1i) + jnp.einsum('bhwns,nse->bhwne', xi, w1r) + b1i
        o1r = jax.nn.relu(o1r)
        o1i = jax.nn.relu(o1i)
        o2r = jnp.einsum('bhwne,nes->bhwns', o1r, w2r) - jnp.einsum('bhwne,nes->bhwns', o1i, w2i) + b2r
        o2i = jnp.einsum('bhwne,nes->bhwns', o1r, w2i) + jnp.einsum('bhwne,nes->bhwns', o1i, w2r) + b2i
        o2r = _softshrink(o2r, LAMBDA)
        o2i = _softshrink(o2i, LAMBDA)
        xc = (o2r + 1j * o2i).reshape(B, H, W // 2 + 1, D)
        out = jnp.fft.irfft2(xc, s=(H, W), axes=(1, 2), norm='ortho')
        return out + residual

    def _L3_conv_ref(x, w1, b1, w2, b2):
        import jax, jax.numpy as jnp
        import numpy as np
        NUM_HEADS = 8
        HIDDEN_SIZE = 192
        BLOCK = HIDDEN_SIZE // NUM_HEADS
        FACTOR = 1
        LAMBDA = 0.01
        FRACTION = 1.0
        SCALE = 0.02

        def softshrink(x, lambd):
            return jnp.where(x > lambd, x - lambd, jnp.where(x < -lambd, x + lambd, jnp.zeros_like(x)))
        bias = x
        dtype = x.dtype
        xf32 = x.astype(jnp.float32)
        B, H, W, C = x.shape
        xs = jnp.fft.rfft2(xf32, axes=(1, 2))
        Wm = W // 2 + 1
        xs = xs.reshape(B, H, Wm, NUM_HEADS, BLOCK)
        total_modes = H // 2 + 1
        kept = int(total_modes * FRACTION)
        lo, hi = (total_modes - kept, min(total_modes + kept, H))
        wk = min(kept, Wm)
        xr = jnp.real(xs[:, lo:hi, :wk])
        xi = jnp.imag(xs[:, lo:hi, :wk])
        o1r = jax.nn.relu(jnp.einsum('bxyhi,hio->bxyho', xr, w1[0]) - jnp.einsum('bxyhi,hio->bxyho', xi, w1[1]) + b1[0])
        o1i = jax.nn.relu(jnp.einsum('bxyhi,hio->bxyho', xi, w1[0]) + jnp.einsum('bxyhi,hio->bxyho', xr, w1[1]) + b1[1])
        o2r = jnp.einsum('bxyho,hoi->bxyhi', o1r, w2[0]) - jnp.einsum('bxyho,hoi->bxyhi', o1i, w2[1]) + b2[0]
        o2i = jnp.einsum('bxyho,hoi->bxyhi', o1i, w2[0]) + jnp.einsum('bxyho,hoi->bxyhi', o1r, w2[1]) + b2[1]
        zr = jnp.zeros((B, H, Wm, NUM_HEADS, BLOCK), dtype=jnp.float32).at[:, lo:hi, :wk].set(o2r)
        zi = jnp.zeros((B, H, Wm, NUM_HEADS, BLOCK), dtype=jnp.float32).at[:, lo:hi, :wk].set(o2i)
        out_c = softshrink(zr, LAMBDA) + 1j * softshrink(zi, LAMBDA)
        out_c = out_c.reshape(B, H, Wm, C)
        out = jnp.fft.irfft2(out_c, s=(H, W), axes=(1, 2))
        return out.astype(dtype) + bias

    def _gn(v, G=32, eps=1e-05):
        B_, H_, W_, C_ = v.shape
        g = v.reshape(B_, H_, W_, G, C_ // G)
        m = jnp.mean(g, axis=(1, 2, 4), keepdims=True)
        s = jnp.var(g, axis=(1, 2, 4), keepdims=True)
        return ((g - m) / jnp.sqrt(s + eps)).reshape(v.shape)

    def _ln_c(v, eps=1e-06):
        m = jnp.mean(v, axis=-1, keepdims=True)
        s = jnp.var(v, axis=-1, keepdims=True)
        return (v - m) / jnp.sqrt(s + eps)

    def _ln_t(v, eps=1e-05):
        m = jnp.mean(v, axis=-1, keepdims=True)
        s = jnp.var(v, axis=-1, keepdims=True)
        return (v - m) / jnp.sqrt(s + eps)

    def _to_tokens(v):
        B_, H_, W_, C_ = v.shape
        return v.reshape(B_, H_ * W_, C_)

    def _from_tokens(t, like):
        return t.reshape(like.shape)
    x = _L0_conv_ref(x, L0_conv_n1_w, L0_conv_n1_b, L0_conv_qkv_w, L0_conv_qkv_b, L0_conv_proj_w, L0_conv_proj_b, L0_conv_rel_pos_h, L0_conv_rel_pos_w, L0_conv_n2_w, L0_conv_n2_b, L0_conv_lin1_w, L0_conv_lin1_b, L0_conv_lin2_w, L0_conv_lin2_b)
    x = _L1_conv_ref(x, L1_conv_ln1_g, L1_conv_ln1_b, L1_conv_qkv_w, L1_conv_qkv_b, L1_conv_proj_w, L1_conv_proj_b, L1_conv_rel_pos_h, L1_conv_rel_pos_w, L1_conv_ln2_g, L1_conv_ln2_b, L1_conv_mlp_w1, L1_conv_mlp_b1, L1_conv_mlp_w2, L1_conv_mlp_b2)
    x = _L2_conv_ref(x, L2_conv_w1r, L2_conv_w1i, L2_conv_b1r, L2_conv_b1i, L2_conv_w2r, L2_conv_w2i, L2_conv_b2r, L2_conv_b2i)
    x = _L3_conv_ref(x, L3_conv_w1, L3_conv_b1, L3_conv_w2, L3_conv_b2)
    return x

_drawn_inputs = setup_inputs


def setup_inputs(seed=0):
    import zlib

    import numpy as np

    out = dict(_drawn_inputs(seed))
    spreads = {'L0_conv_n1_w': (1.0, 0.6),
     'L0_conv_n1_b': (0.0, 0.8),
     'L0_conv_qkv_b': (0.0, 0.284),
     'L0_conv_proj_b': (0.0, 0.1),
     'L0_conv_n2_w': (1.0, 0.6),
     'L0_conv_n2_b': (0.0, 0.8),
     'L0_conv_lin1_b': (0.0, 0.282),
     'L0_conv_lin2_b': (0.0, 0.1),
     'L1_conv_ln1_g': (1.0, 0.6),
     'L1_conv_ln1_b': (0.0, 0.8),
     'L1_conv_qkv_b': (0.0, 0.27),
     'L1_conv_proj_b': (0.0, 0.1),
     'L1_conv_ln2_g': (1.0, 0.6),
     'L1_conv_ln2_b': (0.0, 0.8),
     'L1_conv_mlp_b1': (0.0, 0.29),
     'L1_conv_mlp_b2': (0.0, 0.1),
     'L2_conv_b1r': (0.0, 0.8),
     'L2_conv_b1i': (0.0, 0.8),
     'L2_conv_b2r': (0.0, 0.1),
     'L2_conv_b2i': (0.0, 0.1)}
    factors = {'L0_conv_qkv_w': 7.211,
     'L0_conv_rel_pos_h': 8.0,
     'L0_conv_rel_pos_w': 8.0,
     'L1_conv_qkv_w': 4.546,
     'L1_conv_rel_pos_h': 8.0,
     'L1_conv_rel_pos_w': 8.0,
     'L2_conv_w1r': 8.0,
     'L2_conv_w1i': 8.0,
     'L2_conv_w2r': 5.183,
     'L2_conv_w2i': 5.137,
     'L3_conv_w1': 5.635,
     'L3_conv_b1': 64.0,
     'L3_conv_w2': 4.649,
     'L3_conv_b2': 58.315}
    for name, (base, spread) in spreads.items():
        noise = np.random.default_rng([zlib.crc32(name.encode()), seed]).standard_normal(out[name].shape)
        drawn = base * np.exp(spread * noise) if base else spread * noise
        out[name] = jnp.asarray(drawn.astype(out[name].dtype))
    for name, factor in factors.items():
        out[name] = (out[name] * factor).astype(out[name].dtype)
    return out
```

```python
import concourse.bass as bass
from concourse import mybir
from contextlib import ExitStack

F32 = mybir.dt.float32
ALU = mybir.AluOpType
ACT = mybir.ActivationFunctionType
AX = mybir.AxisListType

B, HH, WW, C = 8, 16, 16, 192
PAIRS = B // 2
WS = 14
NH, HD = 12, 16
HALF = WS // 2 * WS
WIN = WS * WS
CUT = 2 * (HH * WW - WIN)
TOK = 2 * HH * WW
TILES = 5
SIZE = [HALF] * 4 + [CUT]
START = [HALF * t for t in range(5)]
KEYS = [HALF] * 4 + [CUT + 1]
G = C // 96
HG = NH // G
SLOT = 64
REL0 = 32
RW = 2 * WS
RT = 2 * WS - 1
UROW = 2 * RT * NH
MLP = 4 * C
MC = MLP // 128
QSCALE = HD ** -0.5
EPS = [1e-5, 1e-6]
BIG = -1.0e30
FREQ = HH * (WW // 2 + 1)
FC = FREQ // 2
LAMBDA = 0.01
FWD = [1.0 / 16, 1.0]
INV = [1.0 / 16, 1.0 / 256]
UNITS = 2 * NH
CUTS = 3


def build(nc, d):
    with ExitStack() as ctx:
        def sb(name, shape):
            return ctx.enter_context(nc.sbuf_tensor(name, shape, F32))

        def sem(name):
            return ctx.enter_context(nc.semaphore(name))

        bank = [ctx.enter_context(nc.psum_tensor(f"bank{i}", [128, 512], F32)) for i in range(8)]
        setup = sem("setup")
        preset = sem("preset")
        ident = sb("ident", [128, 128])
        half_pow = sb("half_pow", [128, TILES])
        attention_loop(nc, d, ctx, bank, setup, preset, ident, half_pow)
        fourier_loop(nc, d, bank)


def attention_loop(nc, d, outer, bank, setup, preset, ident, half_pow):
    with ExitStack() as ctx:
        def sb(name, shape):
            return ctx.enter_context(nc.sbuf_tensor(name, shape, F32))

        def sem(name):
            return ctx.enter_context(nc.semaphore(name))

        w_qkv = [sb(f"w_qkv{l}", [97, G, 3 * C]) for l in range(2)]
        w_rel = [sb(f"w_rel{l}", [96, 2 * RT * HG]) for l in range(2)]
        w_proj = [sb(f"w_proj{l}", [97, G, C]) for l in range(2)]
        w_up = [sb(f"w_up{l}", [96, G, MLP]) for l in range(2)]
        w_down = [sb(f"w_down{l}", [128, MC, C]) for l in range(2)]
        b_up = [sb(f"b_up{l}", [128, MC]) for l in range(2)]
        b_down = [sb(f"b_down{l}", [128, C]) for l in range(2)]
        affine = [sb(f"affine{l}", [96, 4, G]) for l in range(2)]
        cut_mask = sb("cut_mask", [CUT, CUT + 1])
        pad_mask = sb("pad_mask", [CUT, WIN])
        x_in = sb("x_in", [128, TILES, C])
        x_mid = sb("x_mid", [128, TILES, C])
        x_midb = sb("x_midb", [128, TILES, C])
        x_out = [sb(f"x_out{l}", [128, TILES, C]) for l in range(2)]
        seed = sb("seed", [1, 1])
        wait_pad = sb("wait_pad", [1, 1])
        xn = sb("xn", [128, TILES, C])
        stats = sb("stats", [128, TILES, 6])
        moments = sb("moments", [128, TILES, 2])
        veps = sb("veps", [128, TILES])
        ones = sb("ones", [128, 1])
        eps = sb("eps", [128, 2, TILES])
        rstd = sb("rstd", [128, TILES])
        xT = sb("xT", [97, G, TOK + 1])
        q_tok = sb("q_tok", [128, TILES, NH * SLOT])
        q_flat = sb("q_flat", [128, TILES, C])
        k_tok = sb("k_tok", [128, TILES, NH * SLOT])
        v_pad = sb("v_pad", [128, TILES, NH, 96])
        qT = sb("qT", [96, G, TOK])
        dist = sb("dist", [128, TILES, UROW])
        rel = sb("rel", [128, TILES, RW * NH])
        pad_logit = sb("pad_logit", [CUT, NH, WIN])
        q_aug = sb("q_aug", [128, NH // 2, TOK])
        k_aug = sb("k_aug", [128, NH, TOK + 1])
        probs = sb("probs", [128, 3, 4 * (CUT + 1)])
        probsT = sb("probsT", [128, 2, 4 * CUT])
        cut_s = sb("cut_s", [CUT, 4, CUT + 1])
        neg_max = sb("neg_max", [128, 3, 4])
        pad_bias = sb("pad_bias", [CUT, 4])
        real_max = sb("real_max", [CUT, 4])
        pad_top = sb("pad_top", [CUT, NH])
        row_sum = sb("row_sum", [128, 3, 4])
        pad_sum = sb("pad_sum", [128, 4])
        inv_sum = sb("inv_sum", [128, 3, 4])
        oT = sb("oT", [97, G, TOK])
        hidden = dist[:, :, :].rearrange("p t u -> p (t u)")[:, 0:MC * TOK].rearrange("p (m k) -> p m k", m=MC)

        names = ("x_loaded moments_ready rstd_ready veps_ready xn_ready xT_done xT_lo xT_hi qkv_done kq_copied "
                 "v_copied qT_done qT_lo qT_hi dist_done dist_lo dist_hi dist_stored rel_placed pad_ready pad_half "
                 "pad_topped kT_done k_even k_odd qaug_done qaug_lo qaug_hi scores_done max_ready exp_done "
                 "inv_ready probs_ready probsT_done probsT_ready pv_done oT_ready proj_done mid_ready "
                 "midb_ready up_done gelu_done down_done out_ready stored order_dve order_act").split()
        S = {n: sem(n) for n in names}
        rel_loaded = [sem(f"rel_loaded{t}") for t in range(TILES)]
        PER = dict(moments_ready=2, veps_ready=2, rstd_ready=2, xn_ready=10, xT_done=2, xT_lo=2, xT_hi=2, qkv_done=5,
                   kq_copied=5, v_copied=5, qT_done=1, qT_lo=1, qT_hi=1, dist_done=10, dist_lo=5, dist_hi=5,
                   dist_stored=80, rel_placed=5, pad_ready=1, pad_half=1, pad_topped=1, kT_done=10, k_even=10,
                   k_odd=10, qaug_done=10, qaug_lo=5, qaug_hi=5, scores_done=27, max_ready=27, exp_done=27,
                   inv_ready=27, probs_ready=27, probsT_done=27, probsT_ready=27, pv_done=27, oT_ready=6,
                   proj_done=5, mid_ready=5, midb_ready=1, up_done=6, gelu_done=6, down_done=5, out_ready=5,
                   order_dve=14, order_act=3)
        block = ctx.enter_context(nc.Block())

        def need(eng, name, n, k):
            eng.wait_ge(S[name], n * PER[name] + k)

        SETUP = 16 * (13 * 2 + 8)

        @block.sync
        def _(sp):
            def load(dst, src):
                sp.dma_start(dst, src).then_inc(setup, 16)

            def load_x(i):
                sp.dma_start(x_in[0:HALF, 0:4, :],
                             d["x"][i, 0:4 * HALF, :].rearrange("(t n) c -> n t c", t=4)).then_inc(S["x_loaded"], 16)
                sp.dma_start(x_in[0:CUT, 4, :], d["x"][i, 4 * HALF:TOK, :]).then_inc(S["x_loaded"], 16)

            load_x(0)
            load(ident[:, :], d["ident"])
            load(cut_mask[:, :], d["cut_mask"])
            load(pad_mask[:, :], d["pad_mask"])
            for t in range(TILES):
                load(k_tok[0:KEYS[t], t, :], d["onehot"][4 if t == 4 else t % 2, 0:KEYS[t], :])
            for l in range(2):
                load(affine[l][:, 0, :], d["ln1_w"][l])
                load(affine[l][:, 1, :], d["ln1_b"][l])
                load(affine[l][:, 2, :], d["ln2_w"][l])
                load(affine[l][:, 3, :], d["ln2_b"][l])
                load(w_qkv[l][0:96, :, :], d["qkv_w"][l].rearrange("(g p) n -> p g n", g=G))
                load(w_qkv[l][96:97, 0, :], d["qkv_b"][l].rearrange("(a n) -> a n", a=1))
                load(w_rel[l][:, :], d["rel"][l])
                load(w_proj[l][0:96, :, :], d["proj_w"][l].rearrange("(g p) n -> p g n", g=G))
                load(w_proj[l][96:97, 0, :], d["proj_b"][l].rearrange("(a n) -> a n", a=1))
                load(w_up[l][:, :, :], d["up_w"][l].rearrange("(g p) n -> p g n", g=G))
                load(w_down[l][:, :, :], d["down_w"][l].rearrange("(g p) n -> p g n", g=MC))
                load(b_up[l][:, :], d["up_b"][l])
                load(b_down[l][:, :], d["down_b"][l].rearrange("(a n) -> a n", a=1).broadcast_to([128, C]))
            sp.dma_start(seed[:, :], d["ident"][0:1, 0:1]).then_inc(S["stored"], 16)

            U, UO = d["dist"].tensor, UROW * TOK

            def gather(t, l, part, dims, first, at, count):
                src = bass.AP(U, l * UO + first, dims + [[1, WS * NH]])
                sp.dma_start(rel[at:at + count, t, part * WS * NH:(part + 1) * WS * NH], src)\
                    .then_inc(rel_loaded[t], 16)

            with sp.Fori(0, PAIRS) as i:
                for l in range(2):
                    n = 2 * i + l
                    for t in range(TILES):
                        need(sp, "dist_lo", n, t + 1)
                        need(sp, "dist_hi", n, t + 1)
                        sp.dma_start(d["dist"][l, START[t]:START[t] + SIZE[t], :], dist[0:SIZE[t], t, :])\
                            .then_inc(S["dist_stored"], 16)
                    need(sp, "dist_stored", n, 80)
                    R, D = UROW, NH
                    for t in range(4):
                        base = START[t] * R
                        gather(t, l, 0, [[WS * R - D, 7], [R, WS]], base + (WS - 1 - 7 * (t % 2)) * D, 0, HALF)
                        gather(t, l, 1, [[WS * R, 7], [R - D, WS]], base + RT * NH + (WS - 1) * D, 0, HALF)
                    base, top = START[4] * R, (WS - 1) * D
                    for a in range(2):
                        at = 28 * a
                        gather(4, l, 0, [[2 * R - D, WS], [R, 2]], base + at * R + top, at, 28)
                        gather(4, l, 1, [[2 * R, WS], [R - D, 2]], base + at * R + RT * NH + top, at, 28)
                        at = 56 + 28 * a
                        gather(4, l, 0, [[WS * R - D, 2], [R, WS]], base + at * R + top, at, 28)
                        gather(4, l, 1, [[WS * R, 2], [R - D, WS]], base + at * R + RT * NH + top, at, 28)
                        at = 112 + 4 * a
                        gather(4, l, 0, [[2 * R - D, 2], [R, 2]], base + at * R + top, at, 4)
                        gather(4, l, 1, [[2 * R, 2], [R - D, 2]], base + at * R + RT * NH + top, at, 4)
                    if l == 0:
                        need(sp, "mid_ready", n, 5)
                        sp.dma_start(x_in[0:HALF, 0:4, :], d["x"][bass.ds(i + 1, 1), 0:4 * HALF, :]
                                     .rearrange("o (t n) c -> (o n) t c", t=4)).then_inc(S["x_loaded"], 16)
                        sp.dma_start(x_in[0:CUT, 4, :], d["x"][bass.ds(i + 1, 1), 4 * HALF:TOK, :]
                                     .rearrange("o n c -> (o n) c")).then_inc(S["x_loaded"], 16)
                need(sp, "out_ready", 2 * i + 1, 5)
                for a in range(2):
                    img = d["mid"][bass.ds(2 * i + a, 1)].rearrange("o h w c -> (o h) w c")
                    for r in range(2):
                        sp.dma_start(img[7 * r:7 * r + 7, 0:WS, :], x_out[1][0:HALF, 2 * a + r, :])\
                            .then_inc(S["stored"], 16)
                    sp.dma_start(img[0:WS, WS:WW, :], x_out[1][28 * a:28 * a + 28, 4, :]).then_inc(S["stored"], 16)
                    sp.dma_start(img[WS:HH, 0:WS, :], x_out[1][56 + 28 * a:84 + 28 * a, 4, :])\
                        .then_inc(S["stored"], 16)
                    sp.dma_start(img[WS:HH, WS:WW, :], x_out[1][112 + 4 * a:116 + 4 * a, 4, :])\
                        .then_inc(S["stored"], 16)
            sp.wait_ge(S["stored"], 16 + 160 * PAIRS)
            sp.wait_ge(S["x_loaded"], 32 * (PAIRS + 1))

        @block.gpsimd
        def _(pool):
            g = nc.gpsimd
            g.memset(half_pow[:, :], -0.5).then_inc(preset, 1)
            g.memset(ones[:, :], 1.0).then_inc(preset, 1)
            for l in range(2):
                g.memset(eps[:, l, :], EPS[l]).then_inc(preset, 1)
            g.memset(q_tok[:, :, :], 0.0).then_inc(preset, 1)
            g.memset(v_pad[:, :, :, :], 0.0).then_inc(preset, 1)
            g.memset(moments[:, :, :], 1.0).then_inc(preset, 1)
            pool.wait_ge(preset, PRESETS)
            pool.wait_ge(setup, SETUP)

            def copy(dst, src):
                return g.tensor_tensor(dst, src, ones[0:src.shape[0], :].unsqueeze(2).to_broadcast(src.shape),
                                       ALU.mult)

            def rsqrt(n, l, k):
                need(pool, "moments_ready", n, k)
                g.tensor_tensor(veps[:, :], moments[:, :, 1], eps[:, l, :], ALU.add).then_inc(S["veps_ready"], 1)
                need(pool, "veps_ready", n, k)
                g.tensor_tensor(rstd[:, :], veps[:, :], half_pow[:, :], ALU.pow).then_inc(S["rstd_ready"], 1)

            def normalise(n, u):
                need(pool, "inv_ready", n, u + 1)
                if u < UNITS:
                    rows, k, m = HALF, 2, WIN
                else:
                    rows, k, m = CUT, 4, CUT + 1
                p = probs[0:rows, u % 3, 0:k * m].rearrange("p (k m) -> p k m", k=k)
                g.tensor_tensor(p, p, inv_sum[0:rows, u % 3, 0:k].unsqueeze(2).to_broadcast([rows, k, m]),
                                ALU.mult).then_inc(S["probs_ready"], 1)

            with pool.Fori(0, PAIRS) as i:
                for l in range(2):
                    n = 2 * i + l
                    rsqrt(n, l, 1)
                    for t in range(TILES):
                        need(pool, "kq_copied", n, t + 1)
                        src = q_flat[0:SIZE[t], t, :].rearrange("p (h c) -> p h c", c=HD)
                        copy(q_tok[0:SIZE[t], t, :].rearrange("p (h s) -> p h s", s=SLOT)[:, :, 0:HD], src)
                    for t in range(TILES):
                        pool.wait_ge(rel_loaded[t], n * (32 if t < 4 else 192) + (32 if t < 4 else 192))
                        dst = q_tok[0:SIZE[t], t, :].rearrange("p (h s) -> p h s", s=SLOT)[:, :, REL0:REL0 + RW]
                        src = rel[0:SIZE[t], t, :].rearrange("p (r h) -> p h r", h=NH)
                        copy(dst, src).then_inc(S["rel_placed"], 1)
                    r4 = rel[0:CUT, 4, :].rearrange("p (a r h) -> p a h r", a=2, h=NH)
                    lg = pad_logit[:, :, :].rearrange("p h (y x) -> p h y x", y=WS)
                    g.tensor_tensor(lg, r4[:, 0].unsqueeze(3).to_broadcast([CUT, NH, WS, WS]),
                                    r4[:, 1].unsqueeze(2).to_broadcast([CUT, NH, WS, WS]), ALU.add)\
                        .then_inc(S["pad_half"], 1)
                    need(pool, "pad_half", n, 1)
                    g.tensor_tensor(pad_logit[:, :, :], pad_logit[:, :, :],
                                    pad_mask[:, :].unsqueeze(1).to_broadcast([CUT, NH, WIN]), ALU.add)\
                        .then_inc(S["pad_ready"], 1)
                    for u in range(UNITS + CUTS):
                        normalise(n, u)
                    rsqrt(n, l, 2)
                    need(pool, "mid_ready", n, 5)
                    g.tensor_tensor(x_midb[0:CUT, :, :], x_mid[0:CUT, :, :],
                                    b_down[l][0:CUT, :].unsqueeze(1).to_broadcast([CUT, TILES, C]), ALU.add)\
                        .then_inc(S["midb_ready"], 1)

        @block.vector
        def _(dve):
            v = nc.vector
            v.memset(x_mid[64:128, :, :], 0.0).then_inc(preset, 1)
            v.memset(xT[0:96, :, TOK:TOK + 1], 0.0).then_inc(preset, 1)
            v.memset(xT[96:97, 0, :], 1.0).then_inc(preset, 1)
            v.memset(oT[96:97, 0, :], 1.0).then_inc(preset, 1)
            for p in range(NH // 2):
                v.memset(k_aug[64:128, 2 * p, :], 0.0).then_inc(preset, 1)
                v.memset(k_aug[0:64, 2 * p + 1, :], 0.0).then_inc(preset, 1)
            dve.wait_ge(setup, SETUP)
            dve.wait_ge(preset, PRESETS)
            chain = [0]

            def after(n, ins):
                chain[0] += 1
                ins.then_inc(S["order_dve"], 1)
                need(dve, "order_dve", n, chain[0])

            def layer_norm(n, src, k):
                for t in range(TILES):
                    last = v.bn_stats(stats[0:SIZE[t], t, :], src[0:SIZE[t], t, :])
                after(n, last)
                v.memset(wait_pad[:, :], 0.0)
                for t in range(TILES):
                    last = v.bn_aggr(moments[0:SIZE[t], t, :], stats[0:SIZE[t], t, :])
                last.then_inc(S["moments_ready"], 1)
                need(dve, "moments_ready", n, k)
                need(dve, "rstd_ready", n, k)
                for t in range(TILES):
                    v.tensor_scalar(xn[0:SIZE[t], t, :], src[0:SIZE[t], t, :], moments[0:SIZE[t], t, 0:1],
                                    rstd[0:SIZE[t], t:t + 1], ALU.subtract, ALU.mult).then_inc(S["xn_ready"], 1)

            def attend(n, u):
                s = bank[[0, 1, 6][u % 3]]
                need(dve, "scores_done", n, u + 1)
                if u < UNITS:
                    v.tensor_reduce(neg_max[0:HALF, u % 3, 0:2],
                                    s[0:HALF, 0:2 * WIN].rearrange("p (r m) -> p r m", r=2), AX.X, ALU.max,
                                    negate=True).then_inc(S["max_ready"], 1)
                    return
                sg = u - UNITS
                if sg:
                    need(dve, "exp_done", n, u)
                after(n, v.tensor_tensor(cut_s[:, :, :], s[0:CUT, 0:4 * (CUT + 1)].rearrange("p (j m) -> p j m", j=4),
                                         cut_mask[:, :].unsqueeze(1).to_broadcast([CUT, 4, CUT + 1]), ALU.add))
                v.tensor_reduce(real_max[:, :], cut_s[:, :, 0:CUT], AX.X, ALU.max)
                after(n, v.tensor_tensor(pad_bias[:, :], cut_s[:, :, CUT], pad_top[:, 4 * sg:4 * sg + 4], ALU.add))
                after(n, v.tensor_tensor(real_max[:, :], real_max[:, :], pad_bias[:, :], ALU.max))
                v.tensor_scalar(neg_max[0:CUT, u % 3, :], real_max[:, :], -1.0, None, ALU.mult)
                v.tensor_tensor(pad_bias[:, :], cut_s[:, :, CUT], real_max[:, :], ALU.subtract)\
                    .then_inc(S["max_ready"], 1)

            def invert(n, u):
                need(dve, "exp_done", n, u + 1)
                rows, k = (HALF, 2) if u < UNITS else (CUT, 4)
                if u >= UNITS:
                    after(n, v.tensor_tensor(row_sum[0:CUT, u % 3, :], row_sum[0:CUT, u % 3, :], pad_sum[0:CUT, :],
                                             ALU.add))
                v.reciprocal(inv_sum[0:rows, u % 3, 0:k], row_sum[0:rows, u % 3, 0:k]).then_inc(S["inv_ready"], 1)

            def copy_probsT(n, u):
                need(dve, "probsT_done", n, u + 1)
                if u >= 2:
                    need(dve, "pv_done", n, u - 1)
                rows, m = (HALF, 4 * HALF) if u < UNITS else (CUT + 1, 4 * CUT)
                v.tensor_copy(probsT[0:rows, u % 2, 0:m], bank[2 + u % 2][0:rows, 0:m]).then_inc(S["probsT_ready"], 1)

            with dve.Fori(0, PAIRS) as i:
                for l in range(2):
                    n = 2 * i + l
                    chain[0] = 0
                    if l == 0:
                        dve.wait_ge(S["x_loaded"], 32 * i + 32)
                    src = x_in if l == 0 else x_out[0]
                    layer_norm(n, src, 1)
                    need(dve, "xT_done", n, 1)
                    v.tensor_scalar(xT[0:96, 0, 0:TOK], bank[0][0:96, :], affine[l][:, 0, 0:1], affine[l][:, 1, 0:1],
                                    ALU.mult, ALU.add).then_inc(S["xT_lo"], 1)
                    for t in range(TILES):
                        need(dve, "qkv_done", n, t + 1)
                        for gg in range(G):
                            dst = v_pad[0:KEYS[t], t, HG * gg:HG * gg + HG, :].rearrange("p h s -> p (h s)")
                            dst = bass.AP(dst.tensor, dst.offset, [dst.ap[0], [96 + HD, HG], [1, HD]])
                            last = v.tensor_copy(dst, bank[2 + t % 2][0:KEYS[t], C + 96 * gg:C + 96 * gg + 96]
                                                 .rearrange("p (h c) -> p h c", c=HD))
                        last.then_inc(S["v_copied"], 1)
                    need(dve, "qT_done", n, 1)
                    v.tensor_copy(qT[:, 0, :], bank[0][0:96, :]).then_inc(S["qT_lo"], 1)
                    for t in range(TILES):
                        need(dve, "dist_done", n, 2 * t + 1)
                        v.tensor_copy(dist[0:SIZE[t], t, :].rearrange("p (r h) -> p r h", h=NH)[:, :, 0:HG],
                                      bank[2 + 2 * t % 4][0:SIZE[t], 0:2 * RT * HG]
                                      .rearrange("p (r h) -> p r h", h=HG)).then_inc(S["dist_lo"], 1)
                    for t in range(TILES):
                        for b in range(2):
                            need(dve, "kT_done", n, 2 * t + b + 1)
                            v.tensor_copy(k_aug[64:128, 6 * b + 1:6 * b + 6:2, START[t]:START[t] + KEYS[t]],
                                          bank[6 + b][64:128, 0:3 * KEYS[t]].rearrange("p (k m) -> p k m", k=3))\
                                .then_inc(S["k_odd"], 1)
                    for t in range(TILES):
                        need(dve, "qaug_done", n, 2 * t + 2)
                        v.tensor_copy(q_aug[:, 3:6, START[t]:START[t] + SIZE[t]],
                                      bank[7][:, 0:3 * SIZE[t]].rearrange("p (k m) -> p k m", k=3))\
                            .then_inc(S["qaug_hi"], 1)
                    need(dve, "pad_ready", n, 1)
                    v.tensor_reduce(pad_top[:, :], pad_logit[:, :, :], AX.X, ALU.max).then_inc(S["pad_topped"], 1)
                    need(dve, "pad_topped", n, 1)
                    ALLU = UNITS + CUTS
                    for u in range(ALLU + 2):
                        if u < ALLU:
                            attend(n, u)
                        if 1 <= u <= ALLU:
                            invert(n, u - 1)
                        if u >= 2:
                            copy_probsT(n, u - 2)
                    for t in range(TILES):
                        need(dve, "proj_done", n, t + 1)
                        v.tensor_tensor(x_mid[0:SIZE[t], t, :], bank[2 + t % 2][0:SIZE[t], 0:C],
                                        src[0:SIZE[t], t, :], ALU.add).then_inc(S["mid_ready"], 1)
                    need(dve, "mid_ready", n, 5)
                    layer_norm(n, x_mid, 2)
                    need(dve, "xT_done", n, 2)
                    v.tensor_scalar(xT[0:96, 0, 0:TOK], bank[0][0:96, :], affine[l][:, 2, 0:1], affine[l][:, 3, 0:1],
                                    ALU.mult, ALU.add).then_inc(S["xT_lo"], 1)
                    need(dve, "midb_ready", n, 1)
                    if l == 1:
                        dve.wait_ge(S["stored"], 16 + 160 * i)
                    for t in range(TILES):
                        need(dve, "down_done", n, t + 1)
                        v.tensor_tensor(x_out[l][0:SIZE[t], t, :], bank[t % 4][0:SIZE[t], 0:C],
                                        x_midb[0:SIZE[t], t, :], ALU.add).then_inc(S["out_ready"], 1)
                    need(dve, "out_ready", n, 5)
                    assert chain[0] == PER["order_dve"], chain[0]

        @block.scalar
        def _(act):
            s = nc.scalar
            act.wait_ge(setup, SETUP)
            act.wait_ge(preset, PRESETS)

            def exps(n, u):
                need(act, "max_ready", n, u + 1)
                if u >= 3:
                    need(act, "probsT_done", n, u - 2)
                sl = u % 3
                if u < UNITS:
                    for r in range(2):
                        last = s.activation(probs[0:HALF, sl, r * WIN:(r + 1) * WIN],
                                            bank[[0, 1, 6][sl]][0:HALF, r * WIN:(r + 1) * WIN], ACT.Exp,
                                            bias=neg_max[0:HALF, sl, r:r + 1], accum_out=row_sum[0:HALF, sl, r:r + 1])
                    last.then_inc(S["exp_done"], 1)
                    return
                sg = u - UNITS
                if sg:
                    need(act, "inv_ready", n, u)
                m = CUT + 1
                for j in range(4):
                    s.activation(probs[0:CUT, sl, j * m:j * m + CUT], cut_s[:, j, 0:CUT], ACT.Exp,
                                 bias=neg_max[0:CUT, sl, j:j + 1], accum_out=row_sum[0:CUT, sl, j:j + 1])
                    last = s.activation(pad_logit[:, 4 * sg + j, :], pad_logit[:, 4 * sg + j, :], ACT.Exp, bias=pad_bias[:, j:j + 1],
                                 accum_out=pad_sum[0:CUT, j:j + 1])
                last.then_inc(S["order_act"], 1)
                need(act, "order_act", n, sg + 1)
                s.activation(probs[0:CUT, sl, 0:4 * m].rearrange("p (j m) -> p j m", j=4)[:, :, CUT], pad_sum[0:CUT, :],
                             ACT.Copy).then_inc(S["exp_done"], 1)

            def copy_oT(n, k):
                need(act, "pv_done", n, OT_AT[k])
                a, gg = k // 2, k % 2
                m, lo = (WIN, WIN * a) if a < 2 else (CUT, 4 * HALF)
                s.activation(oT[0:96, gg, lo:lo + m], bank[4 + k % 2][0:96, 0:m], ACT.Copy)\
                    .then_inc(S["oT_ready"], 1)

            with act.Fori(0, PAIRS) as i:
                for l in range(2):
                    n = 2 * i + l
                    need(act, "xT_done", n, 1)
                    s.activation(xT[0:96, 1, 0:TOK], bank[1][0:96, :], ACT.Identity, bias=affine[l][:, 1, 1:2],
                                 scale=affine[l][:, 0, 1:2]).then_inc(S["xT_hi"], 1)
                    for t in range(TILES):
                        need(act, "qkv_done", n, t + 1)
                        need(act, "v_copied", n, t + 1)
                        s.activation(k_tok[0:KEYS[t], t, :].rearrange("p (h s) -> p h s", s=SLOT)[:, :, 0:HD],
                                     bank[2 + t % 2][0:KEYS[t], 0:C].rearrange("p (h c) -> p h c", c=HD), ACT.Copy,
                                     scale=QSCALE)
                        s.activation(q_flat[0:SIZE[t], t, :], bank[4 + t % 2][0:SIZE[t], 0:C], ACT.Copy)\
                            .then_inc(S["kq_copied"], 1)
                    need(act, "qT_done", n, 1)
                    s.activation(qT[:, 1, :], bank[1][0:96, :], ACT.Copy).then_inc(S["qT_hi"], 1)
                    for t in range(TILES):
                        need(act, "dist_done", n, 2 * t + 2)
                        s.activation(dist[0:SIZE[t], t, :].rearrange("p (r h) -> p r h", h=NH)[:, :, HG:NH],
                                     bank[2 + (2 * t + 1) % 4][0:SIZE[t], 0:2 * RT * HG]
                                     .rearrange("p (r h) -> p r h", h=HG), ACT.Copy).then_inc(S["dist_hi"], 1)
                    for t in range(TILES):
                        for b in range(2):
                            need(act, "kT_done", n, 2 * t + b + 1)
                            s.activation(k_aug[0:64, 6 * b:6 * b + 5:2, START[t]:START[t] + KEYS[t]],
                                         bank[6 + b][0:64, 0:3 * KEYS[t]].rearrange("p (k m) -> p k m", k=3),
                                         ACT.Copy).then_inc(S["k_even"], 1)
                    for t in range(TILES):
                        need(act, "qaug_done", n, 2 * t + 1)
                        s.activation(q_aug[:, 0:3, START[t]:START[t] + SIZE[t]],
                                     bank[6][:, 0:3 * SIZE[t]].rearrange("p (k m) -> p k m", k=3),
                                     ACT.Copy).then_inc(S["qaug_lo"], 1)
                    done = 0
                    for u in range(UNITS + CUTS + 4):
                        if u < UNITS + CUTS:
                            exps(n, u)
                        while done < 6 and OT_AT[done] <= u - 3:
                            copy_oT(n, done)
                            done += 1
                    need(act, "xT_done", n, 2)
                    s.activation(xT[0:96, 1, 0:TOK], bank[1][0:96, :], ACT.Identity, bias=affine[l][:, 3, 1:2],
                                 scale=affine[l][:, 2, 1:2]).then_inc(S["xT_hi"], 1)
                    for f in range(MC):
                        need(act, "up_done", n, f + 1)
                        s.activation(hidden[:, f, :], bank[4 + f % 4][:, :], ACT.Gelu, bias=b_up[l][:, f:f + 1])\
                            .then_inc(S["gelu_done"], 1)

        @block.tensor
        def _(pe):
            t_ = nc.tensor
            pe.wait_ge(setup, SETUP)
            pe.wait_ge(preset, PRESETS)

            def transpose_xn(n, k):
                for t in range(TILES):
                    need(pe, "xn_ready", n, 5 * (k - 1) + t + 1)
                    for gg in range(G):
                        last = t_.transpose(bank[gg][0:96, START[t]:START[t] + SIZE[t]],
                                            xn[0:SIZE[t], t, 96 * gg:96 * gg + 96], ident[0:SIZE[t], 0:SIZE[t]])
                last.then_inc(S["xT_done"], 1)
                need(pe, "xT_lo", n, k)
                need(pe, "xT_hi", n, k)

            def scores(n, u):
                sbank = bank[[0, 1, 6][u % 3]]
                if u >= 3:
                    need(pe, "exp_done", n, u - 2)
                if u < UNITS:
                    a, h = u // NH, u % NH
                    for r in range(2):
                        last = t_.matmul(sbank[0:HALF, r * WIN:(r + 1) * WIN],
                                         q_aug[:, h // 2, START[2 * a + r]:START[2 * a + r] + HALF],
                                         k_aug[:, h, WIN * a:WIN * a + WIN], start=True, stop=True)
                else:
                    m = CUT + 1
                    for j in range(4):
                        h = 4 * (u - UNITS) + j
                        last = t_.matmul(sbank[0:CUT, j * m:(j + 1) * m], q_aug[:, h // 2, 4 * HALF:TOK],
                                         k_aug[:, h, 4 * HALF:TOK + 1], start=True, stop=True)
                last.then_inc(S["scores_done"], 1)

            def transpose_probs(n, u):
                need(pe, "probs_ready", n, u + 1)
                if u >= 2:
                    need(pe, "probsT_ready", n, u - 1)
                o = bank[2 + u % 2]
                if u < UNITS:
                    for kk in range(2):
                        for r in range(2):
                            last = t_.transpose(o[0:HALF, (2 * kk + r) * HALF:(2 * kk + r + 1) * HALF],
                                                probs[0:HALF, u % 3, r * WIN + kk * HALF:r * WIN + (kk + 1) * HALF],
                                                ident[0:HALF, 0:HALF])
                else:
                    m = CUT + 1
                    for j in range(4):
                        last = t_.transpose(o[0:m, j * CUT:(j + 1) * CUT], probs[0:CUT, u % 3, j * m:(j + 1) * m],
                                            ident[0:CUT, 0:CUT])
                last.then_inc(S["probsT_done"], 1)

            def values(n, u):
                need(pe, "probsT_ready", n, u + 1)
                if u < UNITS:
                    a, h = u // NH, u % NH
                    k, hh = 2 * a + h // HG, h % HG
                    if hh == 0 and k >= 2:
                        need(pe, "oT_ready", n, k - 1)
                    for kk in range(2):
                        last = t_.matmul(bank[4 + k % 2][0:96, 0:WIN], v_pad[0:HALF, 2 * a + kk, h, :],
                                         probsT[0:HALF, u % 2, kk * WIN:(kk + 1) * WIN],
                                         start=(hh == 0 and kk == 0), stop=(hh == HG - 1 and kk == 1))
                else:
                    for j in range(4):
                        h = 4 * (u - UNITS) + j
                        k = 4 + h // HG
                        if h % HG == 0:
                            need(pe, "oT_ready", n, k - 1)
                        last = t_.matmul(bank[4 + k % 2][0:96, 0:CUT], v_pad[0:CUT + 1, 4, h, :],
                                         probsT[0:CUT + 1, u % 2, j * CUT:(j + 1) * CUT],
                                         start=(h % HG == 0), stop=(h % HG == HG - 1))
                last.then_inc(S["pv_done"], 1)

            with pe.Fori(0, PAIRS) as i:
                for l in range(2):
                    n = 2 * i + l
                    transpose_xn(n, 1)
                    for t in range(TILES):
                        if t >= 2:
                            need(pe, "v_copied", n, t - 1)
                            need(pe, "kq_copied", n, t - 1)
                        for gg in range(G):
                            rows = 97 - gg
                            t_.matmul(bank[2 + t % 2][0:KEYS[t], 0:2 * C], xT[0:rows, gg, START[t]:START[t] + KEYS[t]],
                                      w_qkv[l][0:rows, gg, C:3 * C], start=(gg == 0), stop=(gg == 1))
                        for gg in range(G):
                            rows = 97 - gg
                            last = t_.matmul(bank[4 + t % 2][0:SIZE[t], 0:C],
                                             xT[0:rows, gg, START[t]:START[t] + SIZE[t]],
                                             w_qkv[l][0:rows, gg, 0:C], start=(gg == 0), stop=(gg == 1))
                        last.then_inc(S["qkv_done"], 1)
                    for t in range(TILES):
                        need(pe, "kq_copied", n, t + 1)
                        for gg in range(G):
                            last = t_.transpose(bank[gg][0:96, START[t]:START[t] + SIZE[t]],
                                                q_flat[0:SIZE[t], t, 96 * gg:96 * gg + 96],
                                                ident[0:SIZE[t], 0:SIZE[t]])
                    last.then_inc(S["qT_done"], 1)
                    need(pe, "qT_lo", n, 1)
                    need(pe, "qT_hi", n, 1)
                    need(pe, "v_copied", n, 5)
                    for t in range(TILES):
                        for gg in range(G):
                            if t >= 2:
                                need(pe, ["dist_lo", "dist_hi"][gg], n, t - 1)
                            t_.matmul(bank[2 + (2 * t + gg) % 4][0:SIZE[t], 0:2 * RT * HG],
                                      qT[:, gg, START[t]:START[t] + SIZE[t]], w_rel[l][:, :], start=True, stop=True)\
                                .then_inc(S["dist_done"], 1)
                    for t in range(TILES):
                        for b in range(2):
                            if t >= 1:
                                need(pe, "k_even", n, 2 * t + b - 1)
                                need(pe, "k_odd", n, 2 * t + b - 1)
                            for p in range(3):
                                last = t_.transpose(bank[6 + b][:, p * KEYS[t]:(p + 1) * KEYS[t]],
                                                    k_tok[0:KEYS[t], t, 128 * (3 * b + p):128 * (3 * b + p) + 128],
                                                    ident[0:KEYS[t], 0:KEYS[t]])
                            last.then_inc(S["kT_done"], 1)
                    need(pe, "k_even", n, 10)
                    need(pe, "k_odd", n, 10)
                    for t in range(TILES):
                        need(pe, "rel_placed", n, t + 1)
                        for b in range(2):
                            if t >= 1:
                                need(pe, ["qaug_lo", "qaug_hi"][b], n, t)
                            for p in range(3):
                                last = t_.transpose(bank[6 + b][:, p * SIZE[t]:(p + 1) * SIZE[t]],
                                                    q_tok[0:SIZE[t], t, 128 * (3 * b + p):128 * (3 * b + p) + 128],
                                                    ident[0:SIZE[t], 0:SIZE[t]])
                            last.then_inc(S["qaug_done"], 1)
                    need(pe, "qaug_lo", n, 5)
                    need(pe, "qaug_hi", n, 5)
                    need(pe, "dist_lo", n, 5)
                    need(pe, "dist_hi", n, 5)
                    for u in range(UNITS + CUTS + 3):
                        if u < UNITS + CUTS:
                            scores(n, u)
                        if 2 <= u < UNITS + CUTS + 2:
                            transpose_probs(n, u - 2)
                        if u >= 3:
                            values(n, u - 3)
                    need(pe, "oT_ready", n, 6)
                    for t in range(TILES):
                        if t >= 2:
                            need(pe, "mid_ready", n, t - 1)
                        for gg in range(G):
                            rows = 97 - gg
                            last = t_.matmul(bank[2 + t % 2][0:SIZE[t], 0:C], oT[0:rows, gg, START[t]:START[t] + SIZE[t]],
                                             w_proj[l][0:rows, gg, :], start=(gg == 0), stop=(gg == 1))
                        last.then_inc(S["proj_done"], 1)
                    transpose_xn(n, 2)
                    for f in range(MC):
                        if f >= 4:
                            need(pe, "gelu_done", n, f - 3)
                        for gg in range(G):
                            last = t_.matmul(bank[4 + f % 4][:, :], w_up[l][:, gg, 128 * f:128 * f + 128],
                                             xT[0:96, gg, 0:TOK], start=(gg == 0), stop=(gg == 1))
                        last.then_inc(S["up_done"], 1)
                    for t in range(TILES):
                        if t >= 4:
                            need(pe, "out_ready", n, t - 3)
                        for f in range(MC):
                            if t == 0:
                                need(pe, "gelu_done", n, f + 1)
                            last = t_.matmul(bank[t % 4][0:SIZE[t], 0:C], hidden[:, f, START[t]:START[t] + SIZE[t]],
                                             w_down[l][:, f, :], start=(f == 0), stop=(f == MC - 1))
                        last.then_inc(S["down_done"], 1)


PRESETS = 9 + NH + 1 + 1
OT_AT = [6, 12, 18, 24, 26, 27]


def fourier_loop(nc, d, bank):
    with ExitStack() as ctx:
        def sb(name, shape):
            return ctx.enter_context(nc.sbuf_tensor(name, shape, F32))

        def sem(name):
            return ctx.enter_context(nc.semaphore(name))

        fwd = sb("fwd", [128, 2, 2 * FREQ])
        inv = sb("inv", [FC, 4, 2 * 128])
        w1 = [sb(f"w1_{l}", [96, G, 3, 96]) for l in range(2)]
        w2 = [sb(f"w2_{l}", [97, G, 3, 96]) for l in range(2)]
        b1 = [sb(f"b1_{l}", [96, 2, G]) for l in range(2)]
        y_in = sb("y_in", [128, 4, C])
        y_mid = sb("y_mid", [128, 4, C])
        y_out = sb("y_out", [128, 4, C])
        xf = sb("xf", [96, G, 2, 2, FREQ])
        o1 = sb("o1", [97, G, 2, 2, FREQ])
        seed = sb("f_seed", [1, 1])
        clamp = sb("clamp", [FC, 4, G * 2 * 96])
        o2 = sb("o2", [FC, 4, 2, C])
        setup = sem("f_setup")
        preset = sem("f_preset")
        names = ("f_loaded fwd_done xf_a xf_b mix1_done relu_done mix2_done clamped o2_ready inv_done y_ready "
                 "f_stored").split()
        S = {n: sem(n) for n in names}
        PER = dict(fwd_done=4, xf_a=2, xf_b=2, mix1_done=4, relu_done=4, mix2_done=4, clamped=4, o2_ready=4,
                   inv_done=4, y_ready=4)
        SETUP = 16 * (2 + 2 * 10)

        def need(eng, name, n, k):
            eng.wait_ge(S[name], n * PER[name] + k)

        block = ctx.enter_context(nc.Block())

        @block.sync
        def _(sp):
            def load(dst, src):
                sp.dma_start(dst, src).then_inc(setup, 16)

            sp.dma_start(y_in[:, :, :], d["mid"][0:2].rearrange("a h w c -> (a h w) c")
                         .rearrange("(t p) c -> p t c", p=128)).then_inc(S["f_loaded"], 16)
            load(fwd[:, :, :], d["fwd"].rearrange("(k p) f -> p k f", p=128))
            load(inv[:, :, :], d["inv"].rearrange("(k p) t -> p k t", p=FC))
            for l in range(2):
                for r in range(2):
                    load(w1[l][:, :, r, :], d["fw1"][l, r].rearrange("g p e -> p g e"))
                    load(w2[l][0:96, :, 1 + r, :], d["fw2"][l, r].rearrange("g p e -> p g e"))
                    load(b1[l][:, r, :], d["fb1"][l, r])
                load(w2[l][96:97, :, 1, :], d["fb2"][l, 0:1].rearrange("o (g e) -> o g e", g=G))
                load(w2[l][96:97, :, 2, :], d["fb2"][l, 1:2].rearrange("o (g e) -> o g e", g=G))
                load(w1[l][:, :, 2, :], d["fw1"][l, 1].rearrange("g p e -> p g e"))
                load(w2[l][0:96, :, 0, :], d["fw2"][l, 1].rearrange("g p e -> p g e"))
            sp.dma_start(seed[:, :], d["ident"][0:1, 0:1]).then_inc(S["f_stored"], 16)

            def store(i):
                need(sp, "y_ready", 2 * i + 1, 4)
                sp.dma_start(d["out"][bass.ds(2 * i, 2)].rearrange("a h w c -> (a h w) c")
                             .rearrange("(t p) c -> p t c", p=128), y_out[:, :, :]).then_inc(S["f_stored"], 16)

            with sp.Fori(0, PAIRS - 1) as i:
                need(sp, "y_ready", 2 * i, 4)
                sp.dma_start(y_in[:, :, :], d["mid"][bass.ds(2 * i + 2, 2)].rearrange("a h w c -> (a h w) c")
                             .rearrange("(t p) c -> p t c", p=128)).then_inc(S["f_loaded"], 16)
                store(i)
            store(PAIRS - 1)
            sp.wait_ge(S["f_stored"], 16 + 16 * PAIRS)
            sp.wait_ge(S["f_loaded"], 16 * PAIRS)

        @block.gpsimd
        def _(pool):
            pool.wait_ge(setup, SETUP)
            for l in range(2):
                nc.gpsimd.tensor_scalar(w1[l][:, :, 2, :], w1[l][:, :, 2, :], -1.0, None, ALU.mult)\
                    .then_inc(preset, 1)
                nc.gpsimd.tensor_scalar(w2[l][0:96, :, 0, :], w2[l][0:96, :, 0, :], -1.0, None, ALU.mult)\
                    .then_inc(preset, 1)

        def xf_view(gg, a):
            return xf[:, gg, :, a, :]

        @block.vector
        def _(dve):
            v = nc.vector
            v.memset(o1[96:97, :, :, :, :], 1.0).then_inc(preset, 1)
            dve.wait_ge(preset, 5)
            with dve.Fori(0, PAIRS) as i:
                for l in range(2):
                    n = 2 * i + l
                    for gg in range(G):
                        need(dve, "fwd_done", n, 2 * gg + 1)
                        v.tensor_scalar(xf_view(gg, 0), bank[2 * gg][0:96, 0:2 * FREQ]
                                        .rearrange("p (r f) -> p r f", r=2), FWD[l], None, ALU.mult)\
                            .then_inc(S["xf_a"], 1)
                    for k in range(4):
                        need(dve, "mix2_done", n, k + 1)
                        v.tensor_scalar(clamp[:, k, :], bank[k][0:FC, 0:4 * 96], -LAMBDA, LAMBDA, ALU.max, ALU.min)\
                            .then_inc(S["clamped"], 1)
                        need(dve, "clamped", n, k + 1)
                        v.tensor_tensor(o2[:, k, :, :].rearrange("p r (g e) -> p g r e", g=G),
                                        bank[k][0:FC, 0:4 * 96].rearrange("p (g r e) -> p g r e", g=G, r=2),
                                        clamp[:, k, :].rearrange("p (g r e) -> p g r e", g=G, r=2), ALU.subtract)\
                            .then_inc(S["o2_ready"], 1)
                    if l == 1:
                        dve.wait_ge(S["f_stored"], 16 * i + 16)
                    src, dst = (y_in, y_mid) if l == 0 else (y_mid, y_out)
                    for t in range(4):
                        need(dve, "inv_done", n, t + 1)
                        v.scalar_tensor_tensor(out=dst[:, t, :], in0=bank[4 + t][:, 0:C], scalar=INV[l],
                                               in1=src[:, t, :], op0=ALU.mult, op1=ALU.add)\
                            .then_inc(S["y_ready"], 1)

        @block.scalar
        def _(act):
            s = nc.scalar
            act.wait_ge(preset, 5)
            with act.Fori(0, PAIRS) as i:
                for l in range(2):
                    n = 2 * i + l
                    for gg in range(G):
                        need(act, "fwd_done", n, 2 * gg + 2)
                        s.activation(xf_view(gg, 1), bank[2 * gg + 1][0:96, 0:2 * FREQ]
                                     .rearrange("p (r f) -> p r f", r=2), ACT.Copy, scale=FWD[l])\
                            .then_inc(S["xf_b"], 1)
                    for k in range(4):
                        gg, r = k // 2, k % 2
                        need(act, "mix1_done", n, k + 1)
                        s.activation(o1[0:96, gg, r, :, :].rearrange("p a f -> p (a f)"),
                                     bank[4 + k][0:96, 0:2 * FREQ], ACT.Relu, bias=b1[l][:, r, gg:gg + 1])\
                            .then_inc(S["relu_done"], 1)

        @block.tensor
        def _(pe):
            t_ = nc.tensor
            pe.wait_ge(preset, 5)
            with pe.Fori(0, PAIRS) as i:
                for l in range(2):
                    n = 2 * i + l
                    if l == 0:
                        pe.wait_ge(S["f_loaded"], 16 * i + 16)
                    else:
                        need(pe, "y_ready", 2 * i, 4)
                    src = y_in if l == 0 else y_mid
                    for gg in range(G):
                        for a in range(2):
                            for k in range(2):
                                last = t_.matmul(bank[2 * gg + a][0:96, 0:2 * FREQ],
                                                 src[:, 2 * a + k, 96 * gg:96 * gg + 96], fwd[:, k, :],
                                                 start=(k == 0), stop=(k == 1))
                            last.then_inc(S["fwd_done"], 1)
                    for gg in range(G):
                        need(pe, "xf_a", n, gg + 1)
                        need(pe, "xf_b", n, gg + 1)
                        for r in range(2):
                            for z in range(2):
                                w = (0 if z == 0 else 2) if r == 0 else (1 if z == 0 else 0)
                                last = t_.matmul(bank[4 + 2 * gg + r][0:96, 0:2 * FREQ], w1[l][:, gg, w, :],
                                                 xf[:, gg, z, :, :].rearrange("p a f -> p (a f)"),
                                                 start=(z == 0), stop=(z == 1))
                            last.then_inc(S["mix1_done"], 1)
                    for a in range(2):
                        for c in range(2):
                            for gg in range(G):
                                if a == 0 and c == 0:
                                    need(pe, "relu_done", n, 2 * gg + 2)
                                lo = a * FREQ + c * FC
                                for z in range(2):
                                    rows = 97 - z
                                    rhs = w2[l][0:rows, gg, 1:3, :] if z == 0 else w2[l][0:96, gg, 0:2, :]
                                    last = t_.matmul(bank[2 * a + c][0:FC, 192 * gg:192 * gg + 192],
                                                     o1[0:rows, gg, z, :, :].rearrange("p a f -> p (a f)")[:, lo:lo + FC],
                                                     rhs.rearrange("p r e -> p (r e)"), start=(z == 0), stop=(z == 1))
                            last.then_inc(S["mix2_done"], 1)
                    for a in range(2):
                        for hf in range(2):
                            need(pe, "o2_ready", n, 2 * a + 2)
                            for c in range(2):
                                for z in range(2):
                                    last = t_.matmul(bank[4 + 2 * a + hf][:, 0:C],
                                                     inv[:, 2 * c + z, 128 * hf:128 * hf + 128], o2[:, 2 * a + c, z, :],
                                                     start=(c == 0 and z == 0), stop=(c == 1 and z == 1))
                            last.then_inc(S["inv_done"], 1)


def kernel(**inputs):
    import numpy as np
    import concourse.bacc as bacc
    from concourse.bass_utils import run_bass_kernel_spmd

    def get(name):
        return np.asarray(inputs[name])

    order = []
    at = np.arange(HH * WW).reshape(HH, WW)
    for a in range(2):
        order.append(a * 256 + at[0:WS, 0:WS].ravel())
    for rows, cols in ((slice(0, WS), slice(WS, WW)), (slice(WS, HH), slice(0, WS)), (slice(WS, HH), slice(WS, WW))):
        for a in range(2):
            order.append(a * 256 + at[rows, cols].ravel())
    order = np.concatenate(order)
    x = get("x").reshape(PAIRS, TOK, C)[:, order]
    x = np.concatenate([x, x[:1]])

    def rel_blocks(name):
        out = np.zeros((96, 2, RT, HG), np.float32)
        for axis, part in enumerate("hw"):
            r = get(f"{name}_rel_pos_{part}")[::-1]
            for h in range(HG):
                out[HD * h:HD * h + HD, axis, :, h] = r.T
        return out.reshape(96, 2 * RT * HG)

    def blocks(w):
        out = np.zeros((G, 96, 96), np.float32)
        for b in range(8):
            s = slice(24 * (b % 4), 24 * (b % 4) + 24)
            out[b // 4, s, s] = w[b]
        return out

    pos = order % 256
    ph, pw = (pos // WW) % WS, (pos % WW) % WS
    onehot = np.zeros((5, 128, NH, SLOT), np.float32)
    for t in (0, 1, 4):
        for n in range(SIZE[t]):
            tok = START[t] + n
            onehot[t, n, :, REL0 + ph[tok]] = 1
            onehot[t, n, :, REL0 + WS + pw[tok]] = 1
    onehot = onehot.reshape(5, 128, NH * SLOT)
    c = np.arange(4 * HALF, TOK)
    row, col = (order[c] % 256) // WW, order[c] % WW
    window = (order[c] // 256) * 4 + (row >= WS) * 2 + (col >= WS)
    cut_mask = np.zeros((CUT, CUT + 1), np.float32)
    cut_mask[:, :CUT] = np.where(window[:, None] == window[None, :], 0, BIG)
    ky, kx = np.arange(WIN) // WS, np.arange(WIN) % WS
    real_y = ky[None] + WS * (row >= WS)[:, None] < HH
    real_x = kx[None] + WS * (col >= WS)[:, None] < WW
    pad_mask = np.where(real_y & real_x, BIG, 0).astype(np.float32)
    th, tw = np.arange(256) // WW, np.arange(256) % WW
    kh, kw = np.arange(FREQ) // 9, np.arange(FREQ) % 9
    turn = ((th[:, None] * kh[None] + tw[:, None] * kw[None]) % 16) * (2 * np.pi / 16)
    fwd = np.concatenate([np.cos(turn), -np.sin(turn)], 1).astype(np.float32)
    weight = np.where((kw == 0) | (kw == 8), 1.0, 2.0)[:, None]
    icos, isin = weight * np.cos(turn.T), -weight * np.sin(turn.T)
    inv = np.concatenate([icos[:FC], isin[:FC], icos[FC:], isin[FC:]]).astype(np.float32)

    L = ("L0_conv", "L1_conv")
    both = {
        "ln1_w": ("n1_w", "ln1_g"), "ln1_b": ("n1_b", "ln1_b"), "ln2_w": ("n2_w", "ln2_g"), "ln2_b": ("n2_b", "ln2_b"),
        "qkv_w": ("qkv_w",) * 2, "qkv_b": ("qkv_b",) * 2, "proj_w": ("proj_w",) * 2, "proj_b": ("proj_b",) * 2,
        "up_w": ("lin1_w", "mlp_w1"), "up_b": ("lin1_b", "mlp_b1"),
        "down_w": ("lin2_w", "mlp_w2"), "down_b": ("lin2_b", "mlp_b2"),
    }
    arrays = {"x": x}
    for key, (a, b) in both.items():
        arrays[key] = np.stack([get(f"{L[0]}_{a}"), get(f"{L[1]}_{b}")])
    arrays["rel"] = np.stack([rel_blocks(n) for n in L])
    arrays["fw1"] = np.stack([np.stack([blocks(get("L2_conv_w1r")), blocks(get("L2_conv_w1i"))]),
                              np.stack([blocks(w) for w in get("L3_conv_w1")])])
    arrays["fw2"] = np.stack([np.stack([blocks(get("L2_conv_w2r")), blocks(get("L2_conv_w2i"))]),
                              np.stack([blocks(w) for w in get("L3_conv_w2")])])
    for k in "12":
        arrays[f"fb{k}"] = np.stack([np.stack([get(f"L2_conv_b{k}r").reshape(C), get(f"L2_conv_b{k}i").reshape(C)]),
                                     get(f"L3_conv_b{k}").reshape(2, C)])
    for k in ("ln1_w", "ln1_b", "ln2_w", "ln2_b"):
        arrays[k] = arrays[k].reshape(2, G, 96).transpose(0, 2, 1)
    arrays["up_b"] = arrays["up_b"].reshape(2, MC, 128).transpose(0, 2, 1)
    arrays["fb1"] = arrays["fb1"].reshape(2, 2, G, 96).transpose(0, 1, 3, 2)
    arrays.update(ident=np.eye(128, dtype=np.float32), onehot=onehot, cut_mask=cut_mask, pad_mask=pad_mask,
                  fwd=fwd, inv=inv)
    arrays = {k: np.ascontiguousarray(a) for k, a in arrays.items()}

    nc = bacc.Bacc("TRN2", target_bir_lowering=False, num_devices=1)
    d = {k: nc.dram_tensor(f"in_{k}", a.shape, F32, kind="ExternalInput").ap() for k, a in arrays.items()}
    d["dist"] = nc.dram_tensor("distances", (2, TOK, UROW), F32, kind="Internal").ap()
    d["mid"] = nc.dram_tensor("between_loops", (B, HH, WW, C), F32, kind="Internal").ap()
    d["out"] = nc.dram_tensor("out", (B, HH, WW, C), F32, kind="ExternalOutput").ap()
    build(nc, d)
    r = run_bass_kernel_spmd(nc, [{f"in_{k}": a for k, a in arrays.items()}], core_ids=[0])
    return r.results[0]["out"]
```

```python
import concourse.bass as bass
from concourse import mybir
from contextlib import ExitStack

F32 = mybir.dt.float32
F32R = mybir.dt.float32r
BF16 = mybir.dt.bfloat16
ALU = mybir.AluOpType
ACT = mybir.ActivationFunctionType
AX = mybir.AxisListType

B, HH, WW, C = 8, 16, 16, 192
PAIRS = B // 2
WS = 14
NH, HD = 12, 16
HALF = WS // 2 * WS
WIN = WS * WS
CUT = 2 * (HH * WW - WIN)
TOK = 2 * HH * WW
TILES = 5
SIZE = [HALF] * 4 + [CUT]
START = [HALF * t for t in range(5)]
KEYS = [HALF] * 4 + [CUT + 1]
G = C // 96
HG = NH // G
KSLOT = 4 * HD
RW = 2 * WS
QSLOT = KSLOT + 2 * RW
RT = 2 * WS - 1
UROW = 2 * RT * NH
MLP = 4 * C
MC = MLP // 128
QSCALE = HD ** -0.5
EPS = [1e-5, 1e-6]
BIG = -1.0e30
QUAD = 4
QUADS = NH // QUAD
CK = CUT + 2
CLASSES = 128
FREQ = HH * (WW // 2 + 1)
FC = FREQ // 2
LAMBDA = 0.01
FWD = [1.0 / 16, 1.0]
INV = [1.0 / 16, 1.0 / 256]


def unit_order():
    order = []
    for k in range(2 * QUADS):
        heads = [(k // QUADS, QUAD * (k % QUADS) + e) for e in range(QUAD)]
        cut = [(None, 2 * k - 2), (None, 2 * k - 1)] if 1 <= k <= QUADS else []
        order += heads[:1] + cut[:1] + heads[1:2] + cut[1:] + heads[2:]
    return order


SEQ = unit_order()
STEPS = len(SEQ)
SLOTS = [(j, part) for j, (a, _) in enumerate(SEQ) for part in (("full",) if a is not None else ("pad", "cut"))]
S_BANKS = (0, 1, 6, 7)
OUT_BANKS = (4, 5)


def slot(j, part):
    return SLOTS.index((j, part))


def quad(j):
    a, h = SEQ[j]
    if a is not None:
        k = QUADS * a + h // QUAD
        return k % 2, h % QUAD == 0, h % QUAD == QUAD - 1
    return h // 2 % 2, h % 2 == 0, h % 2 == 1


OUT_UNITS = [j for j in range(STEPS) if quad(j)[2]]


def free_output(j):
    mine = [n for n, u in enumerate(OUT_UNITS) if u < j and quad(u)[0] == quad(j)[0]]
    return mine[-1] + 1 if mine else 0


def build(nc, d):
    with ExitStack() as ctx:
        def sb(name, shape):
            return ctx.enter_context(nc.sbuf_tensor(name, shape, F32))

        def sem(name):
            return ctx.enter_context(nc.semaphore(name))

        bank = [ctx.enter_context(nc.psum_tensor(f"bank{i}", [128, 512], F32)) for i in range(8)]
        setup = sem("setup")
        preset = sem("preset")
        weights = sem("weights")
        ident = sb("ident", [128, 128])
        half_pow = sb("half_pow", [128, TILES])
        attention_loop(nc, d, bank, setup, preset, weights, ident, half_pow)
        fourier_loop(nc, d, bank)


def attention_loop(nc, d, bank, setup, preset, weights, ident, half_pow):
    with ExitStack() as ctx:
        def sb(name, shape, dtype=F32):
            return ctx.enter_context(nc.sbuf_tensor(name, shape, dtype))

        def sem(name):
            return ctx.enter_context(nc.semaphore(name))

        w_qkv = [sb(f"w_qkv{l}", [97, G, 3 * C]) for l in range(2)]
        w_rel = [sb(f"w_rel{l}", [96, 2 * RT * HG]) for l in range(2)]
        w_proj = [sb(f"w_proj{l}", [128, QUADS, C]) for l in range(2)]
        b_proj = [sb(f"b_proj{l}", [128, C]) for l in range(2)]
        w_up = [sb(f"w_up{l}", [96, G, MLP]) for l in range(2)]
        w_down = [sb(f"w_down{l}", [128, MC, C]) for l in range(2)]
        b_up = [sb(f"b_up{l}", [128, MC]) for l in range(2)]
        b_down = [sb(f"b_down{l}", [128, C]) for l in range(2)]
        affine = [sb(f"affine{l}", [96, 4, G]) for l in range(2)]
        q_class = sb("q_class", [CLASSES, CUT], BF16)
        cut_mask = sb("cut_mask", [CLASSES, 2 * CK], BF16)
        pad_mask = sb("pad_mask", [CLASSES, 2 * WIN], BF16)
        pad_keys = sb("pad_keys", [QSLOT, WIN], F32R)
        x_in = sb("x_in", [128, TILES, C])
        x_mid = [sb(f"x_mid{l}", [128, TILES, C]) for l in range(2)]
        seed = sb("seed", [1, 1])
        wait_pad = sb("wait_pad", [1, 1])
        xn = sb("xn", [128, TILES, C])
        stats = sb("stats", [128, TILES, 6])
        moments = sb("moments", [128, TILES, 2])
        veps = sb("veps", [128, TILES])
        ones = sb("ones", [128, 1])
        eps = sb("eps", [128, 2, TILES])
        rstd = sb("rstd", [128, TILES])
        xT = sb("xT", [97, G, TOK + 1])
        k_tok = sb("k_tok", [128, 2, NH * KSLOT], F32R)
        v_pad = sb("v_pad", [128, TILES, NH, 128], F32R)
        QT = 3
        q_tok = sb("q_tok", [128, QT * NH * QSLOT], F32R)
        probsT = q_tok[:, 0:2 * 2 * QUAD * CUT].rearrange("p (s z m) -> p s z m", s=2, z=2)
        q_tok = q_tok[:, :].rearrange("p (t m) -> p t m", t=QT)
        q_out = sb("q_out", [128, TILES * C + G * TOK])
        q_flat = q_out[:, 0:TILES * C].rearrange("p (t c) -> p t c", t=TILES)
        qT = q_out[0:96, TILES * C:TILES * C + G * TOK].rearrange("p (g m) -> p g m", g=G)
        oT = q_out[:, 0:QUADS * TOK].rearrange("p (g m) -> p g m", g=QUADS)
        dist = sb("dist", [128, TILES, UROW])
        hidden = dist[:, :, :].rearrange("p t u -> p (t u)")[:, 0:MC * TOK].rearrange("p (m k) -> p m k", m=MC)
        rel = sb("rel", [128, TILES, RW * NH])
        q_aug = sb("q_aug", [QSLOT, NH, TOK], F32R)
        k_aug = sb("k_aug", [QSLOT, NH, TOK + 2], F32R)
        PS = 4
        probs = sb("probs", [128, PS, 2 * WIN])
        neg_max = sb("neg_max", [128, PS, 2])
        row_sum = sb("row_sum", [128, PS, 2])
        inv_sum = sb("inv_sum", [128, PS, 2])
        pad_bias = sb("pad_bias", [CUT, PS, 2])
        neg_pad = sb("neg_pad", [CUT, 2])
        neg_real = sb("neg_real", [CUT, 2])
        stage = dist[:, :, :].rearrange("p t u -> p (t u)")

        names = ("x_loaded moments_ready rstd_ready veps_ready xn_ready xT_done xT_lo xT_hi q_done q_copied "
                 "qT_done qT_lo qT_hi dist_done dist_lo dist_hi dist_stored kv_done kv_hi kv_lo kT_done k_even "
                 "k_odd q_hi q_placed rel_placed qaug_done qaug_act qaug_dve scores_done max_ready exp_done "
                 "inv_ready probs_ready probsT_done probsT_hi probsT_lo pv_done oT_ready proj_done base_ready "
                 "mid_ready midb_ready up_done gelu_done down_done out_ready stored order_dve").split()
        S = {n: sem(n) for n in names}
        rel_loaded = [sem(f"rel_loaded{t}") for t in range(TILES)]
        PER = dict(moments_ready=10, veps_ready=10, rstd_ready=10, xn_ready=10, xT_done=2, xT_lo=2, xT_hi=2,
                   q_done=5, q_copied=5, qT_done=1, qT_lo=1, qT_hi=1, dist_done=10, dist_lo=5, dist_hi=5,
                   dist_stored=80, kv_done=5, kv_hi=5, kv_lo=5, kT_done=10, k_even=10, k_odd=10, q_hi=5, q_placed=5,
                   rel_placed=5, qaug_done=15, qaug_act=8, qaug_dve=7, scores_done=len(SLOTS), max_ready=STEPS,
                   exp_done=STEPS, inv_ready=STEPS, probs_ready=STEPS, probsT_done=STEPS, probsT_hi=STEPS,
                   probsT_lo=STEPS, pv_done=STEPS, oT_ready=len(OUT_UNITS), proj_done=5, base_ready=1, mid_ready=5,
                   midb_ready=1, up_done=6, gelu_done=6, down_done=5, out_ready=5, order_dve=39)
        block = ctx.enter_context(nc.Block())

        def need(eng, name, n, k):
            eng.wait_ge(S[name], n * PER[name] + k)

        def v_parts(t):
            v = v_pad[0:KEYS[t], t, :, :].rearrange("p h s -> p (h s)")
            return [bass.AP(v.tensor, v.offset + HD * z, [v.ap[0], [QUAD * 128, QUADS], [128 + 32, QUAD], [1, HD]])
                    for z in range(2)]

        SETUP = 16 * (13 * 2 + 5)

        @block.sync
        def _(sp):
            def load(dst, src):
                sp.dma_start(dst, src).then_inc(setup, 16)

            def load_x(i):
                sp.dma_start(x_in[0:HALF, 0:4, :],
                             d["x"][i, 0:4 * HALF, :].rearrange("(t n) c -> n t c", t=4)).then_inc(S["x_loaded"], 16)
                sp.dma_start(x_in[0:CUT, 4, :], d["x"][i, 4 * HALF:TOK, :]).then_inc(S["x_loaded"], 16)

            load_x(0)
            load(ident[:, :], d["ident"])
            load(stage[:, 0:CUT], d["q_class"])
            load(stage[:, CUT:CUT + 2 * CK], d["cut_mask"])
            load(stage[:, CUT + 2 * CK:CUT + 2 * CK + 2 * WIN], d["pad_mask"])
            load(stage[KSLOT:QSLOT, 1024:1024 + TOK + 2], d["onehot"])
            for l in range(2):
                load(affine[l][:, 0, :], d["ln1_w"][l])
                load(affine[l][:, 1, :], d["ln1_b"][l])
                load(affine[l][:, 2, :], d["ln2_w"][l])
                load(affine[l][:, 3, :], d["ln2_b"][l])
                load(w_qkv[l][0:96, :, :], d["qkv_w"][l].rearrange("(g p) n -> p g n", g=G))
                load(w_qkv[l][96:97, 0, :], d["qkv_b"][l].rearrange("(a n) -> a n", a=1))
                load(w_rel[l][:, :], d["rel"][l])
                load(w_proj[l][:, :, :], d["proj_w"][l])
                load(b_proj[l][:, :], d["proj_b"][l].rearrange("(a n) -> a n", a=1).broadcast_to([128, C]))
                load(w_up[l][:, :, :], d["up_w"][l].rearrange("(g p) n -> p g n", g=G))
                load(w_down[l][:, :, :], d["down_w"][l].rearrange("(g p) n -> p g n", g=MC))
                load(b_up[l][:, :], d["up_b"][l])
                load(b_down[l][:, :], d["down_b"][l].rearrange("(a n) -> a n", a=1).broadcast_to([128, C]))
            sp.dma_start(seed[:, :], d["ident"][0:1, 0:1]).then_inc(S["stored"], 16)

            U, UO = d["dist"].tensor, UROW * TOK

            def gather(t, l, part, dims, first, at, count):
                src = bass.AP(U, l * UO + first, dims + [[1, WS * NH]])
                sp.dma_start(rel[at:at + count, t, part * WS * NH:(part + 1) * WS * NH], src)\
                    .then_inc(rel_loaded[t], 16)

            with sp.Fori(0, PAIRS) as i:
                for l in range(2):
                    n = 2 * i + l
                    for t in range(TILES):
                        need(sp, "dist_lo", n, t + 1)
                        need(sp, "dist_hi", n, t + 1)
                        sp.dma_start(d["dist"][l, START[t]:START[t] + SIZE[t], :], dist[0:SIZE[t], t, :])\
                            .then_inc(S["dist_stored"], 16)
                    need(sp, "dist_stored", n, 80)
                    R, D = UROW, NH
                    for t in range(4):
                        base = START[t] * R
                        gather(t, l, 0, [[WS * R - D, 7], [R, WS]], base + (WS - 1 - 7 * (t % 2)) * D, 0, HALF)
                        gather(t, l, 1, [[WS * R, 7], [R - D, WS]], base + RT * NH + (WS - 1) * D, 0, HALF)
                    base, top = START[4] * R, (WS - 1) * D
                    for a in range(2):
                        at = 28 * a
                        gather(4, l, 0, [[2 * R - D, WS], [R, 2]], base + at * R + top, at, 28)
                        gather(4, l, 1, [[2 * R, WS], [R - D, 2]], base + at * R + RT * NH + top, at, 28)
                        at = 56 + 28 * a
                        gather(4, l, 0, [[WS * R - D, 2], [R, WS]], base + at * R + top, at, 28)
                        gather(4, l, 1, [[WS * R, 2], [R - D, WS]], base + at * R + RT * NH + top, at, 28)
                        at = 112 + 4 * a
                        gather(4, l, 0, [[2 * R - D, 2], [R, 2]], base + at * R + top, at, 4)
                        gather(4, l, 1, [[2 * R, 2], [R - D, 2]], base + at * R + RT * NH + top, at, 4)
                    if l == 0:
                        need(sp, "base_ready", n, 1)
                        need(sp, "xn_ready", n, 5)
                        sp.dma_start(x_in[0:HALF, 0:4, :], d["x"][bass.ds(i + 1, 1), 0:4 * HALF, :]
                                     .rearrange("o (t n) c -> (o n) t c", t=4)).then_inc(S["x_loaded"], 16)
                        sp.dma_start(x_in[0:CUT, 4, :], d["x"][bass.ds(i + 1, 1), 4 * HALF:TOK, :]
                                     .rearrange("o n c -> (o n) c")).then_inc(S["x_loaded"], 16)
                need(sp, "out_ready", 2 * i + 1, 5)
                for a in range(2):
                    img = d["mid"][bass.ds(2 * i + a, 1)].rearrange("o h w c -> (o h) w c")
                    for r in range(2):
                        sp.dma_start(img[7 * r:7 * r + 7, 0:WS, :], x_mid[1][0:HALF, 2 * a + r, :])\
                            .then_inc(S["stored"], 16)
                    sp.dma_start(img[0:WS, WS:WW, :], x_mid[1][28 * a:28 * a + 28, 4, :]).then_inc(S["stored"], 16)
                    sp.dma_start(img[WS:HH, 0:WS, :], x_mid[1][56 + 28 * a:84 + 28 * a, 4, :])\
                        .then_inc(S["stored"], 16)
                    sp.dma_start(img[WS:HH, WS:WW, :], x_mid[1][112 + 4 * a:116 + 4 * a, 4, :])\
                        .then_inc(S["stored"], 16)
            sp.wait_ge(S["stored"], 16 + 160 * PAIRS)
            sp.wait_ge(S["x_loaded"], 32 * (PAIRS + 1))

        @block.gpsimd
        def _(pool):
            g = nc.gpsimd
            g.memset(half_pow[:, :], -0.5).then_inc(preset, 1)
            g.memset(ones[:, :], 1.0).then_inc(preset, 1)
            for l in range(2):
                g.memset(eps[:, l, :], EPS[l]).then_inc(preset, 1)
            g.memset(v_pad[:, :, :, :].bitcast(F32), 0.0).then_inc(preset, 1)
            g.memset(moments[:, :, :], 1.0).then_inc(preset, 1)
            pool.wait_ge(preset, PRESETS)
            pool.wait_ge(setup, SETUP)
            for l in range(2):
                for gg in range(G):
                    w = w_qkv[l][0:97 - gg, gg, C:2 * C]
                    g.tensor_scalar(w, w, QSCALE, None, ALU.mult).then_inc(weights, 1)

            def rsqrt(n, l, k):
                for t in range(TILES):
                    c = 5 * (k - 1) + t + 1
                    need(pool, "moments_ready", n, c)
                    g.tensor_tensor(veps[:, t:t + 1], moments[:, t, 1:2], eps[:, l, 0:1], ALU.add)\
                        .then_inc(S["veps_ready"], 1)
                    need(pool, "veps_ready", n, c)
                    g.tensor_tensor(rstd[:, t:t + 1], veps[:, t:t + 1], half_pow[:, 0:1], ALU.pow)\
                        .then_inc(S["rstd_ready"], 1)

            def normalise(n, j):
                need(pool, "inv_ready", n, j + 1)
                rows, k, m, step = (HALF, 2, WIN, WIN) if SEQ[j][0] is not None else (CUT, 2, CUT + 1, CK)
                p = probs[0:rows, j % PS, 0:k * step].rearrange("p (k m) -> p k m", k=k)[:, :, 0:m]
                g.tensor_tensor(p, p, inv_sum[0:rows, j % PS, 0:k].unsqueeze(2).to_broadcast([rows, k, m]),
                                ALU.mult).then_inc(S["probs_ready"], 1)

            def add_bias(dst, src, b):
                g.tensor_tensor(dst[0:HALF, 0:4, :], src[0:HALF, 0:4, :],
                                b[0:HALF, :].unsqueeze(1).to_broadcast([HALF, 4, C]), ALU.add)
                return g.tensor_tensor(dst[0:CUT, 4, :], src[0:CUT, 4, :], b[0:CUT, :], ALU.add)

            def place_q(n, t):
                need(pool, "q_copied", n, t + 1)
                if t >= QT:
                    need(pool, "qaug_done", n, 3 * (t - QT) + 3)
                q = q_tok[0:SIZE[t], t % QT, :].rearrange("p (h s) -> p h s", s=QSLOT)[:, :, 0:KSLOT]
                q = q.rearrange("p h (z d c) -> p h z d c", z=2, d=2)
                src = q_flat[0:SIZE[t], t, :].rearrange("p (h c) -> p h c", c=HD)
                one = ones[0:SIZE[t], :].unsqueeze(2).to_broadcast([SIZE[t], NH, HD])
                for e in range(2):
                    last = g.tensor_tensor(q[:, :, 0, e, :], src, one, ALU.mult)
                last.then_inc(S["q_hi"], 1)
                need(pool, "q_hi", n, t + 1)
                for e in range(2):
                    last = g.tensor_tensor(q[:, :, 1, e, :], src, q[:, :, 0, 0, :].bitcast(F32), ALU.subtract)
                last.then_inc(S["q_placed"], 1)

            with pool.Fori(0, PAIRS) as i:
                for l in range(2):
                    n = 2 * i + l
                    src = x_in if l == 0 else x_mid[0]
                    rsqrt(n, l, 1)
                    if l == 1:
                        pool.wait_ge(S["stored"], 16 + 160 * i)
                    add_bias(x_mid[l], src, b_proj[l]).then_inc(S["base_ready"], 1)
                    for t in range(TILES):
                        place_q(n, t)
                    for j in range(STEPS):
                        normalise(n, j)
                    rsqrt(n, l, 2)
                    need(pool, "xn_ready", n, 10)
                    add_bias(x_mid[l], x_mid[l], b_down[l]).then_inc(S["midb_ready"], 1)

        @block.vector
        def _(dve):
            v = nc.vector
            v.memset(xT[0:96, :, TOK:TOK + 1], 0.0).then_inc(preset, 1)
            v.memset(xT[96:97, 0, :], 1.0).then_inc(preset, 1)
            v.memset(k_aug[0:KSLOT, :, TOK + 1:TOK + 2].bitcast(F32), 0.0).then_inc(preset, 1)
            v.memset(pad_keys[0:KSLOT, :].bitcast(F32), 0.0).then_inc(preset, 1)
            dve.wait_ge(setup, SETUP)
            dve.wait_ge(preset, PRESETS)
            v.tensor_copy(q_class[:, :], stage[:, 0:CUT]).then_inc(weights, 1)
            v.tensor_copy(cut_mask[:, :], stage[:, CUT:CUT + 2 * CK]).then_inc(weights, 1)
            v.tensor_copy(pad_mask[:, :], stage[:, CUT + 2 * CK:CUT + 2 * CK + 2 * WIN]).then_inc(weights, 1)
            hot = stage[KSLOT:QSLOT, 1024:1024 + TOK + 2]
            v.tensor_copy(pad_keys[KSLOT:QSLOT, :], hot[:, 0:WIN]).then_inc(weights, 1)
            v.tensor_copy(k_aug[KSLOT:QSLOT, :, :], hot.unsqueeze(1).to_broadcast([2 * RW, NH, TOK + 2]))\
                .then_inc(weights, 1)
            dve.wait_ge(weights, WEIGHTS)
            chain = [0]

            def after(n, ins):
                chain[0] += 1
                ins.then_inc(S["order_dve"], 1)
                need(dve, "order_dve", n, chain[0])

            def residual_norm(n, src, k, total=None, add=None):
                for step in range(TILES + 2):
                    if add and step < TILES:
                        add(step)
                    t = step - 1
                    if 0 <= t < TILES:
                        if add:
                            need(dve, *total, t + 1)
                        after(n, v.bn_stats(stats[0:SIZE[t], t, :], src[0:SIZE[t], t, :]))
                        v.memset(wait_pad[:, :], 0.0)
                        v.bn_aggr(moments[0:SIZE[t], t, :], stats[0:SIZE[t], t, :]).then_inc(S["moments_ready"], 1)
                    if step >= 2:
                        normal(n, src, k, step - 2)

            def normal(n, src, k, t):
                need(dve, "moments_ready", n, 5 * (k - 1) + t + 1)
                need(dve, "rstd_ready", n, 5 * (k - 1) + t + 1)
                v.tensor_scalar(xn[0:SIZE[t], t, :], src[0:SIZE[t], t, :], moments[0:SIZE[t], t, 0:1],
                                rstd[0:SIZE[t], t:t + 1], ALU.subtract, ALU.mult).then_inc(S["xn_ready"], 1)

            def attend(n, j):
                a, h = SEQ[j]
                sl = j % PS
                if a is not None:
                    k = slot(j, "full")
                    need(dve, "scores_done", n, k + 1)
                    v.tensor_reduce(neg_max[0:HALF, sl, 0:2], bank[S_BANKS[k % 4]][0:HALF, 0:2 * WIN]
                                    .rearrange("p (r m) -> p r m", r=2), AX.X, ALU.max,
                                    negate=True).then_inc(S["max_ready"], 1)
                    return
                k = slot(j, "pad")
                need(dve, "scores_done", n, k + 1)
                v.tensor_reduce(neg_pad[:, :], bank[S_BANKS[k % 4]][0:CUT, 0:2 * WIN]
                                .rearrange("p (r m) -> p r m", r=2), AX.X, ALU.max, negate=True)
                k = slot(j, "cut")
                need(dve, "scores_done", n, k + 1)
                s = bank[S_BANKS[k % 4]][0:CUT, 0:2 * CK].rearrange("p (e m) -> p e m", e=2)
                after(n, v.tensor_reduce(neg_real[:, :], s[:, :, 0:CUT], AX.X, ALU.max, negate=True))
                after(n, v.tensor_tensor(neg_pad[:, :], neg_pad[:, :], s[:, :, CUT], ALU.subtract))
                after(n, v.tensor_tensor(neg_max[0:CUT, sl, :], neg_real[:, :], neg_pad[:, :], ALU.min))
                v.tensor_tensor(pad_bias[:, sl, :], s[:, :, CUT], neg_max[0:CUT, sl, :], ALU.add)\
                    .then_inc(S["max_ready"], 1)

            def invert(n, j):
                sl = j % PS
                need(dve, "exp_done", n, j + 1)
                rows = HALF if SEQ[j][0] is not None else CUT
                if SEQ[j][0] is None:
                    mass = probs[0:CUT, sl, 0:2 * CK].rearrange("p (e m) -> p e m", e=2)[:, :, CUT]
                    after(n, v.tensor_tensor(row_sum[0:CUT, sl, :], row_sum[0:CUT, sl, :], mass, ALU.add))
                v.reciprocal(inv_sum[0:rows, sl, :], row_sum[0:rows, sl, :]).then_inc(S["inv_ready"], 1)

            def probsT_low(n, j):
                need(dve, "probsT_hi", n, j + 1)
                rows, m = (HALF, 4 * HALF) if SEQ[j][0] is not None else (CUT + 1, 2 * CUT)
                v.tensor_tensor(probsT[0:rows, j % 2, 1, 0:m], bank[2 + j % 2][0:rows, 0:m],
                                probsT[0:rows, j % 2, 0, 0:m].bitcast(F32), ALU.subtract)\
                    .then_inc(S["probsT_lo"], 1)

            def copy_odd(n, t):
                for b in range(2):
                    need(dve, "kT_done", n, 2 * t + b + 1)
                    v.tensor_copy(k_aug[0:KSLOT, 6 * b + 1:6 * b + 6:2, START[t]:START[t] + KEYS[t]],
                                  bank[6 + b][KSLOT:128, 0:3 * KEYS[t]].rearrange("p (k m) -> p k m", k=3))\
                        .then_inc(S["k_odd"], 1)

            def place_rel(n, t):
                dve.wait_ge(rel_loaded[t], n * (32 if t < 4 else 192) + (32 if t < 4 else 192))
                if t >= QT:
                    need(dve, "qaug_done", n, 3 * (t - QT) + 3)
                q = q_tok[0:SIZE[t], t % QT, :].rearrange("p (h s) -> p h s", s=QSLOT)
                src = rel[0:SIZE[t], t, :].rearrange("p (r h) -> p h r", h=NH)
                after(n, v.tensor_copy(q[:, :, KSLOT:KSLOT + RW], src))
                v.tensor_tensor(q[:, :, KSLOT + RW:QSLOT], src, q[:, :, KSLOT:KSLOT + RW].bitcast(F32), ALU.subtract)\
                    .then_inc(S["rel_placed"], 1)

            def copy_qaug(n, t):
                for b in range(3):
                    c = 3 * t + b
                    if c % 2:
                        need(dve, "qaug_done", n, c + 1)
                        v.tensor_copy(q_aug[:, 4 * b:4 * b + 4, START[t]:START[t] + SIZE[t]],
                                      bank[4 + c % 4][0:QSLOT, 0:4 * SIZE[t]].rearrange("p (k m) -> p k m", k=4))\
                            .then_inc(S["qaug_dve"], 1)

            with dve.Fori(0, PAIRS) as i:
                for l in range(2):
                    n = 2 * i + l
                    src = x_in if l == 0 else x_mid[0]
                    if l == 0:
                        chain[0] = 0
                        dve.wait_ge(S["x_loaded"], 32 * i + 32)
                        residual_norm(n, src, 1)
                    need(dve, "xT_done", n, 1)
                    v.tensor_scalar(xT[0:96, 0, 0:TOK], bank[0][0:96, :], affine[l][:, 0, 0:1], affine[l][:, 1, 0:1],
                                    ALU.mult, ALU.add).then_inc(S["xT_lo"], 1)
                    need(dve, "qT_done", n, 1)
                    v.tensor_copy(qT[:, 0, :], bank[0][0:96, :]).then_inc(S["qT_lo"], 1)
                    for t in range(TILES):
                        need(dve, "dist_done", n, 2 * t + 1)
                        v.tensor_copy(dist[0:SIZE[t], t, :].rearrange("p (r h) -> p r h", h=NH)[:, :, 0:HG],
                                      bank[2 + 2 * t % 4][0:SIZE[t], 0:2 * RT * HG]
                                      .rearrange("p (r h) -> p r h", h=HG)).then_inc(S["dist_lo"], 1)
                    for t in range(TILES):
                        need(dve, "kv_hi", n, t + 1)
                        k = k_tok[0:KEYS[t], t % 2, :].rearrange("p (h d z c) -> p h d z c", d=2, z=2, c=HD)
                        src = bank[t % 2][0:KEYS[t], 0:C].rearrange("p (h c) -> p h c", c=HD)
                        wide = [KEYS[t], NH, 2, HD]
                        v.tensor_tensor(k[:, :, :, 1, :], src.unsqueeze(2).to_broadcast(wide),
                                        k[:, :, :, 0, :].bitcast(F32), ALU.subtract)
                        hi, lo = v_parts(t)
                        v.tensor_tensor(lo, bank[t % 2][0:KEYS[t], C:2 * C].rearrange("p (q e c) -> p q e c", e=QUAD, c=HD),
                                        hi.bitcast(F32), ALU.subtract).then_inc(S["kv_lo"], 1)
                        if t >= 1:
                            copy_odd(n, t - 1)
                    copy_odd(n, TILES - 1)
                    for t in range(TILES):
                        if t >= QT:
                            copy_qaug(n, t - QT)
                        place_rel(n, t)
                    for t in range(TILES - QT, TILES):
                        copy_qaug(n, t)
                    for j in range(STEPS + 3):
                        if j < STEPS:
                            attend(n, j)
                        if 1 <= j <= STEPS:
                            invert(n, j - 1)
                        if j >= 3:
                            probsT_low(n, j - 3)

                    def add_attention(t):
                        need(dve, "proj_done", n, t + 1)
                        v.tensor_tensor(x_mid[l][0:SIZE[t], t, :], bank[2 + t % 2][0:SIZE[t], 0:C],
                                        x_mid[l][0:SIZE[t], t, :], ALU.add).then_inc(S["mid_ready"], 1)

                    need(dve, "base_ready", n, 1)
                    residual_norm(n, x_mid[l], 2, ("mid_ready", n), add_attention)
                    need(dve, "xT_done", n, 2)
                    v.tensor_scalar(xT[0:96, 0, 0:TOK], bank[0][0:96, :], affine[l][:, 2, 0:1], affine[l][:, 3, 0:1],
                                    ALU.mult, ALU.add).then_inc(S["xT_lo"], 1)
                    need(dve, "midb_ready", n, 1)

                    def add_mlp(t):
                        need(dve, "down_done", n, t + 1)
                        v.tensor_tensor(x_mid[l][0:SIZE[t], t, :], bank[2 + t % 4][0:SIZE[t], 0:C],
                                        x_mid[l][0:SIZE[t], t, :], ALU.add).then_inc(S["out_ready"], 1)

                    assert chain[0] == PER["order_dve"], chain[0]
                    if l == 0:
                        chain[0] = 0
                        residual_norm(n + 1, x_mid[0], 1, ("out_ready", n), add_mlp)
                    else:
                        for t in range(TILES):
                            add_mlp(t)
                        need(dve, "out_ready", n, 5)

        @block.scalar
        def _(act):
            s = nc.scalar
            act.wait_ge(setup, SETUP)
            act.wait_ge(preset, PRESETS)
            act.wait_ge(weights, WEIGHTS)

            def exps(n, j):
                a, h = SEQ[j]
                sl = j % PS
                need(act, "max_ready", n, j + 1)
                if j >= PS:
                    need(act, "probsT_done", n, j - PS + 1)
                if a is not None:
                    b = bank[S_BANKS[slot(j, "full") % 4]]
                    for r in range(2):
                        last = s.activation(probs[0:HALF, sl, r * WIN:(r + 1) * WIN], b[0:HALF, r * WIN:(r + 1) * WIN],
                                            ACT.Exp, bias=neg_max[0:HALF, sl, r:r + 1],
                                            accum_out=row_sum[0:HALF, sl, r:r + 1])
                else:
                    b = bank[S_BANKS[slot(j, "cut") % 4]]
                    for e in range(2):
                        s.activation(probs[0:CUT, sl, e * CK:e * CK + CUT], b[0:CUT, e * CK:e * CK + CUT], ACT.Exp,
                                     bias=neg_max[0:CUT, sl, e:e + 1], accum_out=row_sum[0:CUT, sl, e:e + 1])
                    for e in range(2):
                        b = bank[S_BANKS[slot(j, "pad") % 4]][0:CUT, WIN * e:WIN * e + WIN]
                        last = s.activation(b, b, ACT.Exp, bias=pad_bias[:, sl, e:e + 1],
                                            accum_out=probs[0:CUT, sl, e * CK + CUT:e * CK + CUT + 1])
                last.then_inc(S["exp_done"], 1)

            def copy_even(n, t):
                for b in range(2):
                    need(act, "kT_done", n, 2 * t + b + 1)
                    s.activation(k_aug[0:KSLOT, 6 * b:6 * b + 5:2, START[t]:START[t] + KEYS[t]],
                                 bank[6 + b][0:KSLOT, 0:3 * KEYS[t]].rearrange("p (k m) -> p k m", k=3),
                                 ACT.Copy).then_inc(S["k_even"], 1)

            def probsT_high(n, j):
                need(act, "probsT_done", n, j + 1)
                if j >= 2:
                    need(act, "pv_done", n, j - 1)
                rows, m = (HALF, 4 * HALF) if SEQ[j][0] is not None else (CUT + 1, 2 * CUT)
                s.activation(probsT[0:rows, j % 2, 0, 0:m], bank[2 + j % 2][0:rows, 0:m], ACT.Copy)\
                    .then_inc(S["probsT_hi"], 1)

            def copy_oT(n, j):
                need(act, "pv_done", n, j + 1)
                a, h = SEQ[j]
                b = bank[OUT_BANKS[quad(j)[0]]]
                if a is not None:
                    s.activation(oT[:, h // QUAD, WIN * a:WIN * a + WIN], b[:, 0:WIN], ACT.Copy)\
                        .then_inc(S["oT_ready"], 1)
                else:
                    s.activation(oT[:, h // 2, 4 * HALF:TOK], b[:, 0:CUT], ACT.Copy).then_inc(S["oT_ready"], 1)

            with act.Fori(0, PAIRS) as i:
                for l in range(2):
                    n = 2 * i + l
                    need(act, "xT_done", n, 1)
                    s.activation(xT[0:96, 1, 0:TOK], bank[1][0:96, :], ACT.Identity, bias=affine[l][:, 1, 1:2],
                                 scale=affine[l][:, 0, 1:2]).then_inc(S["xT_hi"], 1)
                    for t in range(TILES):
                        need(act, "q_done", n, t + 1)
                        s.activation(q_flat[0:SIZE[t], t, :], bank[4 + t % 2][0:SIZE[t], 0:C], ACT.Copy)\
                            .then_inc(S["q_copied"], 1)
                    need(act, "qT_done", n, 1)
                    s.activation(qT[:, 1, :], bank[1][0:96, :], ACT.Copy).then_inc(S["qT_hi"], 1)
                    for t in range(TILES):
                        need(act, "dist_done", n, 2 * t + 2)
                        s.activation(dist[0:SIZE[t], t, :].rearrange("p (r h) -> p r h", h=NH)[:, :, HG:NH],
                                     bank[2 + (2 * t + 1) % 4][0:SIZE[t], 0:2 * RT * HG]
                                     .rearrange("p (r h) -> p r h", h=HG), ACT.Copy).then_inc(S["dist_hi"], 1)
                    for t in range(TILES):
                        need(act, "kv_done", n, t + 1)
                        if t >= 2:
                            need(act, "kT_done", n, 2 * t - 2)
                        k = k_tok[0:KEYS[t], t % 2, :].rearrange("p (h d z c) -> p h d z c", d=2, z=2, c=HD)
                        src = bank[t % 2][0:KEYS[t], 0:C].rearrange("p (h c) -> p h c", c=HD)
                        s.activation(k[:, :, :, 0, :], src.unsqueeze(2).to_broadcast([KEYS[t], NH, 2, HD]), ACT.Copy)
                        s.activation(v_parts(t)[0], bank[t % 2][0:KEYS[t], C:2 * C]
                                     .rearrange("p (q e c) -> p q e c", e=QUAD, c=HD), ACT.Copy)\
                            .then_inc(S["kv_hi"], 1)
                        if t >= 1:
                            copy_even(n, t - 1)
                    copy_even(n, TILES - 1)
                    for c in range(0, 3 * TILES, 2):
                        t, b = c // 3, c % 3
                        need(act, "qaug_done", n, c + 1)
                        s.activation(q_aug[:, 4 * b:4 * b + 4, START[t]:START[t] + SIZE[t]],
                                     bank[4 + c % 4][0:QSLOT, 0:4 * SIZE[t]].rearrange("p (k m) -> p k m", k=4),
                                     ACT.Copy).then_inc(S["qaug_act"], 1)
                    for j in range(STEPS + 5):
                        if 3 <= j < STEPS + 3:
                            probsT_high(n, j - 3)
                        if j - 5 in OUT_UNITS:
                            copy_oT(n, j - 5)
                        if j < STEPS:
                            exps(n, j)
                    need(act, "xT_done", n, 2)
                    s.activation(xT[0:96, 1, 0:TOK], bank[1][0:96, :], ACT.Identity, bias=affine[l][:, 3, 1:2],
                                 scale=affine[l][:, 2, 1:2]).then_inc(S["xT_hi"], 1)
                    for f in range(MC):
                        need(act, "up_done", n, f + 1)
                        s.activation(hidden[:, f, :], bank[4 + f % 4][:, :], ACT.Gelu, bias=b_up[l][:, f:f + 1])\
                            .then_inc(S["gelu_done"], 1)

        @block.tensor
        def _(pe):
            t_ = nc.tensor
            pe.wait_ge(setup, SETUP)
            pe.wait_ge(preset, PRESETS)
            pe.wait_ge(weights, WEIGHTS)

            def transpose_xn(n, k):
                for t in range(TILES):
                    need(pe, "xn_ready", n, 5 * (k - 1) + t + 1)
                    for gg in range(G):
                        last = t_.transpose(bank[gg][0:96, START[t]:START[t] + SIZE[t]],
                                            xn[0:SIZE[t], t, 96 * gg:96 * gg + 96], ident[0:SIZE[t], 0:SIZE[t]])
                last.then_inc(S["xT_done"], 1)
                need(pe, "xT_lo", n, k)
                need(pe, "xT_hi", n, k)

            def scores(n, k):
                j, part = SLOTS[k]
                a, h = SEQ[j]
                b = bank[S_BANKS[k % 4]]
                if k >= 4:
                    need(pe, "exp_done", n, SLOTS[k - 4][0] + 1)
                if part == "full":
                    for r in range(2):
                        last = t_.matmul(b[0:HALF, r * WIN:(r + 1) * WIN],
                                         q_aug[:, h, START[2 * a + r]:START[2 * a + r] + HALF],
                                         k_aug[:, h, WIN * a:WIN * a + WIN], start=True, stop=True)
                else:
                    m, keys, mask = (CK, None, cut_mask) if part == "cut" else (WIN, pad_keys, pad_mask)
                    t_.matmul(b[0:CUT, 0:2 * m], q_class[:, :], mask[:, :], start=True, stop=False)
                    for e in range(2):
                        hh = 2 * h + e
                        key = k_aug[:, hh, 4 * HALF:TOK + 2] if keys is None else keys[:, :]
                        last = t_.matmul(b[0:CUT, e * m:(e + 1) * m], q_aug[:, hh, 4 * HALF:TOK], key,
                                         start=False, stop=(e == 1))
                last.then_inc(S["scores_done"], 1)

            def transpose_probs(n, j):
                need(pe, "probs_ready", n, j + 1)
                if j >= 2:
                    need(pe, "probsT_lo", n, j - 1)
                o = bank[2 + j % 2]
                if SEQ[j][0] is not None:
                    for kk in range(2):
                        for r in range(2):
                            last = t_.transpose(o[0:HALF, (2 * kk + r) * HALF:(2 * kk + r + 1) * HALF],
                                                probs[0:HALF, j % PS, r * WIN + kk * HALF:r * WIN + (kk + 1) * HALF],
                                                ident[0:HALF, 0:HALF])
                else:
                    for e in range(2):
                        last = t_.transpose(o[0:CUT + 1, e * CUT:(e + 1) * CUT],
                                            probs[0:CUT, j % PS, e * CK:e * CK + CUT + 1], ident[0:CUT, 0:CUT])
                last.then_inc(S["probsT_done"], 1)

            def values(n, j):
                a, h = SEQ[j]
                b, opens, closes = quad(j)
                b = bank[OUT_BANKS[b]]
                need(pe, "probsT_lo", n, j + 1)
                if opens and free_output(j):
                    need(pe, "oT_ready", n, free_output(j))
                if a is not None:
                    for kk in range(2):
                        for z in range(2):
                            last = t_.matmul(b[:, 0:WIN], v_pad[0:HALF, 2 * a + kk, h, :],
                                             probsT[0:HALF, j % 2, z, kk * WIN:(kk + 1) * WIN],
                                             start=(opens and kk == 0 and z == 0), stop=(closes and kk == 1 and z == 1))
                else:
                    for e in range(2):
                        for z in range(2):
                            last = t_.matmul(b[:, 0:CUT], v_pad[0:CUT + 1, 4, 2 * h + e, :],
                                             probsT[0:CUT + 1, j % 2, z, e * CUT:(e + 1) * CUT],
                                             start=(opens and e == 0 and z == 0),
                                             stop=(closes and e == 1 and z == 1))
                last.then_inc(S["pv_done"], 1)

            with pe.Fori(0, PAIRS) as i:
                for l in range(2):
                    n = 2 * i + l
                    transpose_xn(n, 1)
                    for t in range(TILES):
                        if t >= 2:
                            need(pe, "q_copied", n, t - 1)
                        for gg in range(G):
                            rows = 97 - gg
                            last = t_.matmul(bank[4 + t % 2][0:SIZE[t], 0:C],
                                             xT[0:rows, gg, START[t]:START[t] + SIZE[t]],
                                             w_qkv[l][0:rows, gg, 0:C], start=(gg == 0), stop=(gg == 1))
                        last.then_inc(S["q_done"], 1)
                    for t in range(TILES):
                        need(pe, "q_copied", n, t + 1)
                        for gg in range(G):
                            last = t_.transpose(bank[gg][0:96, START[t]:START[t] + SIZE[t]],
                                                q_flat[0:SIZE[t], t, 96 * gg:96 * gg + 96],
                                                ident[0:SIZE[t], 0:SIZE[t]])
                    last.then_inc(S["qT_done"], 1)
                    need(pe, "qT_lo", n, 1)
                    need(pe, "qT_hi", n, 1)
                    for t in range(TILES):
                        for gg in range(G):
                            if t >= 2:
                                need(pe, ["dist_lo", "dist_hi"][gg], n, t - 1)
                            t_.matmul(bank[2 + (2 * t + gg) % 4][0:SIZE[t], 0:2 * RT * HG],
                                      qT[:, gg, START[t]:START[t] + SIZE[t]], w_rel[l][:, :], start=True, stop=True)\
                                .then_inc(S["dist_done"], 1)
                    def transpose_k(t):
                        need(pe, "kv_lo", n, t + 1)
                        for b in range(2):
                            if t >= 1:
                                need(pe, "k_even", n, 2 * t + b - 1)
                                need(pe, "k_odd", n, 2 * t + b - 1)
                            for p in range(3):
                                last = t_.transpose(bank[6 + b][:, p * KEYS[t]:(p + 1) * KEYS[t]],
                                                    k_tok[0:KEYS[t], t % 2, 128 * (3 * b + p):128 * (3 * b + p) + 128]
                                                    .bitcast(F32), ident[0:KEYS[t], 0:KEYS[t]])
                            last.then_inc(S["kT_done"], 1)

                    for t in range(TILES):
                        if t >= 2:
                            need(pe, "kv_lo", n, t - 1)
                        for gg in range(G):
                            rows = 97 - gg
                            last = t_.matmul(bank[t % 2][0:KEYS[t], 0:2 * C],
                                             xT[0:rows, gg, START[t]:START[t] + KEYS[t]],
                                             w_qkv[l][0:rows, gg, C:3 * C], start=(gg == 0), stop=(gg == 1))
                        last.then_inc(S["kv_done"], 1)
                        if t >= 1:
                            transpose_k(t - 1)
                    transpose_k(TILES - 1)
                    need(pe, "k_even", n, 10)
                    need(pe, "k_odd", n, 10)
                    for c in range(3 * TILES):
                        t, b = c // 3, c % 3
                        need(pe, "rel_placed", n, t + 1)
                        need(pe, "q_placed", n, t + 1)
                        if c >= 4:
                            need(pe, ["qaug_act", "qaug_dve"][c % 2], n, (c - 4) // 2 + 1)
                        for e in range(4):
                            at = (4 * b + e) * QSLOT
                            last = t_.transpose(bank[4 + c % 4][0:QSLOT, e * SIZE[t]:(e + 1) * SIZE[t]],
                                                q_tok[0:SIZE[t], t % QT, at:at + QSLOT].bitcast(F32),
                                                ident[0:SIZE[t], 0:SIZE[t]])
                        last.then_inc(S["qaug_done"], 1)
                    need(pe, "qaug_act", n, 8)
                    need(pe, "qaug_dve", n, 7)
                    need(pe, "dist_lo", n, 5)
                    need(pe, "dist_hi", n, 5)
                    k = 0
                    for j in range(STEPS + 4):
                        while k < len(SLOTS) and SLOTS[k][0] == j:
                            scores(n, k)
                            k += 1
                        if 3 <= j < STEPS + 3:
                            transpose_probs(n, j - 3)
                        if j >= 4:
                            values(n, j - 4)
                    need(pe, "oT_ready", n, len(OUT_UNITS))
                    for t in range(TILES):
                        if t >= 2:
                            need(pe, "mid_ready", n, t - 1)
                        for gg in range(QUADS):
                            last = t_.matmul(bank[2 + t % 2][0:SIZE[t], 0:C], oT[:, gg, START[t]:START[t] + SIZE[t]],
                                             w_proj[l][:, gg, :], start=(gg == 0), stop=(gg == QUADS - 1))
                        last.then_inc(S["proj_done"], 1)
                    transpose_xn(n, 2)
                    for f in range(MC):
                        if f >= 4:
                            need(pe, "gelu_done", n, f - 3)
                        for gg in range(G):
                            last = t_.matmul(bank[4 + f % 4][:, :], w_up[l][:, gg, 128 * f:128 * f + 128],
                                             xT[0:96, gg, 0:TOK], start=(gg == 0), stop=(gg == 1))
                        last.then_inc(S["up_done"], 1)
                    for t in range(TILES):
                        if t >= 4:
                            need(pe, "out_ready", n, t - 3)
                        for f in range(MC):
                            if t == 0:
                                need(pe, "gelu_done", n, f + 1)
                            last = t_.matmul(bank[2 + t % 4][0:SIZE[t], 0:C], hidden[:, f, START[t]:START[t] + SIZE[t]],
                                             w_down[l][:, f, :], start=(f == 0), stop=(f == MC - 1))
                        last.then_inc(S["down_done"], 1)


PRESETS = 4 + 2 + 4
WEIGHTS = 4 + 5


def fourier_loop(nc, d, bank):
    with ExitStack() as ctx:
        def sb(name, shape):
            return ctx.enter_context(nc.sbuf_tensor(name, shape, F32))

        def sem(name):
            return ctx.enter_context(nc.semaphore(name))

        fwd = sb("fwd", [128, 2, 2 * FREQ])
        inv = sb("inv", [FC, 4, 2 * 128])
        w1 = [sb(f"w1_{l}", [96, G, 3, 96]) for l in range(2)]
        w2 = [sb(f"w2_{l}", [97, G, 3, 96]) for l in range(2)]
        b1 = [sb(f"b1_{l}", [96, 2, G]) for l in range(2)]
        y_in = sb("y_in", [128, 4, C])
        y_mid = sb("y_mid", [128, 4, C])
        y_out = sb("y_out", [128, 4, C])
        xf = sb("xf", [96, G, 2, 2, FREQ])
        o1 = sb("o1", [97, G, 2, 2, FREQ])
        seed = sb("f_seed", [1, 1])
        clamp = sb("clamp", [FC, 4, G * 2 * 96])
        o2 = sb("o2", [FC, 4, 2, C])
        setup = sem("f_setup")
        preset = sem("f_preset")
        names = ("f_loaded fwd_done xf_a xf_b mix1_done relu_done mix2_done clamped o2_ready inv_done y_ready "
                 "f_stored").split()
        S = {n: sem(n) for n in names}
        PER = dict(fwd_done=4, xf_a=2, xf_b=2, mix1_done=4, relu_done=4, mix2_done=4, clamped=4, o2_ready=4,
                   inv_done=4, y_ready=4)
        SETUP = 16 * (2 + 2 * 10)

        def need(eng, name, n, k):
            eng.wait_ge(S[name], n * PER[name] + k)

        block = ctx.enter_context(nc.Block())

        @block.sync
        def _(sp):
            def load(dst, src):
                sp.dma_start(dst, src).then_inc(setup, 16)

            sp.dma_start(y_in[:, :, :], d["mid"][0:2].rearrange("a h w c -> (a h w) c")
                         .rearrange("(t p) c -> p t c", p=128)).then_inc(S["f_loaded"], 16)
            load(fwd[:, :, :], d["fwd"].rearrange("(k p) f -> p k f", p=128))
            load(inv[:, :, :], d["inv"].rearrange("(k p) t -> p k t", p=FC))
            for l in range(2):
                for r in range(2):
                    load(w1[l][:, :, r, :], d["fw1"][l, r].rearrange("g p e -> p g e"))
                    load(w2[l][0:96, :, 1 + r, :], d["fw2"][l, r].rearrange("g p e -> p g e"))
                    load(b1[l][:, r, :], d["fb1"][l, r])
                load(w2[l][96:97, :, 1, :], d["fb2"][l, 0:1].rearrange("o (g e) -> o g e", g=G))
                load(w2[l][96:97, :, 2, :], d["fb2"][l, 1:2].rearrange("o (g e) -> o g e", g=G))
                load(w1[l][:, :, 2, :], d["fw1"][l, 1].rearrange("g p e -> p g e"))
                load(w2[l][0:96, :, 0, :], d["fw2"][l, 1].rearrange("g p e -> p g e"))
            sp.dma_start(seed[:, :], d["ident"][0:1, 0:1]).then_inc(S["f_stored"], 16)

            def store(i):
                need(sp, "y_ready", 2 * i + 1, 4)
                sp.dma_start(d["out"][bass.ds(2 * i, 2)].rearrange("a h w c -> (a h w) c")
                             .rearrange("(t p) c -> p t c", p=128), y_out[:, :, :]).then_inc(S["f_stored"], 16)

            with sp.Fori(0, PAIRS - 1) as i:
                need(sp, "y_ready", 2 * i, 4)
                sp.dma_start(y_in[:, :, :], d["mid"][bass.ds(2 * i + 2, 2)].rearrange("a h w c -> (a h w) c")
                             .rearrange("(t p) c -> p t c", p=128)).then_inc(S["f_loaded"], 16)
                store(i)
            store(PAIRS - 1)
            sp.wait_ge(S["f_stored"], 16 + 16 * PAIRS)
            sp.wait_ge(S["f_loaded"], 16 * PAIRS)

        @block.gpsimd
        def _(pool):
            pool.wait_ge(setup, SETUP)
            for l in range(2):
                nc.gpsimd.tensor_scalar(w1[l][:, :, 2, :], w1[l][:, :, 2, :], -1.0, None, ALU.mult)\
                    .then_inc(preset, 1)
                nc.gpsimd.tensor_scalar(w2[l][0:96, :, 0, :], w2[l][0:96, :, 0, :], -1.0, None, ALU.mult)\
                    .then_inc(preset, 1)

        def xf_view(gg, a):
            return xf[:, gg, :, a, :]

        @block.vector
        def _(dve):
            v = nc.vector
            v.memset(o1[96:97, :, :, :, :], 1.0).then_inc(preset, 1)
            dve.wait_ge(preset, 5)
            with dve.Fori(0, PAIRS) as i:
                for l in range(2):
                    n = 2 * i + l
                    for gg in range(G):
                        need(dve, "fwd_done", n, 2 * gg + 1)
                        v.tensor_scalar(xf_view(gg, 0), bank[2 * gg][0:96, 0:2 * FREQ]
                                        .rearrange("p (r f) -> p r f", r=2), FWD[l], None, ALU.mult)\
                            .then_inc(S["xf_a"], 1)
                    for k in range(4):
                        need(dve, "mix2_done", n, k + 1)
                        v.tensor_scalar(clamp[:, k, :], bank[k][0:FC, 0:4 * 96], -LAMBDA, LAMBDA, ALU.max, ALU.min)\
                            .then_inc(S["clamped"], 1)
                        need(dve, "clamped", n, k + 1)
                        v.tensor_tensor(o2[:, k, :, :].rearrange("p r (g e) -> p g r e", g=G),
                                        bank[k][0:FC, 0:4 * 96].rearrange("p (g r e) -> p g r e", g=G, r=2),
                                        clamp[:, k, :].rearrange("p (g r e) -> p g r e", g=G, r=2), ALU.subtract)\
                            .then_inc(S["o2_ready"], 1)
                    if l == 1:
                        dve.wait_ge(S["f_stored"], 16 * i + 16)
                    src, dst = (y_in, y_mid) if l == 0 else (y_mid, y_out)
                    for t in range(4):
                        need(dve, "inv_done", n, t + 1)
                        v.scalar_tensor_tensor(out=dst[:, t, :], in0=bank[4 + t][:, 0:C], scalar=INV[l],
                                               in1=src[:, t, :], op0=ALU.mult, op1=ALU.add)\
                            .then_inc(S["y_ready"], 1)

        @block.scalar
        def _(act):
            s = nc.scalar
            act.wait_ge(preset, 5)
            with act.Fori(0, PAIRS) as i:
                for l in range(2):
                    n = 2 * i + l
                    for gg in range(G):
                        need(act, "fwd_done", n, 2 * gg + 2)
                        s.activation(xf_view(gg, 1), bank[2 * gg + 1][0:96, 0:2 * FREQ]
                                     .rearrange("p (r f) -> p r f", r=2), ACT.Copy, scale=FWD[l])\
                            .then_inc(S["xf_b"], 1)
                    for k in range(4):
                        gg, r = k // 2, k % 2
                        need(act, "mix1_done", n, k + 1)
                        s.activation(o1[0:96, gg, r, :, :].rearrange("p a f -> p (a f)"),
                                     bank[4 + k][0:96, 0:2 * FREQ], ACT.Relu, bias=b1[l][:, r, gg:gg + 1])\
                            .then_inc(S["relu_done"], 1)

        @block.tensor
        def _(pe):
            t_ = nc.tensor
            pe.wait_ge(preset, 5)
            with pe.Fori(0, PAIRS) as i:
                for l in range(2):
                    n = 2 * i + l
                    if l == 0:
                        pe.wait_ge(S["f_loaded"], 16 * i + 16)
                    else:
                        need(pe, "y_ready", 2 * i, 4)
                    src = y_in if l == 0 else y_mid
                    for gg in range(G):
                        for a in range(2):
                            for k in range(2):
                                last = t_.matmul(bank[2 * gg + a][0:96, 0:2 * FREQ],
                                                 src[:, 2 * a + k, 96 * gg:96 * gg + 96], fwd[:, k, :],
                                                 start=(k == 0), stop=(k == 1))
                            last.then_inc(S["fwd_done"], 1)
                    for gg in range(G):
                        need(pe, "xf_a", n, gg + 1)
                        need(pe, "xf_b", n, gg + 1)
                        for r in range(2):
                            for z in range(2):
                                w = (0 if z == 0 else 2) if r == 0 else (1 if z == 0 else 0)
                                last = t_.matmul(bank[4 + 2 * gg + r][0:96, 0:2 * FREQ], w1[l][:, gg, w, :],
                                                 xf[:, gg, z, :, :].rearrange("p a f -> p (a f)"),
                                                 start=(z == 0), stop=(z == 1))
                            last.then_inc(S["mix1_done"], 1)
                    for a in range(2):
                        for c in range(2):
                            for gg in range(G):
                                if a == 0 and c == 0:
                                    need(pe, "relu_done", n, 2 * gg + 2)
                                lo = a * FREQ + c * FC
                                for z in range(2):
                                    rows = 97 - z
                                    rhs = w2[l][0:rows, gg, 1:3, :] if z == 0 else w2[l][0:96, gg, 0:2, :]
                                    last = t_.matmul(bank[2 * a + c][0:FC, 192 * gg:192 * gg + 192],
                                                     o1[0:rows, gg, z, :, :].rearrange("p a f -> p (a f)")[:, lo:lo + FC],
                                                     rhs.rearrange("p r e -> p (r e)"), start=(z == 0), stop=(z == 1))
                            last.then_inc(S["mix2_done"], 1)
                    for a in range(2):
                        for hf in range(2):
                            need(pe, "o2_ready", n, 2 * a + 2)
                            for c in range(2):
                                for z in range(2):
                                    last = t_.matmul(bank[4 + 2 * a + hf][:, 0:C],
                                                     inv[:, 2 * c + z, 128 * hf:128 * hf + 128], o2[:, 2 * a + c, z, :],
                                                     start=(c == 0 and z == 0), stop=(c == 1 and z == 1))
                            last.then_inc(S["inv_done"], 1)


def kernel(**inputs):
    import numpy as np
    import concourse.bacc as bacc
    from concourse.bass_utils import run_bass_kernel_spmd

    def get(name):
        return np.asarray(inputs[name])

    order = []
    at = np.arange(HH * WW).reshape(HH, WW)
    for a in range(2):
        order.append(a * 256 + at[0:WS, 0:WS].ravel())
    for rows, cols in ((slice(0, WS), slice(WS, WW)), (slice(WS, HH), slice(0, WS)), (slice(WS, HH), slice(WS, WW))):
        for a in range(2):
            order.append(a * 256 + at[rows, cols].ravel())
    order = np.concatenate(order)
    x = get("x").reshape(PAIRS, TOK, C)[:, order]
    x = np.concatenate([x, x[:1]])

    def rel_blocks(name):
        out = np.zeros((96, 2, RT, HG), np.float32)
        for axis, part in enumerate("hw"):
            r = get(f"{name}_rel_pos_{part}")[::-1]
            for h in range(HG):
                out[HD * h:HD * h + HD, axis, :, h] = r.T
        return out.reshape(96, 2 * RT * HG)

    def blocks(w):
        out = np.zeros((G, 96, 96), np.float32)
        for b in range(8):
            s = slice(24 * (b % 4), 24 * (b % 4) + 24)
            out[b // 4, s, s] = w[b]
        return out

    pos = order % 256
    ph, pw = (pos // WW) % WS, (pos % WW) % WS
    onehot = np.zeros((2, RW, TOK + 2), np.float32)
    onehot[:, ph, np.arange(TOK)] = 1
    onehot[:, WS + pw, np.arange(TOK)] = 1
    onehot = onehot.reshape(2 * RW, TOK + 2)
    c = np.arange(4 * HALF, TOK)
    row, col = (order[c] % 256) // WW, order[c] % WW
    window = (order[c] // 256) * 4 + (row >= WS) * 2 + (col >= WS)
    classes = np.unique(window)
    q_class = np.zeros((CLASSES, CUT), np.float32)
    q_class[:len(classes)] = classes[:, None] == window[None]
    cut_mask = np.zeros((CLASSES, 2, CK), np.float32)
    cut_mask[:len(classes), :, :CUT] = np.where(classes[:, None] == window[None], 0, BIG)[:, None]
    ky, kx = np.arange(WIN) // WS, np.arange(WIN) % WS
    real_y = ky[None] + WS * (classes // 2 % 2)[:, None] < HH
    real_x = kx[None] + WS * (classes % 2)[:, None] < WW
    pad_mask = np.zeros((CLASSES, 2, WIN), np.float32)
    pad_mask[:len(classes)] = np.where(real_y & real_x, BIG, 0)[:, None]
    cut_mask, pad_mask = cut_mask.reshape(CLASSES, 2 * CK), pad_mask.reshape(CLASSES, 2 * WIN)
    th, tw = np.arange(256) // WW, np.arange(256) % WW
    kh, kw = np.arange(FREQ) // 9, np.arange(FREQ) % 9
    turn = ((th[:, None] * kh[None] + tw[:, None] * kw[None]) % 16) * (2 * np.pi / 16)
    fwd = np.concatenate([np.cos(turn), -np.sin(turn)], 1).astype(np.float32)
    weight = np.where((kw == 0) | (kw == 8), 1.0, 2.0)[:, None]
    icos, isin = weight * np.cos(turn.T), -weight * np.sin(turn.T)
    inv = np.concatenate([icos[:FC], isin[:FC], icos[FC:], isin[FC:]]).astype(np.float32)

    L = ("L0_conv", "L1_conv")
    both = {
        "ln1_w": ("n1_w", "ln1_g"), "ln1_b": ("n1_b", "ln1_b"), "ln2_w": ("n2_w", "ln2_g"), "ln2_b": ("n2_b", "ln2_b"),
        "qkv_w": ("qkv_w",) * 2, "qkv_b": ("qkv_b",) * 2, "proj_w": ("proj_w",) * 2, "proj_b": ("proj_b",) * 2,
        "up_w": ("lin1_w", "mlp_w1"), "up_b": ("lin1_b", "mlp_b1"),
        "down_w": ("lin2_w", "mlp_w2"), "down_b": ("lin2_b", "mlp_b2"),
    }
    arrays = {"x": x}
    for key, (a, b) in both.items():
        arrays[key] = np.stack([get(f"{L[0]}_{a}"), get(f"{L[1]}_{b}")])
    arrays["rel"] = np.stack([rel_blocks(n) for n in L])
    arrays["fw1"] = np.stack([np.stack([blocks(get("L2_conv_w1r")), blocks(get("L2_conv_w1i"))]),
                              np.stack([blocks(w) for w in get("L3_conv_w1")])])
    arrays["fw2"] = np.stack([np.stack([blocks(get("L2_conv_w2r")), blocks(get("L2_conv_w2i"))]),
                              np.stack([blocks(w) for w in get("L3_conv_w2")])])
    for k in "12":
        arrays[f"fb{k}"] = np.stack([np.stack([get(f"L2_conv_b{k}r").reshape(C), get(f"L2_conv_b{k}i").reshape(C)]),
                                     get(f"L3_conv_b{k}").reshape(2, C)])
    w = arrays["proj_w"].reshape(2, QUADS, QUAD, 1, HD, C)
    arrays["proj_w"] = np.broadcast_to(w, (2, QUADS, QUAD, 2, HD, C)).reshape(2, QUADS, 128, C).transpose(0, 2, 1, 3)
    for k in ("ln1_w", "ln1_b", "ln2_w", "ln2_b"):
        arrays[k] = arrays[k].reshape(2, G, 96).transpose(0, 2, 1)
    arrays["up_b"] = arrays["up_b"].reshape(2, MC, 128).transpose(0, 2, 1)
    arrays["fb1"] = arrays["fb1"].reshape(2, 2, G, 96).transpose(0, 1, 3, 2)
    arrays.update(ident=np.eye(128, dtype=np.float32), onehot=onehot, q_class=q_class, cut_mask=cut_mask, pad_mask=pad_mask,
                  fwd=fwd, inv=inv)
    arrays = {k: np.ascontiguousarray(a) for k, a in arrays.items()}

    nc = bacc.Bacc("TRN2", target_bir_lowering=False, num_devices=1)
    d = {k: nc.dram_tensor(f"in_{k}", a.shape, F32, kind="ExternalInput").ap() for k, a in arrays.items()}
    d["dist"] = nc.dram_tensor("distances", (2, TOK, UROW), F32, kind="Internal").ap()
    d["mid"] = nc.dram_tensor("between_loops", (B, HH, WW, C), F32, kind="Internal").ap()
    d["out"] = nc.dram_tensor("out", (B, HH, WW, C), F32, kind="ExternalOutput").ap()
    build(nc, d)
    r = run_bass_kernel_spmd(nc, [{f"in_{k}": a for k, a in arrays.items()}], core_ids=[0])
    return r.results[0]["out"]
```

```python
import concourse.bass as bass
from concourse import mybir
from contextlib import ExitStack

F32 = mybir.dt.float32
F32R = mybir.dt.float32r
BF16 = mybir.dt.bfloat16
ALU = mybir.AluOpType
ACT = mybir.ActivationFunctionType
AX = mybir.AxisListType

B, HH, WW, C = 8, 16, 16, 192
PAIRS = B // 2
WS = 14
NH, HD = 12, 16
HALF = WS // 2 * WS
WIN = WS * WS
CUT = 2 * (HH * WW - WIN)
TOK = 2 * HH * WW
TILES = 5
SIZE = [HALF] * 4 + [CUT]
START = [HALF * t for t in range(5)]
KEYS = [HALF] * 4 + [CUT + 1]
G = C // 96
HG = NH // G
KSLOT = 4 * HD
RW = 2 * WS
QSLOT = KSLOT + 2 * RW
RT = 2 * WS - 1
UROW = 2 * RT * NH
MLP = 4 * C
MC = MLP // 128
QSCALE = HD ** -0.5
EPS = [1e-5, 1e-6]
BIG = -1.0e30
CUTS = HG // 2
CK = CUT + 2
CLASSES = 128
FREQ = HH * (WW // 2 + 1)
FC = FREQ // 2
LAMBDA = 0.01
FWD = [1.0 / 16, 1.0]
INV = [1.0 / 16, 1.0 / 256]


def unit_order():
    order = []
    for k in range(2 * G):
        heads = [(k // G, HG * (k % G) + e) for e in range(HG)]
        if 1 <= k <= G:
            for e, cut in ((5, 2), (3, 1), (1, 0)):
                heads.insert(e, (None, CUTS * (k - 1) + cut))
        order += heads
    return order


SEQ = unit_order()
STEPS = len(SEQ)
SLOTS = [(j, part) for j, (a, _) in enumerate(SEQ) for part in (("full",) if a is not None else ("pad", "cut"))]
S_BANKS = (0, 1, 6, 7)
OUT_BANKS = (4, 5)
BY_ACT = [j for j in range(STEPS) if j % 2 == 1]
BY_DVE = [j for j in range(STEPS) if j % 2 != 1]


def slot(j, part):
    return SLOTS.index((j, part))


def output(j):
    a, h = SEQ[j]
    if a is not None:
        return (G * a + h // HG) % 2, h % HG == 0, h % HG == HG - 1
    return h // CUTS % 2, h % CUTS == 0, h % CUTS == CUTS - 1


def copied(j):
    name, mine = ("probsT_act", BY_ACT) if j in BY_ACT else ("probsT_dve", BY_DVE)
    return name, mine.index(j) + 1


OUT_UNITS = [j for j in range(STEPS) if output(j)[2]]


def free_output(j):
    mine = [n for n, u in enumerate(OUT_UNITS) if u < j and output(u)[0] == output(j)[0]]
    return mine[-1] + 1 if mine else 0


MIDDLE = [("dist", 0), ("kv", 0), ("dist", 1), ("dist", 2), ("kv", 1), ("dist", 3), ("kT", 0), ("dist", 4),
          ("kv", 2), ("kT", 1), ("kv", 3), ("kT", 2), ("kv", 4), ("kT", 3)]


def build(nc, d):
    with ExitStack() as ctx:
        def sb(name, shape):
            return ctx.enter_context(nc.sbuf_tensor(name, shape, F32))

        def sem(name):
            return ctx.enter_context(nc.semaphore(name))

        bank = [ctx.enter_context(nc.psum_tensor(f"bank{i}", [128, 512], F32)) for i in range(8)]
        setup = sem("setup")
        setup_qkv = sem("setup_qkv")
        setup_rest = sem("setup_rest")
        preset = sem("preset")
        weights = sem("weights")
        ident = sb("ident", [128, 128])
        half_pow = sb("half_pow", [128, TILES])
        fwd = sb("fwd", [128, 2, 2, FC])
        inv = sb("inv", [FC, 2, 2, 128])
        w1 = [sb(f"w1_{l}", [128, 4, 128]) for l in range(2)]
        w2 = [sb(f"w2_{l}", [128, 4, 96]) for l in range(2)]
        b1 = [sb(f"b1_{l}", [128, 4]) for l in range(2)]
        xn = sb("xn", [128, TILES, C])
        x_mid = [sb(f"x_mid{l}", [128, TILES, C]) for l in range(2)]
        stored = sem("stored")
        f_loaded = sem("f_loaded")
        rel = sb("rel", [128, TILES, RW * NH])
        fold = rel[:, :, :].rearrange("p t m -> p (t m)")[:, 0:2 * 2 * 4 * 64]\
            .rearrange("p (z a g e) -> p z a g e", z=2, a=2, g=4)
        half = sb("half", [128, 1])
        sums = sem("sums")
        folded = sem("folded")
        fourier = (fwd, inv, w1, w2, b1, xn, f_loaded, fold, half, sums, folded)
        attention_loop(nc, d, bank, setup, setup_qkv, setup_rest, preset, weights, ident, half_pow, x_mid, rel,
                       stored, fourier)
        fourier_loop(nc, d, bank, stored, fourier)


def attention_loop(nc, d, bank, setup, setup_qkv, setup_rest, preset, weights, ident, half_pow, x_mid, rel,
                   stored, fourier):
    with ExitStack() as ctx:
        def sb(name, shape, dtype=F32):
            return ctx.enter_context(nc.sbuf_tensor(name, shape, dtype))

        def sem(name):
            return ctx.enter_context(nc.semaphore(name))

        xn, f_loaded, fold, half = fourier[5:9]
        w_qkv = [sb(f"w_qkv{l}", [97, G, 3 * C]) for l in range(2)]
        w_rel = [sb(f"w_rel{l}", [96, 2 * RT * HG]) for l in range(2)]
        w_proj = [sb(f"w_proj{l}", [96, G, C]) for l in range(2)]
        b_proj = [sb(f"b_proj{l}", [128, C]) for l in range(2)]
        w_up = [sb(f"w_up{l}", [96, G, MLP]) for l in range(2)]
        w_down = [sb(f"w_down{l}", [128, MC, C]) for l in range(2)]
        b_up = [sb(f"b_up{l}", [128, MC]) for l in range(2)]
        b_down = [sb(f"b_down{l}", [128, C]) for l in range(2)]
        affine = [sb(f"affine{l}", [96, 4, G]) for l in range(2)]
        q_class = sb("q_class", [CLASSES, CUT], BF16)
        cut_mask = sb("cut_mask", [CLASSES, 2 * CK], BF16)
        pad_mask = sb("pad_mask", [CLASSES, 2 * WIN], BF16)
        pad_keys = sb("pad_keys", [QSLOT, WIN], F32R)
        x_in = sb("x_in", [128, TILES, C])
        seed = sb("seed", [1, 1])
        wait_pad = sb("wait_pad", [1, 1])
        stats = sb("stats", [128, TILES, 6])
        moments = sb("moments", [128, TILES, 2])
        veps = sb("veps", [128, TILES])
        ones = sb("ones", [128, 1])
        rstd = sb("rstd", [128, TILES])
        xT = sb("xT", [97, G, TOK + 1])
        k_tok = sb("k_tok", [128, 2, NH * KSLOT], F32R)
        v_pad = sb("v_pad", [128, TILES, NH, 96])
        QT = 4
        LAG = 3
        q_tok = sb("q_tok", [128, QT * NH * QSLOT], F32R)
        probsT = q_tok[:, 0:2 * 2 * WIN].bitcast(F32).rearrange("p (s m) -> p s m", s=2)
        q_tok = q_tok[:, :].rearrange("p (t m) -> p t m", t=QT)
        q_out = sb("q_out", [128, TILES * C + G * TOK])
        q_flat = q_out[:, 0:TILES * C].rearrange("p (t c) -> p t c", t=TILES)
        qT = q_out[0:96, TILES * C:TILES * C + G * TOK].rearrange("p (g m) -> p g m", g=G)
        oT = q_out[0:96, 0:G * TOK].rearrange("p (g m) -> p g m", g=G)
        dist = sb("dist", [128, TILES, UROW])
        hidden = dist[:, :, :].rearrange("p t u -> p (t u)")[:, 0:MC * TOK].rearrange("p (m k) -> p m k", m=MC)
        q_aug = sb("q_aug", [QSLOT, NH, TOK], F32R)
        k_aug = sb("k_aug", [QSLOT, NH, TOK + 2], F32R)
        PS = 4
        probs = sb("probs", [128, PS, 2 * WIN])
        neg_max = sb("neg_max", [128, PS, 2])
        row_sum = sb("row_sum", [128, PS, 2])
        inv_sum = sb("inv_sum", [128, PS, 2])
        pad_bias = sb("pad_bias", [CUT, PS, 2])
        neg_pad = sb("neg_pad", [CUT, 2])
        neg_real = sb("neg_real", [CUT, 2])
        stage = dist[:, :, :].rearrange("p t u -> p (t u)")

        hot = stage[KSLOT:QSLOT, 1024:1024 + TOK + 2]

        names = ("x_loaded moments_ready rstd_ready veps_ready xn_ready xT_done xT_lo xT_hi q_done q_copied "
                 "qT_done qT_lo qT_hi dist_done dist_lo dist_hi kv_done kv_hi kv_lo kT_done k_even "
                 "k_odd q_hi q_placed rel_hi rel_placed qaug_done qaug_act qaug_dve scores_done max_ready exp_done "
                 "inv_ready probs_ready probsT_done probsT_act probsT_dve pv_done oT_ready proj_done base_ready "
                 "mid_ready midb_ready up_done gelu_done down_done out_ready order_dve").split()
        S = {n: sem(n) for n in names}
        dist_stored = [sem(f"dist_stored{t}") for t in range(TILES)]
        rel_loaded = [sem(f"rel_loaded{t}") for t in range(TILES)]
        PER = dict(moments_ready=10, veps_ready=10, rstd_ready=10, xn_ready=10, xT_done=2, xT_lo=2, xT_hi=2,
                   q_done=5, q_copied=5, qT_done=1, qT_lo=1, qT_hi=1, dist_done=10, dist_lo=5, dist_hi=5,
                   kv_done=5, kv_hi=5, kv_lo=5, kT_done=10, k_even=10, k_odd=10, q_hi=5, q_placed=5,
                   rel_hi=5, rel_placed=5, qaug_done=15, qaug_act=8, qaug_dve=7, scores_done=len(SLOTS), max_ready=STEPS,
                   exp_done=STEPS, inv_ready=STEPS, probs_ready=STEPS, probsT_done=STEPS, probsT_act=len(BY_ACT),
                   probsT_dve=len(BY_DVE), pv_done=STEPS, oT_ready=len(OUT_UNITS), proj_done=5, base_ready=1, mid_ready=5,
                   midb_ready=1, up_done=6, gelu_done=6, down_done=5, out_ready=5, order_dve=34)
        block = ctx.enter_context(nc.Block())

        def need(eng, name, n, k):
            eng.wait_ge(S[name], n * PER[name] + k)

        def v_columns(t):
            v = v_pad[0:KEYS[t], t, :, :].rearrange("p h s -> p (h s)")
            return bass.AP(v.tensor, v.offset, [v.ap[0], [HG * 96, G], [96 + HD, HG], [1, HD]])

        SETUP = 16 * (5 + 2)
        SETUP_QKV = 16 * (2 * 2 + 2)
        SETUP_REST = 16 * (2 * 5 + 2 + 2 + 2 * 3)

        R, D = UROW, NH

        def gather(eng, t, l, part, dims, first, at, count):
            src = bass.AP(d["dist"].tensor, l * UROW * TOK + first, dims + [[1, WS * NH]])
            eng.dma_start(rel[at:at + count, t, part * WS * NH:(part + 1) * WS * NH], src).then_inc(rel_loaded[t], 16)

        def gather_cut(eng, l, a):
            base, top = START[4] * R, (WS - 1) * D
            at = 28 * a
            gather(eng, 4, l, 0, [[2 * R - D, WS], [R, 2]], base + at * R + top, at, 28)
            gather(eng, 4, l, 1, [[2 * R, WS], [R - D, 2]], base + at * R + RT * NH + top, at, 28)
            at = 56 + 28 * a
            gather(eng, 4, l, 0, [[WS * R - D, 2], [R, WS]], base + at * R + top, at, 28)
            gather(eng, 4, l, 1, [[WS * R, 2], [R - D, WS]], base + at * R + RT * NH + top, at, 28)
            at = 112 + 4 * a
            gather(eng, 4, l, 0, [[2 * R - D, 2], [R, 2]], base + at * R + top, at, 4)
            gather(eng, 4, l, 1, [[2 * R, 2], [R - D, 2]], base + at * R + RT * NH + top, at, 4)

        @block.sync
        def _(sp):
            def load(dst, src):
                sp.dma_start(dst, src).then_inc(setup, 16)

            def load_x(i):
                sp.dma_start(x_in[0:HALF, 0:4, :],
                             d["x"][i, 0:4 * HALF, :].rearrange("(t n) c -> n t c", t=4)).then_inc(S["x_loaded"], 16)
                sp.dma_start(x_in[0:CUT, 4, :], d["x"][i, 4 * HALF:TOK, :]).then_inc(S["x_loaded"], 16)

            load_x(0)
            load(ident[:, :], d["ident"])
            load(stage[KSLOT:QSLOT, 1024:1024 + TOK + 2], d["onehot"])
            load(stage[:, 0:CUT], d["q_class"])
            load(stage[:, CUT:CUT + 2 * CK], d["cut_mask"])
            load(stage[:, CUT + 2 * CK:CUT + 2 * CK + 2 * WIN], d["pad_mask"])
            for l in range(2):
                load(affine[l][:, :, :], d["affine"][l])

            def load(dst, src):
                sp.dma_start(dst, src).then_inc(setup_qkv, 16)

            for l in range(2):
                load(w_qkv[l][0:96, :, :], d["qkv_w"][l].rearrange("(g p) n -> p g n", g=G))
                load(w_qkv[l][96:97, 0, :], d["qkv_b"][l].rearrange("(a n) -> a n", a=1))
            load(w_rel[0][:, :], d["rel"][0])
            load(b_proj[0][:, :], d["proj_b"][0].rearrange("(a n) -> a n", a=1).broadcast_to([128, C]))

            def load(dst, src):
                sp.dma_start(dst, src).then_inc(setup_rest, 16)

            for l in range(2):
                if l == 1:
                    load(w_rel[l][:, :], d["rel"][l])
                    load(b_proj[l][:, :], d["proj_b"][l].rearrange("(a n) -> a n", a=1).broadcast_to([128, C]))
                load(w_proj[l][:, :, :], d["proj_w"][l].rearrange("(g p) n -> p g n", g=G))
                load(b_down[l][:, :], d["down_b"][l].rearrange("(a n) -> a n", a=1).broadcast_to([128, C]))
                load(b_up[l][:, :], d["up_b"][l])
                load(w_up[l][:, :, :], d["up_w"][l].rearrange("(g p) n -> p g n", g=G))
                load(w_down[l][:, :, :], d["down_w"][l].rearrange("(g p) n -> p g n", g=MC))
            fwd, inv, w1, w2, b1 = fourier[:5]
            load(fwd[:, :, :, :], d["fwd"])
            load(inv[:, :, :, :], d["inv"])
            for l in range(2):
                load(w1[l][:, :, :], d["fw1"][l])
                load(w2[l][:, :, :], d["fw2"][l])
                load(b1[l][:, :], d["fb1"][l])
            sp.dma_start(seed[:, :], d["ident"][0:1, 0:1]).then_inc(stored, 16)

            with sp.Fori(0, PAIRS) as i:
                for l in range(2):
                    n = 2 * i + l
                    def store_distances(t):
                        need(sp, "dist_lo", n, t + 1)
                        need(sp, "dist_hi", n, t + 1)
                        sp.dma_start(d["dist"][l, START[t]:START[t] + SIZE[t], :], dist[0:SIZE[t], t, :])\
                            .then_inc(dist_stored[t], 16)

                    store_distances(0)
                    for t in range(4):
                        store_distances(t + 1)
                        sp.wait_ge(dist_stored[t], 16 * n + 16)
                        base = START[t] * R
                        gather(sp, t, l, 0, [[WS * R - D, 7], [R, WS]], base + (WS - 1 - 7 * (t % 2)) * D, 0, HALF)
                        gather(sp, t, l, 1, [[WS * R, 7], [R - D, WS]], base + RT * NH + (WS - 1) * D, 0, HALF)
                    sp.wait_ge(dist_stored[4], 16 * n + 16)
                    gather_cut(sp, l, 0)
                    gather_cut(sp, l, 1)
                    if l == 0:
                        need(sp, "base_ready", n, 1)
                        need(sp, "xn_ready", n, 5)
                        sp.dma_start(x_in[0:HALF, 0:4, :], d["x"][bass.ds(i + 1, 1), 0:4 * HALF, :]
                                     .rearrange("o (t n) c -> (o n) t c", t=4)).then_inc(S["x_loaded"], 16)
                        sp.dma_start(x_in[0:CUT, 4, :], d["x"][bass.ds(i + 1, 1), 4 * HALF:TOK, :]
                                     .rearrange("o n c -> (o n) c")).then_inc(S["x_loaded"], 16)
                for a in range(2):
                    img = d["mid"][bass.ds(2 * i + a, 1)].rearrange("o h w c -> (o h) w c")
                    for r in range(2):
                        need(sp, "out_ready", 2 * i + 1, 2 * a + r + 1)
                        sp.dma_start(img[7 * r:7 * r + 7, 0:WS, :], x_mid[1][0:HALF, 2 * a + r, :])\
                            .then_inc(stored, 16)
                need(sp, "out_ready", 2 * i + 1, 5)
                for a in range(2):
                    img = d["mid"][bass.ds(2 * i + a, 1)].rearrange("o h w c -> (o h) w c")
                    sp.dma_start(img[0:WS, WS:WW, :], x_mid[1][28 * a:28 * a + 28, 4, :]).then_inc(stored, 16)
                    sp.dma_start(img[WS:HH, 0:WS, :], x_mid[1][56 + 28 * a:84 + 28 * a, 4, :])\
                        .then_inc(stored, 16)
                    sp.dma_start(img[WS:HH, WS:WW, :], x_mid[1][112 + 4 * a:116 + 4 * a, 4, :])\
                        .then_inc(stored, 16)
            sp.wait_ge(S["x_loaded"], 32 * (PAIRS + 1))

        @block.gpsimd
        def _(pool):
            g = nc.gpsimd
            g.memset(half_pow[:, :], -0.5).then_inc(preset, 1)
            g.memset(ones[:, :], 1.0).then_inc(preset, 1)
            g.memset(veps[:, :], 1.0).then_inc(preset, 1)
            g.memset(moments[:, :, :], 1.0).then_inc(preset, 1)
            g.memset(half[:, :], 0.5).then_inc(preset, 1)
            g.memset(v_pad[:, :, :, :], 0.0).then_inc(weights, 1)
            pool.wait_ge(preset, PRESETS)

            def rsqrt(n, k):
                for t in range(TILES):
                    need(pool, "veps_ready", n, 5 * (k - 1) + t + 1)
                    g.tensor_tensor(rstd[:, t:t + 1], veps[:, t:t + 1], half_pow[:, 0:1], ALU.pow)\
                        .then_inc(S["rstd_ready"], 1)

            def normalise(n, j):
                need(pool, "inv_ready", n, j + 1)
                rows, k, m, step = (HALF, 2, WIN, WIN) if SEQ[j][0] is not None else (CUT, 2, CUT + 1, CK)
                p = probs[0:rows, j % PS, 0:k * step].rearrange("p (k m) -> p k m", k=k)[:, :, 0:m]
                g.tensor_tensor(p, p, inv_sum[0:rows, j % PS, 0:k].unsqueeze(2).to_broadcast([rows, k, m]),
                                ALU.mult).then_inc(S["probs_ready"], 1)

            def add_bias(dst, src, b):
                g.tensor_tensor(dst[0:HALF, 0:4, :], src[0:HALF, 0:4, :],
                                b[0:HALF, :].unsqueeze(1).to_broadcast([HALF, 4, C]), ALU.add)
                return g.tensor_tensor(dst[0:CUT, 4, :], src[0:CUT, 4, :], b[0:CUT, :], ALU.add)

            def place_q(n, t):
                need(pool, "q_copied", n, t + 1)
                if t >= QT:
                    need(pool, "qaug_done", n, 3 * (t - QT) + 3)
                q = q_tok[0:SIZE[t], t % QT, :].rearrange("p (h s) -> p h s", s=QSLOT)[:, :, 0:KSLOT]
                q = q.rearrange("p h (z d c) -> p h z d c", z=2, d=2)
                src = q_flat[0:SIZE[t], t, :].rearrange("p (h c) -> p h c", c=HD)
                one = ones[0:SIZE[t], :].unsqueeze(2).to_broadcast([SIZE[t], NH, HD])
                for e in range(2):
                    last = g.tensor_tensor(q[:, :, 0, e, :], src, one, ALU.mult)
                last.then_inc(S["q_hi"], 1)
                need(pool, "q_hi", n, t + 1)
                for e in range(2):
                    last = g.tensor_tensor(q[:, :, 1, e, :], src, q[:, :, 0, 0, :].bitcast(F32), ALU.subtract)
                last.then_inc(S["q_placed"], 1)

            rsqrt(0, 1)
            pool.wait_ge(setup_qkv, SETUP_QKV)
            with pool.Fori(0, PAIRS) as i:
                for l in range(2):
                    n = 2 * i + l
                    src = x_in if l == 0 else x_mid[0]
                    if l == 1:
                        pool.wait_ge(stored, 16 + 160 * i)
                    add_bias(x_mid[l], src, b_proj[l]).then_inc(S["base_ready"], 1)
                    for t in range(TILES):
                        place_q(n, t)
                    for j in range(STEPS):
                        normalise(n, j)
                    rsqrt(n, 2)
                    need(pool, "xn_ready", n, 10)
                    add_bias(x_mid[l], x_mid[l], b_down[l]).then_inc(S["midb_ready"], 1)
                    rsqrt(n + 1, 1)
            g.memset(fold[:, :, :, :, 48:64], 0.0)
            fold_input(nc, pool, 0, fourier)

        @block.vector
        def _(dve):
            v = nc.vector
            v.memset(xT[0:96, :, TOK:TOK + 1], 0.0).then_inc(preset, 1)
            v.memset(xT[96:97, 0, :], 1.0).then_inc(preset, 1)
            v.memset(k_aug[0:KSLOT, :, TOK + 1:TOK + 2].bitcast(F32), 0.0).then_inc(preset, 1)
            v.memset(pad_keys[0:KSLOT, :].bitcast(F32), 0.0).then_inc(preset, 1)
            dve.wait_ge(setup, SETUP)
            dve.wait_ge(preset, PRESETS)
            v.tensor_copy(q_class[:, :], stage[:, 0:CUT]).then_inc(weights, 1)
            v.tensor_copy(cut_mask[:, :], stage[:, CUT:CUT + 2 * CK]).then_inc(weights, 1)
            v.tensor_copy(pad_mask[:, :], stage[:, CUT + 2 * CK:CUT + 2 * CK + 2 * WIN]).then_inc(weights, 1)
            v.tensor_copy(pad_keys[KSLOT:QSLOT, :], hot[:, 0:WIN]).then_inc(weights, 1)
            v.tensor_copy(k_aug[KSLOT:QSLOT, 0:HG, :], hot.unsqueeze(1).to_broadcast([2 * RW, HG, TOK + 2]))\
                .then_inc(weights, 1)
            chain = [0]

            def after(n, ins):
                chain[0] += 1
                ins.then_inc(S["order_dve"], 1)
                need(dve, "order_dve", n, chain[0])

            def residual_norm(n, l, src, k, total=None, add=None):
                for step in range(TILES + 2):
                    if add and step < TILES:
                        add(step)
                    t = step - 1
                    if 0 <= t < TILES:
                        if add:
                            need(dve, *total, t + 1)
                        after(n, v.bn_stats(stats[0:SIZE[t], t, :], src[0:SIZE[t], t, :]))
                        v.memset(wait_pad[:, :], 0.0)
                        v.bn_aggr(moments[0:SIZE[t], t, :], stats[0:SIZE[t], t, :]).then_inc(S["moments_ready"], 1)
                        need(dve, "moments_ready", n, 5 * (k - 1) + t + 1)
                        v.tensor_scalar(veps[0:SIZE[t], t:t + 1], moments[0:SIZE[t], t, 1:2], EPS[l], None, ALU.add)\
                            .then_inc(S["veps_ready"], 1)
                    if step >= 2:
                        normal(n, src, k, step - 2)

            def normal(n, src, k, t):
                need(dve, "rstd_ready", n, 5 * (k - 1) + t + 1)
                v.tensor_scalar(xn[0:SIZE[t], t, :], src[0:SIZE[t], t, :], moments[0:SIZE[t], t, 0:1],
                                rstd[0:SIZE[t], t:t + 1], ALU.subtract, ALU.mult).then_inc(S["xn_ready"], 1)

            def attend(n, j):
                a, h = SEQ[j]
                sl = j % PS
                if a is not None:
                    k = slot(j, "full")
                    need(dve, "scores_done", n, k + 1)
                    v.tensor_reduce(neg_max[0:HALF, sl, 0:2], bank[S_BANKS[k % 4]][0:HALF, 0:2 * WIN]
                                    .rearrange("p (r m) -> p r m", r=2), AX.X, ALU.max,
                                    negate=True).then_inc(S["max_ready"], 1)
                    return
                k = slot(j, "pad")
                need(dve, "scores_done", n, k + 1)
                v.tensor_reduce(neg_pad[:, :], bank[S_BANKS[k % 4]][0:CUT, 0:2 * WIN]
                                .rearrange("p (r m) -> p r m", r=2), AX.X, ALU.max, negate=True)
                k = slot(j, "cut")
                need(dve, "scores_done", n, k + 1)
                s = bank[S_BANKS[k % 4]][0:CUT, 0:2 * CK].rearrange("p (e m) -> p e m", e=2)
                after(n, v.tensor_reduce(neg_real[:, :], s[:, :, 0:CUT], AX.X, ALU.max, negate=True))
                after(n, v.tensor_tensor(neg_pad[:, :], neg_pad[:, :], s[:, :, CUT], ALU.subtract))
                after(n, v.tensor_tensor(neg_max[0:CUT, sl, :], neg_real[:, :], neg_pad[:, :], ALU.min))
                v.tensor_tensor(pad_bias[:, sl, :], s[:, :, CUT], neg_max[0:CUT, sl, :], ALU.add)\
                    .then_inc(S["max_ready"], 1)

            def invert(n, j):
                sl = j % PS
                need(dve, "exp_done", n, j + 1)
                rows = HALF if SEQ[j][0] is not None else CUT
                if SEQ[j][0] is None:
                    mass = probs[0:CUT, sl, 0:2 * CK].rearrange("p (e m) -> p e m", e=2)[:, :, CUT]
                    after(n, v.tensor_tensor(row_sum[0:CUT, sl, :], row_sum[0:CUT, sl, :], mass, ALU.add))
                v.reciprocal(inv_sum[0:rows, sl, :], row_sum[0:rows, sl, :]).then_inc(S["inv_ready"], 1)

            def copy_probsT(n, j):
                need(dve, "probsT_done", n, j + 1)
                if j >= 2:
                    need(dve, "pv_done", n, j - 1)
                rows, m = (HALF, 4 * HALF) if SEQ[j][0] is not None else (CUT + 1, 2 * CUT)
                v.tensor_copy(probsT[0:rows, j % 2, 0:m], bank[2 + j % 2][0:rows, 0:m])\
                    .then_inc(S["probsT_dve"], 1)

            def copy_dist(n, t):
                need(dve, "dist_done", n, 2 * t + 1)
                v.tensor_copy(dist[0:SIZE[t], t, :].rearrange("p (r h) -> p r h", h=NH)[:, :, 0:HG],
                              bank[2 + 2 * t % 4][0:SIZE[t], 0:2 * RT * HG].rearrange("p (r h) -> p r h", h=HG))\
                    .then_inc(S["dist_lo"], 1)

            def k_low(n, t):
                need(dve, "kv_hi", n, t + 1)
                k = k_tok[0:KEYS[t], t % 2, :].rearrange("p (h d z c) -> p h d z c", d=2, z=2, c=HD)
                src = bank[t % 2][0:KEYS[t], 0:C].rearrange("p (h c) -> p h c", c=HD)
                v.tensor_tensor(k[:, :, :, 1, :], src.unsqueeze(2).to_broadcast([KEYS[t], NH, 2, HD]),
                                k[:, :, :, 0, :].bitcast(F32), ALU.subtract).then_inc(S["kv_lo"], 1)

            def copy_odd(n, t):
                for b in range(2):
                    need(dve, "kT_done", n, 2 * t + b + 1)
                    v.tensor_copy(k_aug[0:KSLOT, 6 * b + 1:6 * b + 6:2, START[t]:START[t] + KEYS[t]],
                                  bank[6 + b][KSLOT:128, 0:3 * KEYS[t]].rearrange("p (k m) -> p k m", k=3))\
                        .then_inc(S["k_odd"], 1)

            def place_rel(n, t):
                need(dve, "rel_hi", n, t + 1)
                q = q_tok[0:SIZE[t], t % QT, :].rearrange("p (h s) -> p h s", s=QSLOT)
                src = rel[0:SIZE[t], t, :].rearrange("p (r h) -> p h r", h=NH)
                v.tensor_tensor(q[:, :, KSLOT + RW:QSLOT], src, q[:, :, KSLOT:KSLOT + RW].bitcast(F32), ALU.subtract)\
                    .then_inc(S["rel_placed"], 1)

            def copy_qaug(n, t):
                for b in range(3):
                    c = 3 * t + b
                    if c % 2:
                        need(dve, "qaug_done", n, c + 1)
                        v.tensor_copy(q_aug[:, 4 * b:4 * b + 4, START[t]:START[t] + SIZE[t]],
                                      bank[4 + c % 4][0:QSLOT, 0:4 * SIZE[t]].rearrange("p (k m) -> p k m", k=4))\
                            .then_inc(S["qaug_dve"], 1)

            dve.wait_ge(S["x_loaded"], 32)
            residual_norm(0, 0, x_in, 1)
            dve.wait_ge(weights, WEIGHTS)
            with dve.Fori(0, PAIRS) as i:
                for l in range(2):
                    n = 2 * i + l
                    need(dve, "xT_done", n, 1)
                    v.tensor_scalar(xT[0:96, 0, 0:TOK], bank[0][0:96, :], affine[l][:, 0, 0:1], affine[l][:, 1, 0:1],
                                    ALU.mult, ALU.add).then_inc(S["xT_lo"], 1)
                    need(dve, "qT_done", n, 1)
                    v.tensor_copy(qT[:, 0, :], bank[2][0:96, :]).then_inc(S["qT_lo"], 1)
                    for what, t in MIDDLE:
                        {"dist": copy_dist, "kv": k_low, "kT": copy_odd}[what](n, t)
                    for t in range(TILES):
                        if t == 1:
                            copy_odd(n, TILES - 1)
                        if t >= LAG:
                            copy_qaug(n, t - LAG)
                        place_rel(n, t)
                    for t in range(TILES - LAG, TILES):
                        copy_qaug(n, t)
                    for j in range(STEPS + 3):
                        if j < STEPS:
                            attend(n, j)
                        if j - 3 in BY_DVE:
                            copy_probsT(n, j - 3)
                        if 1 <= j <= STEPS:
                            invert(n, j - 1)

                    def add_attention(t):
                        need(dve, "proj_done", n, t + 1)
                        v.tensor_tensor(x_mid[l][0:SIZE[t], t, :], bank[2 + t % 2][0:SIZE[t], 0:C],
                                        x_mid[l][0:SIZE[t], t, :], ALU.add).then_inc(S["mid_ready"], 1)

                    need(dve, "base_ready", n, 1)
                    residual_norm(n, l, x_mid[l], 2, ("mid_ready", n), add_attention)
                    need(dve, "xT_done", n, 2)
                    v.tensor_scalar(xT[0:96, 0, 0:TOK], bank[0][0:96, :], affine[l][:, 2, 0:1], affine[l][:, 3, 0:1],
                                    ALU.mult, ALU.add).then_inc(S["xT_lo"], 1)
                    need(dve, "midb_ready", n, 1)

                    def add_mlp(t):
                        need(dve, "down_done", n, t + 1)
                        v.tensor_tensor(x_mid[l][0:SIZE[t], t, :], bank[2 + t % 4][0:SIZE[t], 0:C],
                                        x_mid[l][0:SIZE[t], t, :], ALU.add).then_inc(S["out_ready"], 1)

                    assert chain[0] == PER["order_dve"], chain[0]
                    if l == 0:
                        chain[0] = 0
                        residual_norm(n + 1, 1, x_mid[0], 1, ("out_ready", n), add_mlp)
                    else:
                        chain[0] = 0
                        dve.wait_ge(S["x_loaded"], 32 * i + 64)
                        residual_norm(n + 1, 0, x_in, 1)
                        for t in range(TILES):
                            add_mlp(t)
                        need(dve, "out_ready", n, 5)

        @block.scalar
        def _(act):
            s = nc.scalar
            act.wait_ge(setup, SETUP)
            act.wait_ge(preset, PRESETS)
            s.activation(k_aug[KSLOT:QSLOT, HG:NH, :], hot.unsqueeze(1).to_broadcast([2 * RW, HG, TOK + 2]), ACT.Copy)\
                .then_inc(weights, 1)
            act.wait_ge(setup_qkv, SETUP_QKV)
            for l in range(2):
                for gg in range(G):
                    w = w_qkv[l][0:97 - gg, gg, C:2 * C]
                    s.activation(w, w, ACT.Copy, scale=QSCALE).then_inc(weights, 1)
            act.wait_ge(weights, WEIGHTS)

            def exps(n, j):
                a, h = SEQ[j]
                sl = j % PS
                need(act, "max_ready", n, j + 1)
                if j >= PS:
                    need(act, "probsT_done", n, j - PS + 1)
                if a is not None:
                    b = bank[S_BANKS[slot(j, "full") % 4]]
                    for r in range(2):
                        last = s.activation(probs[0:HALF, sl, r * WIN:(r + 1) * WIN], b[0:HALF, r * WIN:(r + 1) * WIN],
                                            ACT.Exp, bias=neg_max[0:HALF, sl, r:r + 1],
                                            accum_out=row_sum[0:HALF, sl, r:r + 1])
                else:
                    b = bank[S_BANKS[slot(j, "cut") % 4]]
                    for e in range(2):
                        s.activation(probs[0:CUT, sl, e * CK:e * CK + CUT], b[0:CUT, e * CK:e * CK + CUT], ACT.Exp,
                                     bias=neg_max[0:CUT, sl, e:e + 1], accum_out=row_sum[0:CUT, sl, e:e + 1])
                    for e in range(2):
                        b = bank[S_BANKS[slot(j, "pad") % 4]][0:CUT, WIN * e:WIN * e + WIN]
                        last = s.activation(b, b, ACT.Exp, bias=pad_bias[:, sl, e:e + 1],
                                            accum_out=probs[0:CUT, sl, e * CK + CUT:e * CK + CUT + 1])
                last.then_inc(S["exp_done"], 1)

            def copy_dist(n, t):
                need(act, "dist_done", n, 2 * t + 2)
                s.activation(dist[0:SIZE[t], t, :].rearrange("p (r h) -> p r h", h=NH)[:, :, HG:NH],
                             bank[2 + (2 * t + 1) % 4][0:SIZE[t], 0:2 * RT * HG]
                             .rearrange("p (r h) -> p r h", h=HG), ACT.Copy).then_inc(S["dist_hi"], 1)

            def k_high(n, t):
                need(act, "kv_done", n, t + 1)
                if t >= 2:
                    need(act, "kT_done", n, 2 * t - 2)
                k = k_tok[0:KEYS[t], t % 2, :].rearrange("p (h d z c) -> p h d z c", d=2, z=2, c=HD)
                src = bank[t % 2][0:KEYS[t], 0:C].rearrange("p (h c) -> p h c", c=HD)
                s.activation(k[:, :, :, 0, :], src.unsqueeze(2).to_broadcast([KEYS[t], NH, 2, HD]), ACT.Copy)
                s.activation(v_columns(t), bank[t % 2][0:KEYS[t], C:2 * C].rearrange("p (g e c) -> p g e c", e=HG, c=HD),
                             ACT.Copy).then_inc(S["kv_hi"], 1)

            def copy_even(n, t):
                for b in range(2):
                    need(act, "kT_done", n, 2 * t + b + 1)
                    s.activation(k_aug[0:KSLOT, 6 * b:6 * b + 5:2, START[t]:START[t] + KEYS[t]],
                                 bank[6 + b][0:KSLOT, 0:3 * KEYS[t]].rearrange("p (k m) -> p k m", k=3),
                                 ACT.Copy).then_inc(S["k_even"], 1)

            def place_rel(n, t):
                act.wait_ge(rel_loaded[t], n * (32 if t < 4 else 192) + (32 if t < 4 else 192))
                if t >= QT:
                    need(act, "qaug_done", n, 3 * (t - QT) + 3)
                q = q_tok[0:SIZE[t], t % QT, :].rearrange("p (h s) -> p h s", s=QSLOT)
                s.activation(q[:, :, KSLOT:KSLOT + RW], rel[0:SIZE[t], t, :].rearrange("p (r h) -> p h r", h=NH),
                             ACT.Copy).then_inc(S["rel_hi"], 1)

            def copy_probsT(n, j):
                need(act, "probsT_done", n, j + 1)
                if j >= 2:
                    need(act, "pv_done", n, j - 1)
                rows, m = (HALF, 4 * HALF) if SEQ[j][0] is not None else (CUT + 1, 2 * CUT)
                s.activation(probsT[0:rows, j % 2, 0:m], bank[2 + j % 2][0:rows, 0:m], ACT.Copy)\
                    .then_inc(S["probsT_act"], 1)

            def copy_oT(n, j):
                need(act, "pv_done", n, j + 1)
                a, h = SEQ[j]
                b = bank[OUT_BANKS[output(j)[0]]]
                if a is not None:
                    s.activation(oT[:, h // HG, WIN * a:WIN * a + WIN], b[0:96, 0:WIN], ACT.Copy)\
                        .then_inc(S["oT_ready"], 1)
                else:
                    s.activation(oT[:, h // CUTS, 4 * HALF:TOK], b[0:96, 0:CUT], ACT.Copy).then_inc(S["oT_ready"], 1)

            with act.Fori(0, PAIRS) as i:
                for l in range(2):
                    n = 2 * i + l
                    need(act, "xT_done", n, 1)
                    s.activation(xT[0:96, 1, 0:TOK], bank[1][0:96, :], ACT.Identity, bias=affine[l][:, 1, 1:2],
                                 scale=affine[l][:, 0, 1:2]).then_inc(S["xT_hi"], 1)
                    for t in range(TILES):
                        need(act, "q_done", n, t + 1)
                        s.activation(q_flat[0:SIZE[t], t, :], bank[4 + t % 2][0:SIZE[t], 0:C], ACT.Copy)\
                            .then_inc(S["q_copied"], 1)
                    need(act, "qT_done", n, 1)
                    s.activation(qT[:, 1, :], bank[3][0:96, :], ACT.Copy).then_inc(S["qT_hi"], 1)
                    for what, t in MIDDLE:
                        {"dist": copy_dist, "kv": k_high, "kT": copy_even}[what](n, t)
                    place_rel(n, 0)
                    copy_even(n, TILES - 1)
                    for t in range(1, LAG):
                        place_rel(n, t)
                    for c in range(0, 3 * TILES, 2):
                        t, b = c // 3, c % 3
                        need(act, "qaug_done", n, c + 1)
                        s.activation(q_aug[:, 4 * b:4 * b + 4, START[t]:START[t] + SIZE[t]],
                                     bank[4 + c % 4][0:QSLOT, 0:4 * SIZE[t]].rearrange("p (k m) -> p k m", k=4),
                                     ACT.Copy).then_inc(S["qaug_act"], 1)
                        if c in (2, 4):
                            place_rel(n, LAG + c // 2 - 1)
                    for j in range(STEPS + 5):
                        if j - 3 in BY_ACT:
                            copy_probsT(n, j - 3)
                        if j - 5 in OUT_UNITS:
                            copy_oT(n, j - 5)
                        if j < STEPS:
                            exps(n, j)
                    need(act, "xT_done", n, 2)
                    s.activation(xT[0:96, 1, 0:TOK], bank[1][0:96, :], ACT.Identity, bias=affine[l][:, 3, 1:2],
                                 scale=affine[l][:, 2, 1:2]).then_inc(S["xT_hi"], 1)
                    for f in range(MC):
                        need(act, "up_done", n, f + 1)
                        s.activation(hidden[:, f, :], bank[4 + f % 4][:, :], ACT.Gelu, bias=b_up[l][:, f:f + 1])\
                            .then_inc(S["gelu_done"], 1)
            act.wait_ge(stored, 16 + 160)
            need(act, "xn_ready", 2 * PAIRS, 5)
            act.dma_start(xn[:, 0:4, :], d["mid"][0:2].rearrange("a h w c -> (a h w) c")
                          .rearrange("(t p) c -> p t c", p=128)).then_inc(f_loaded, 16)

        @block.tensor
        def _(pe):
            t_ = nc.tensor
            pe.wait_ge(setup, SETUP)
            pe.wait_ge(setup_qkv, SETUP_QKV)
            pe.wait_ge(preset, PRESETS)
            pe.wait_ge(weights, WEIGHTS)

            def transpose_xn(n, k):
                for t in range(TILES):
                    need(pe, "xn_ready", n, 5 * (k - 1) + t + 1)
                    for gg in range(G):
                        last = t_.transpose(bank[gg][0:96, START[t]:START[t] + SIZE[t]],
                                            xn[0:SIZE[t], t, 96 * gg:96 * gg + 96], ident[0:SIZE[t], 0:SIZE[t]])
                last.then_inc(S["xT_done"], 1)
                need(pe, "xT_lo", n, k)
                need(pe, "xT_hi", n, k)

            def distances(n, l, t):
                if t == 0:
                    need(pe, "qT_lo", n, 1)
                    need(pe, "qT_hi", n, 1)
                for gg in range(G):
                    if t >= 2:
                        need(pe, ["dist_lo", "dist_hi"][gg], n, t - 1)
                    t_.matmul(bank[2 + (2 * t + gg) % 4][0:SIZE[t], 0:2 * RT * HG],
                              qT[:, gg, START[t]:START[t] + SIZE[t]], w_rel[l][:, :], start=True, stop=True)\
                        .then_inc(S["dist_done"], 1)

            def keys_values(n, l, t):
                if t >= 2:
                    need(pe, "kv_lo", n, t - 1)
                for gg in range(G):
                    rows = 97 - gg
                    last = t_.matmul(bank[t % 2][0:KEYS[t], 0:2 * C], xT[0:rows, gg, START[t]:START[t] + KEYS[t]],
                                     w_qkv[l][0:rows, gg, C:3 * C], start=(gg == 0), stop=(gg == 1))
                last.then_inc(S["kv_done"], 1)

            def transpose_k(n, l, t):
                need(pe, "kv_lo", n, t + 1)
                for b in range(2):
                    if t >= 1:
                        need(pe, "k_even", n, 2 * t + b - 1)
                        need(pe, "k_odd", n, 2 * t + b - 1)
                    for p in range(3):
                        last = t_.transpose(bank[6 + b][:, p * KEYS[t]:(p + 1) * KEYS[t]],
                                            k_tok[0:KEYS[t], t % 2, 128 * (3 * b + p):128 * (3 * b + p) + 128]
                                            .bitcast(F32), ident[0:KEYS[t], 0:KEYS[t]])
                    last.then_inc(S["kT_done"], 1)

            def scores(n, k):
                j, part = SLOTS[k]
                a, h = SEQ[j]
                b = bank[S_BANKS[k % 4]]
                if k >= 4:
                    need(pe, "exp_done", n, SLOTS[k - 4][0] + 1)
                if part == "full":
                    for r in range(2):
                        last = t_.matmul(b[0:HALF, r * WIN:(r + 1) * WIN],
                                         q_aug[:, h, START[2 * a + r]:START[2 * a + r] + HALF],
                                         k_aug[:, h, WIN * a:WIN * a + WIN], start=True, stop=True)
                else:
                    m, keys, mask = (CK, None, cut_mask) if part == "cut" else (WIN, pad_keys, pad_mask)
                    t_.matmul(b[0:CUT, 0:2 * m], q_class[:, :], mask[:, :], start=True, stop=False)
                    for e in range(2):
                        hh = 2 * h + e
                        key = k_aug[:, hh, 4 * HALF:TOK + 2] if keys is None else keys[:, :]
                        last = t_.matmul(b[0:CUT, e * m:(e + 1) * m], q_aug[:, hh, 4 * HALF:TOK], key,
                                         start=False, stop=(e == 1))
                last.then_inc(S["scores_done"], 1)

            def transpose_probs(n, j):
                need(pe, "probs_ready", n, j + 1)
                if j >= 2:
                    need(pe, copied(j - 2)[0], n, copied(j - 2)[1])
                o = bank[2 + j % 2]
                if SEQ[j][0] is not None:
                    for kk in range(2):
                        for r in range(2):
                            last = t_.transpose(o[0:HALF, (2 * kk + r) * HALF:(2 * kk + r + 1) * HALF],
                                                probs[0:HALF, j % PS, r * WIN + kk * HALF:r * WIN + (kk + 1) * HALF],
                                                ident[0:HALF, 0:HALF])
                else:
                    for e in range(2):
                        last = t_.transpose(o[0:CUT + 1, e * CUT:(e + 1) * CUT],
                                            probs[0:CUT, j % PS, e * CK:e * CK + CUT + 1], ident[0:CUT, 0:CUT])
                last.then_inc(S["probsT_done"], 1)

            def values(n, j):
                a, h = SEQ[j]
                b, opens, closes = output(j)
                b = bank[OUT_BANKS[b]]
                need(pe, copied(j)[0], n, copied(j)[1])
                if opens and free_output(j):
                    need(pe, "oT_ready", n, free_output(j))
                if a is not None:
                    for kk in range(2):
                        last = t_.matmul(b[0:96, 0:WIN], v_pad[0:HALF, 2 * a + kk, h, :],
                                         probsT[0:HALF, j % 2, kk * WIN:(kk + 1) * WIN],
                                         start=(opens and kk == 0), stop=(closes and kk == 1))
                else:
                    for e in range(2):
                        last = t_.matmul(b[0:96, 0:CUT], v_pad[0:CUT + 1, 4, 2 * h + e, :],
                                         probsT[0:CUT + 1, j % 2, e * CUT:(e + 1) * CUT],
                                         start=(opens and e == 0), stop=(closes and e == 1))
                last.then_inc(S["pv_done"], 1)

            with pe.Fori(0, PAIRS) as i:
                for l in range(2):
                    n = 2 * i + l
                    transpose_xn(n, 1)
                    for t in range(TILES):
                        if t >= 2:
                            need(pe, "q_copied", n, t - 1)
                        for gg in range(G):
                            rows = 97 - gg
                            last = t_.matmul(bank[4 + t % 2][0:SIZE[t], 0:C],
                                             xT[0:rows, gg, START[t]:START[t] + SIZE[t]],
                                             w_qkv[l][0:rows, gg, 0:C], start=(gg == 0), stop=(gg == 1))
                        last.then_inc(S["q_done"], 1)
                    for t in range(TILES):
                        need(pe, "q_copied", n, t + 1)
                        for gg in range(G):
                            last = t_.transpose(bank[2 + gg][0:96, START[t]:START[t] + SIZE[t]],
                                                q_flat[0:SIZE[t], t, 96 * gg:96 * gg + 96],
                                                ident[0:SIZE[t], 0:SIZE[t]])
                    last.then_inc(S["qT_done"], 1)
                    for what, t in MIDDLE:
                        {"dist": distances, "kv": keys_values, "kT": transpose_k}[what](n, l, t)
                    transpose_k(n, l, TILES - 1)
                    need(pe, "k_even", n, 10)
                    need(pe, "k_odd", n, 10)
                    for c in range(3 * TILES):
                        t, b = c // 3, c % 3
                        need(pe, "rel_placed", n, t + 1)
                        need(pe, "q_placed", n, t + 1)
                        if c >= 4:
                            need(pe, ["qaug_act", "qaug_dve"][c % 2], n, (c - 4) // 2 + 1)
                        for e in range(4):
                            at = (4 * b + e) * QSLOT
                            last = t_.transpose(bank[4 + c % 4][0:QSLOT, e * SIZE[t]:(e + 1) * SIZE[t]],
                                                q_tok[0:SIZE[t], t % QT, at:at + QSLOT].bitcast(F32),
                                                ident[0:SIZE[t], 0:SIZE[t]])
                        last.then_inc(S["qaug_done"], 1)
                    need(pe, "qaug_act", n, 8)
                    need(pe, "qaug_dve", n, 7)
                    need(pe, "dist_lo", n, 5)
                    need(pe, "dist_hi", n, 5)
                    k = 0
                    for j in range(STEPS + 4):
                        if 3 <= j < STEPS + 3:
                            transpose_probs(n, j - 3)
                        while k < len(SLOTS) and SLOTS[k][0] <= j + 1:
                            scores(n, k)
                            k += 1
                        if j >= 4:
                            values(n, j - 4)
                    need(pe, "oT_ready", n, len(OUT_UNITS))
                    pe.wait_ge(setup_rest, SETUP_REST)
                    for t in range(TILES):
                        if t >= 2:
                            need(pe, "mid_ready", n, t - 1)
                        for gg in range(G):
                            last = t_.matmul(bank[2 + t % 2][0:SIZE[t], 0:C], oT[:, gg, START[t]:START[t] + SIZE[t]],
                                             w_proj[l][:, gg, :], start=(gg == 0), stop=(gg == G - 1))
                        last.then_inc(S["proj_done"], 1)
                    transpose_xn(n, 2)
                    for f in range(MC):
                        if f >= 4:
                            need(pe, "gelu_done", n, f - 3)
                        for gg in range(G):
                            last = t_.matmul(bank[4 + f % 4][:, :], w_up[l][:, gg, 128 * f:128 * f + 128],
                                             xT[0:96, gg, 0:TOK], start=(gg == 0), stop=(gg == 1))
                        last.then_inc(S["up_done"], 1)
                    for t in range(TILES):
                        if t >= 4:
                            need(pe, "out_ready", n, t - 3)
                        for f in range(MC):
                            if t == 0:
                                need(pe, "gelu_done", n, f + 1)
                            last = t_.matmul(bank[2 + t % 4][0:SIZE[t], 0:C], hidden[:, f, START[t]:START[t] + SIZE[t]],
                                             w_down[l][:, f, :], start=(f == 0), stop=(f == MC - 1))
                        last.then_inc(S["down_done"], 1)


PRESETS = 4 + 5
WEIGHTS = 5 + 5 + 1


def channels(f, p, a):
    return f[:, p, a, :, 0:48]


def fold_input(nc, pool, i, fourier):
    g = nc.gpsimd
    xn, f_loaded, fold, half, sums, folded = fourier[5:]
    y_in = xn[:, 0:4, :]
    pool.wait_ge(f_loaded, 16 * i + 16)
    for p, op in enumerate((ALU.add, ALU.subtract)):
        for a in range(2):
            x0, x1 = (y_in[:, 2 * a + c, :].rearrange("p (g e) -> p g e", g=4) for c in range(2))
            last = g.tensor_tensor(channels(fold, p, a), x0, x1, op)
        last.then_inc(sums, 1)
        pool.wait_ge(sums, 2 * i + p + 1)
        for a in range(2):
            x = channels(fold, p, a)
            last = g.tensor_tensor(x, x, half[:, :].unsqueeze(2).to_broadcast([128, 4, 48]), ALU.mult)
        last.then_inc(folded, 1)


def fourier_loop(nc, d, bank, stored, fourier):
    fwd, inv, w1, w2, b1, xn, f_loaded, fold_in, half, sums, folded = fourier
    y_in = xn[:, 0:4, :]
    with ExitStack() as ctx:
        def sb(name, shape):
            return ctx.enter_context(nc.sbuf_tensor(name, shape, F32))

        def sem(name):
            return ctx.enter_context(nc.semaphore(name))

        y_out = sb("y_out", [128, 4, C])
        fold = [fold_in] + [sb(f"fold{s}", [128, 2, 2, 4, 64]) for s in (1, 2)]
        seed = sb("f_seed", [1, 1])
        spare = sb("spare", [128, 1])
        neg_lambda = sb("neg_lambda", [FC, 1])
        xf = sb("xf", [128, 4, 2, FREQ])
        o1 = sb("o1", [128, 4, 2, FREQ])
        over = sb("over", [FC, 4, 2 * C])
        o2 = sb("o2", [FC, 2, 2, 2, C])
        preset = sem("f_preset")
        names = ("fwd_done xf_dve xf_act mix1_done relu_act relu_dve mix2_done over_ready "
                 "o2_ready inv_done fold_ready unfolded f_stored").split()
        S = {n: sem(n) for n in names}
        PER = dict(fwd_done=4, xf_dve=4, xf_act=4, mix1_done=4, relu_act=2, relu_dve=2, mix2_done=4, over_ready=4,
                   o2_ready=4, inv_done=2, fold_ready=2)

        def need(eng, name, n, k):
            eng.wait_ge(S[name], n * PER[name] + k)

        block = ctx.enter_context(nc.Block())

        @block.sync
        def _(sp):
            def mid(i):
                return d["mid"][i].rearrange("a h w c -> (a h w) c").rearrange("(t p) c -> p t c", p=128)

            sp.dma_start(seed[:, :], d["ident"][0:1, 0:1]).then_inc(S["f_stored"], 16)

            def store(i):
                sp.wait_ge(S["unfolded"], 2 * i + 3)
                sp.dma_start(d["out"][bass.ds(2 * i, 2)].rearrange("a h w c -> (a h w) c")
                             .rearrange("(t p) c -> p t c", p=128), y_out[:, :, :]).then_inc(S["f_stored"], 16)

            sp.wait_ge(stored, 16 + 160 * PAIRS)
            with sp.Fori(0, PAIRS - 1) as i:
                sp.wait_ge(sums, 2 * i + 2)
                sp.dma_start(y_in[:, :, :], mid(bass.ds(2 * i + 2, 2))).then_inc(f_loaded, 16)
                store(i)
            store(PAIRS - 1)
            sp.wait_ge(S["f_stored"], 16 + 16 * PAIRS)
            sp.wait_ge(f_loaded, 16 * PAIRS)

        @block.gpsimd
        def _(pool):
            g = nc.gpsimd
            def unfold_output(i):
                need(pool, "fold_ready", 2 * i + 1, 2)
                pool.wait_ge(S["f_stored"], 16 * i + 16)
                for c, op in enumerate((ALU.add, ALU.subtract)):
                    for a in range(2):
                        last = g.tensor_tensor(y_out[:, 2 * a + c, :].rearrange("p (g e) -> p g e", g=4),
                                               channels(fold[2], 0, a), channels(fold[2], 1, a), op)
                    last.then_inc(S["unfolded"], 1)

            g.memset(spare[:, :], 0.0).then_inc(S["unfolded"], 1)
            with pool.Fori(0, PAIRS - 1) as i:
                need(pool, "fold_ready", 2 * i, 2)
                fold_input(nc, pool, i + 1, fourier)
                unfold_output(i)
            unfold_output(PAIRS - 1)

        @block.vector
        def _(dve):
            v = nc.vector
            for f in fold[1:]:
                v.memset(f[:, :, :, :, 48:64], 0.0).then_inc(preset, 1)
            v.memset(neg_lambda[:, :], -LAMBDA).then_inc(preset, 1)
            for l in range(2):
                for w, cols in ((w1[l], 64), (w2[l], 48)):
                    w = w[64:128, :, 0:cols]
                    v.tensor_scalar(w, w, -1.0, None, ALU.mult).then_inc(preset, 1)
            dve.wait_ge(preset, FOURIER_PRESETS)
            with dve.Fori(0, PAIRS) as i:
                for l in range(2):
                    n = 2 * i + l
                    for k in range(4):
                        gg, a = k // 2, k % 2
                        need(dve, "fwd_done", n, k + 1)
                        b = bank[k][0:64, 0:2 * FREQ].rearrange("p (z f) -> p z f", z=2)
                        v.tensor_scalar(xf[0:64, 2 * gg, a, :], b[:, 0, :], 2 * FWD[l], None, ALU.mult)
                        v.tensor_scalar(xf[64:128, 2 * gg, a, :], b[:, 1, :], 2 * FWD[l], None, ALU.mult)\
                            .then_inc(S["xf_dve"], 1)
                    for k in (1, 3):
                        need(dve, "mix1_done", n, k + 1)
                        v.tensor_scalar(o1[:, k, :, :].rearrange("p a f -> p (a f)"), bank[4 + k][:, 0:2 * FREQ],
                                        b1[l][:, k:k + 1], 0.0, ALU.add, ALU.max).then_inc(S["relu_dve"], 1)
                    for k in range(4):
                        c, a = k // 2, k % 2
                        need(dve, "over_ready", n, k + 1)
                        v.scalar_tensor_tensor(out=o2[:, c, :, a, :],
                                               in0=bank[k][0:FC, 0:2 * C].rearrange("p (z c) -> p z c", z=2),
                                               scalar=LAMBDA, in1=over[:, k, :].rearrange("p (z c) -> p z c", z=2),
                                               op0=ALU.add, op1=ALU.min).then_inc(S["o2_ready"], 1)
                    if l == 1:
                        dve.wait_ge(S["unfolded"], 2 * i + 1)
                    for p in range(2):
                        need(dve, "inv_done", n, p + 1)
                        for a in range(2):
                            last = v.scalar_tensor_tensor(out=channels(fold[l + 1], p, a),
                                                          in0=bank[4 + p][:, a * C:(a + 1) * C]
                                                          .rearrange("p (g e) -> p g e", g=4), scalar=INV[l],
                                                          in1=channels(fold[l], p, a), op0=ALU.mult, op1=ALU.add)
                        last.then_inc(S["fold_ready"], 1)

        @block.scalar
        def _(act):
            s = nc.scalar
            act.wait_ge(preset, FOURIER_PRESETS)
            with act.Fori(0, PAIRS) as i:
                for l in range(2):
                    n = 2 * i + l
                    for k in range(4):
                        gg, a = k // 2, k % 2
                        need(act, "fwd_done", n, k + 1)
                        b = bank[k][64:128, 0:2 * FREQ].rearrange("p (z f) -> p z f", z=2)
                        s.activation(xf[0:64, 2 * gg + 1, a, :], b[:, 0, :], ACT.Copy, scale=2 * FWD[l])
                        s.activation(xf[64:128, 2 * gg + 1, a, :], b[:, 1, :], ACT.Copy, scale=2 * FWD[l])\
                            .then_inc(S["xf_act"], 1)
                    for k in (0, 2):
                        need(act, "mix1_done", n, k + 1)
                        s.activation(o1[:, k, :, :].rearrange("p a f -> p (a f)"), bank[4 + k][:, 0:2 * FREQ],
                                     ACT.Relu, bias=b1[l][:, k:k + 1]).then_inc(S["relu_act"], 1)
                    for k in range(4):
                        need(act, "mix2_done", n, k + 1)
                        s.activation(over[:, k, :], bank[k][0:FC, 0:2 * C], ACT.Relu, bias=neg_lambda[:, :])\
                            .then_inc(S["over_ready"], 1)

        @block.tensor
        def _(pe):
            t_ = nc.tensor
            pe.wait_ge(preset, FOURIER_PRESETS)
            with pe.Fori(0, PAIRS) as i:
                for l in range(2):
                    n = 2 * i + l
                    for p in range(2):
                        if l == 0:
                            pe.wait_ge(folded, 2 * i + p + 1)
                        else:
                            need(pe, "fold_ready", 2 * i, p + 1)
                        for k in range(4):
                            gg, a = k // 2, k % 2
                            out = bank[k][:, 0:2 * FREQ].rearrange("p (z f) -> p z f", z=2)
                            last = t_.matmul(out[:, :, p * FC:(p + 1) * FC],
                                             fold[l][:, p, a, 2 * gg:2 * gg + 2, :].rearrange("p g e -> p (g e)"),
                                             fwd[:, p, :, :], start=True, stop=True)
                            if p == 1:
                                last.then_inc(S["fwd_done"], 1)
                    for g in range(4):
                        if g % 2 == 0:
                            need(pe, "xf_dve", n, g + 2)
                            need(pe, "xf_act", n, g + 2)
                        t_.matmul(bank[4 + g][:, 0:2 * FREQ], w1[l][:, g, :],
                                  xf[:, g, :, :].rearrange("p a f -> p (a f)"), start=True, stop=True)\
                            .then_inc(S["mix1_done"], 1)
                    for k in range(4):
                        c, a = k // 2, k % 2
                        for g in range(4):
                            if k == 0:
                                need(pe, ["relu_act", "relu_dve"][g % 2], n, g // 2 + 1)
                            out = bank[k][0:FC, 0:2 * C].rearrange("p (z g e) -> p z g e", z=2, g=4)
                            last = t_.matmul(out[:, :, g, :], o1[:, g, a, c * FC:(c + 1) * FC],
                                             w2[l][:, g, :], start=True, stop=True)
                        last.then_inc(S["mix2_done"], 1)
                    for p in range(2):
                        need(pe, "o2_ready", n, 2 * p + 2)
                        for z in range(2):
                            last = t_.matmul(bank[4 + p][:, 0:2 * C], inv[:, p, z, :],
                                             o2[:, p, z, :, :].rearrange("p a c -> p (a c)"),
                                             start=(z == 0), stop=(z == 1))
                        last.then_inc(S["inv_done"], 1)


FOURIER_PRESETS = 3 + 4


def kernel(**inputs):
    import numpy as np
    import concourse.bacc as bacc
    from concourse.bass_utils import run_bass_kernel_spmd

    def get(name):
        return np.asarray(inputs[name])

    order = []
    at = np.arange(HH * WW).reshape(HH, WW)
    for a in range(2):
        order.append(a * 256 + at[0:WS, 0:WS].ravel())
    for rows, cols in ((slice(0, WS), slice(WS, WW)), (slice(WS, HH), slice(0, WS)), (slice(WS, HH), slice(WS, WW))):
        for a in range(2):
            order.append(a * 256 + at[rows, cols].ravel())
    order = np.concatenate(order)
    x = get("x").reshape(PAIRS, TOK, C)[:, order]
    x = np.concatenate([x, x[:1]])

    def rel_blocks(name):
        out = np.zeros((96, 2, RT, HG), np.float32)
        for axis, part in enumerate("hw"):
            r = get(f"{name}_rel_pos_{part}")[::-1]
            for h in range(HG):
                out[HD * h:HD * h + HD, axis, :, h] = r.T
        return out.reshape(96, 2 * RT * HG)

    def blocks(r, i, size):
        out = np.zeros((128, 4, 2 * size), np.float32)
        for b in range(8):
            g, at = b // 2, 24 * (b % 2)
            for row, col, w in ((0, 0, r), (64, 0, i), (0, size, i), (64, size, r)):
                out[row + at:row + at + 24, g, col + at:col + at + 24] = w[b]
        return out

    pos = order % 256
    ph, pw = (pos // WW) % WS, (pos % WW) % WS
    onehot = np.zeros((2, RW, TOK + 2), np.float32)
    onehot[:, ph, np.arange(TOK)] = 1
    onehot[:, WS + pw, np.arange(TOK)] = 1
    onehot = onehot.reshape(2 * RW, TOK + 2)
    c = np.arange(4 * HALF, TOK)
    row, col = (order[c] % 256) // WW, order[c] % WW
    window = (order[c] // 256) * 4 + (row >= WS) * 2 + (col >= WS)
    classes = np.unique(window)
    q_class = np.zeros((CLASSES, CUT), np.float32)
    q_class[:len(classes)] = classes[:, None] == window[None]
    cut_mask = np.zeros((CLASSES, 2, CK), np.float32)
    cut_mask[:len(classes), :, :CUT] = np.where(classes[:, None] == window[None], 0, BIG)[:, None]
    ky, kx = np.arange(WIN) // WS, np.arange(WIN) % WS
    real_y = ky[None] + WS * (classes // 2 % 2)[:, None] < HH
    real_x = kx[None] + WS * (classes % 2)[:, None] < WW
    pad_mask = np.zeros((CLASSES, 2, WIN), np.float32)
    pad_mask[:len(classes)] = np.where(real_y & real_x, BIG, 0)[:, None]
    cut_mask, pad_mask = cut_mask.reshape(CLASSES, 2 * CK), pad_mask.reshape(CLASSES, 2 * WIN)
    th, tw = np.arange(256) // WW, np.arange(256) % WW
    kh, kw = np.arange(FREQ) // 9, np.arange(FREQ) % 9
    turn = ((th[:, None] * kh[None] + tw[:, None] * kw[None]) % 16) * (2 * np.pi / 16)
    parity = [np.flatnonzero(kh % 2 == p) for p in range(2)]
    fwd = np.stack([np.stack([np.cos(turn), -np.sin(turn)])[:, :128, f] for f in parity])
    fwd = fwd.transpose(2, 0, 1, 3).astype(np.float32)
    weight = np.where((kw == 0) | (kw == 8), 1.0, 2.0)[:, None]
    inverse = np.stack([weight * np.cos(turn.T), -weight * np.sin(turn.T)])
    inv = np.stack([inverse[:, f, :128] for f in parity]).transpose(2, 0, 1, 3).astype(np.float32)

    L = ("L0_conv", "L1_conv")
    both = {
        "qkv_w": ("qkv_w",) * 2, "qkv_b": ("qkv_b",) * 2, "proj_w": ("proj_w",) * 2, "proj_b": ("proj_b",) * 2,
        "up_w": ("lin1_w", "mlp_w1"), "up_b": ("lin1_b", "mlp_b1"),
        "down_w": ("lin2_w", "mlp_w2"), "down_b": ("lin2_b", "mlp_b2"),
    }
    arrays = {"x": x}
    for key, (a, b) in both.items():
        arrays[key] = np.stack([get(f"{L[0]}_{a}"), get(f"{L[1]}_{b}")])
    arrays["rel"] = np.stack([rel_blocks(n) for n in L])
    fourier = [[get(f"L2_conv_{k}{z}") for z in "ri"] for k in ("w1", "b1", "w2", "b2")], \
              [get(f"L3_conv_{k}") for k in ("w1", "b1", "w2", "b2")]
    fb1 = np.zeros((2, 128, 4), np.float32)
    fb1[:, 48] = 1
    for l, (_, b, _, _) in enumerate(fourier):
        for z in range(2):
            fb1[l, 64 * z:64 * z + 48] = np.asarray(b[z]).reshape(4, 48).T
    arrays["fb1"] = fb1
    arrays["fw1"] = np.stack([blocks(w[0], w[1], 64) for w, _, _, _ in fourier])
    arrays["fw2"] = np.stack([blocks(w[0], w[1], 48) for _, _, w, _ in fourier])
    for l, (_, _, _, b) in enumerate(fourier):
        arrays["fw2"][l, 48] = np.stack([np.asarray(b[z]).reshape(4, 48) for z in range(2)], 1).reshape(4, 96)
    norms = [[get(f"L0_conv_{k}") for k in ("n1_w", "n1_b", "n2_w", "n2_b")],
             [get(f"L1_conv_{k}") for k in ("ln1_g", "ln1_b", "ln2_g", "ln2_b")]]
    arrays["affine"] = np.array(norms).reshape(2, 4, G, 96).transpose(0, 3, 1, 2)
    arrays["up_b"] = arrays["up_b"].reshape(2, MC, 128).transpose(0, 2, 1)
    arrays.update(ident=np.eye(128, dtype=np.float32), onehot=onehot, q_class=q_class, cut_mask=cut_mask, pad_mask=pad_mask,
                  fwd=fwd, inv=inv)
    arrays = {k: np.ascontiguousarray(a) for k, a in arrays.items()}

    nc = bacc.Bacc("TRN2", target_bir_lowering=False, num_devices=1)
    d = {k: nc.dram_tensor(f"in_{k}", a.shape, F32, kind="ExternalInput").ap() for k, a in arrays.items()}
    d["dist"] = nc.dram_tensor("distances", (2, TOK, UROW), F32, kind="Internal").ap()
    d["mid"] = nc.dram_tensor("between_loops", (B, HH, WW, C), F32, kind="Internal").ap()
    d["out"] = nc.dram_tensor("out", (B, HH, WW, C), F32, kind="ExternalOutput").ap()
    build(nc, d)
    r = run_bass_kernel_spmd(nc, [{f"in_{k}": a for k, a in arrays.items()}], core_ids=[0])
    return r.results[0]["out"]
```
